# Optimizing a Trainium2 kernel written in Bass

```python
import numpy as np
import jax
import jax.numpy as jnp

def _softmax(x, axis=-1):
    return jax.nn.softmax(x, axis=axis)

def _gelu(x):
    return jax.nn.gelu(x, approximate=True)

def _silu(x):
    return jax.nn.silu(x)

def _sigmoid(x):
    return jax.nn.sigmoid(x)

def _layernorm(x, axis=-1, eps=1e-05):
    m = jnp.mean(x, axis=axis, keepdims=True)
    v = jnp.var(x, axis=axis, keepdims=True)
    return (x - m) / jnp.sqrt(v + eps)

def _scatter_add(tgt, idx, src, axis=0):
    return tgt.at[idx].add(src)

def _segment_sum(src, seg, n):
    return jax.ops.segment_sum(src, seg, n)
kernel_name = 'mk_gnn_preln_d4_gnn_r32_7fdbba'

def setup_inputs(seed: int=0):
    np.random.seed(seed)
    _w = jnp.asarray

    def _rec_inputs():
        import jax
        import jax.numpy as jnp
        _gk = jax.random.key(seed)
        x = -0.0003713 + 1 * jax.random.normal(jax.random.fold_in(_gk, 1), (3125, 128), jnp.float32)
        _s = jax.random.randint(jax.random.fold_in(_gk, 2), (50000,), 0, 3125, jnp.int32)
        _d = jax.random.randint(jax.random.fold_in(_gk, 3), (50000,), 0, 3125, jnp.int32)
        _loop = jnp.arange(3125, dtype=jnp.int32)
        src = jnp.concatenate([_s, _d, _loop])
        dst = jnp.concatenate([_d, _s, _loop])
        _o = jnp.argsort(dst, stable=True)
        src = src[_o]
        dst = dst[_o]
        edge_attr_2 = 0.000126197 + 0.999763 * jax.random.normal(jax.random.fold_in(_gk, 12), (103125, 2), jnp.float32)
        edge_attr_32 = 0.000283511 + 1.00007 * jax.random.normal(jax.random.fold_in(_gk, 13), (103125, 32), jnp.float32)
        edge_type_16 = jax.random.randint(jax.random.fold_in(_gk, 15), (103125,), 0, 16, jnp.int32)
        edge_type_2 = jax.random.randint(jax.random.fold_in(_gk, 16), (103125,), 0, 2, jnp.int32)
        edge_weight = jax.random.uniform(jax.random.fold_in(_gk, 17), (103125,), jnp.float32, 0.0, 0.999998)
        return (x, src, dst, edge_attr_2, edge_attr_32, edge_type_16, edge_type_2, edge_weight)
    x, src, dst, edge_attr_2, edge_attr_32, edge_type_16, edge_type_2, edge_weight = _rec_inputs()

    def _L0_gnn_setup():
        import jax, jax.numpy as jnp
        import numpy as np
        N = 3125
        E = 18750
        D = 128
        H = 8
        DH = D // H
        T = 32
        NET = 2

        def _ln(x, g, b, eps=1e-05):
            mu = jnp.mean(x, axis=-1, keepdims=True)
            var = jnp.mean((x - mu) ** 2, axis=-1, keepdims=True)
            return (x - mu) * jax.lax.rsqrt(var + eps) * g + b

        def _expmap(e, c):
            abs_c = jnp.maximum(jnp.abs(c), 1e-15)
            sq = jnp.sqrt(abs_c)
            n = jnp.maximum(jnp.linalg.norm(e, axis=-1, keepdims=True), 1e-15)
            tanh_p = jnp.tanh(sq * n) * e / (sq * n)
            tan_p = jnp.tan(sq * n) * e / (sq * n)
            return jnp.where(c < 0, tanh_p, tan_p)

        def _proj(x, c, eps=1e-05):
            abs_c = jnp.maximum(jnp.abs(c), 1e-15)
            maxnorm = (1.0 - eps) / jnp.sqrt(abs_c)
            norm = jnp.linalg.norm(x, axis=-1, keepdims=True)
            scale = jnp.where(norm > maxnorm, maxnorm / norm, jnp.ones_like(norm))
            return x * scale

        def _forward(x, time_emb, edge_time, Wq, Wk, Wv, rel_q, rel_k, rel_v, Wt, bt, Wd1, bd1, Wd2, bd2, decay_scale, c_mag, hyp_beta, logit_alpha, Wo, bo, g1, be1, g2, be2, Wf1, bf1, Wf2, bf2, src, dst, edge_type):
            n = x.shape[0]
            Q = (x @ Wq).reshape(n, H, DH)
            K = (x @ Wk).reshape(n, H, DH)
            V = (x @ Wv).reshape(n, H, DH)
            q_dst = Q[dst] + rel_q[edge_type].reshape(-1, H, DH)
            k_src = K[src] + rel_k[edge_type].reshape(-1, H, DH)
            v_src = V[src] + rel_v[edge_type].reshape(-1, H, DH)
            k_src = k_src + (time_emb @ Wt + bt).reshape(-1, H, DH)
            euclid = jnp.sum(q_dst * k_src, axis=-1) / np.float32(np.sqrt(DH))
            denom_t = jnp.maximum(1.0, edge_type.max().astype(jnp.float32) + 1.0)
            et = edge_type.astype(jnp.float32)[:, None] / denom_t
            dec_in = jnp.concatenate([edge_time[:, None], et], axis=-1)
            decay_raw = jnp.tanh(jax.nn.relu(dec_in @ Wd1 + bd1) @ Wd2 + bd2)
            decay = jnp.exp(decay_scale[None, :] * decay_raw)
            euclid = euclid * decay
            c = -jnp.abs(c_mag)
            m = _proj(_expmap(x, c), c)
            man_dist = jnp.linalg.norm(m[src] - m[dst], axis=-1)[:, None]
            hyp = -hyp_beta[None, :] * man_dist * decay
            alpha = jax.nn.sigmoid(logit_alpha)[None, :]
            logits = alpha * euclid + (1.0 - alpha) * hyp
            seg_max = jax.ops.segment_max(logits, dst, num_segments=n)
            ex = jnp.exp(logits - seg_max[dst])
            denom = jax.ops.segment_sum(ex, dst, num_segments=n)
            attn = ex / denom[dst]
            agg = jax.ops.segment_sum(v_src * attn[..., None], dst, num_segments=n).reshape(n, D)
            out = agg @ Wo + bo
            x = _ln(x + out, g1, be1)
            ffn = jax.nn.gelu(x @ Wf1 + bf1, approximate=False) @ Wf2 + bf2
            x = _ln(x + ffn, g2, be2)
            return x
        key = jax.random.key(seed)
        ks = jax.random.split(key, 20)

        def lin(k, fi, fo):
            return jax.random.normal(k, (fi, fo), jnp.float32) / np.float32(np.sqrt(fi))
        return {'x': jax.random.normal(ks[0], (N, D), jnp.float32), 'edge_index': jax.random.randint(ks[1], (2, E), 0, N), 'time_emb': jax.random.normal(ks[2], (E, T), jnp.float32), 'edge_type': jax.random.randint(ks[3], (E,), 0, NET), 'edge_time': jax.random.uniform(ks[4], (E,), jnp.float32), 'Wq': lin(ks[5], D, D), 'Wk': lin(ks[6], D, D), 'Wv': lin(ks[7], D, D), 'rel_q': jax.random.normal(ks[8], (NET, D), jnp.float32) * 0.1, 'rel_k': jax.random.normal(ks[9], (NET, D), jnp.float32) * 0.1, 'rel_v': jax.random.normal(ks[10], (NET, D), jnp.float32) * 0.1, 'Wt': lin(ks[11], T, D), 'bt': jnp.zeros((D,), jnp.float32), 'Wd1': lin(ks[12], 2, 64), 'bd1': jnp.zeros((64,), jnp.float32), 'Wd2': lin(ks[13], 64, H), 'bd2': jnp.zeros((H,), jnp.float32), 'decay_scale': jnp.full((H,), 0.5, jnp.float32), 'c_mag': jnp.asarray(1.0, jnp.float32), 'hyp_beta': jnp.ones((H,), jnp.float32), 'logit_alpha': jnp.zeros((H,), jnp.float32), 'Wo': lin(ks[14], D, D), 'bo': jnp.zeros((D,), jnp.float32), 'g1': jnp.ones((D,), jnp.float32), 'be1': jnp.zeros((D,), jnp.float32), 'g2': jnp.ones((D,), jnp.float32), 'be2': jnp.zeros((D,), jnp.float32), 'Wf1': lin(ks[15], D, 4 * D), 'bf1': jnp.zeros((4 * D,), jnp.float32), 'Wf2': lin(ks[16], 4 * D, D), 'bf2': jnp.zeros((D,), jnp.float32)}
    _L0_gnn_all = _L0_gnn_setup()
    _L0_gnn_in = {k: v for k, v in _L0_gnn_all.items() if k in ('Wq', 'Wk', 'Wv', 'rel_q', 'rel_k', 'rel_v', 'Wt', 'bt', 'Wd1', 'bd1', 'Wd2', 'bd2', 'decay_scale', 'c_mag', 'hyp_beta', 'logit_alpha', 'Wo', 'bo', 'g1', 'be1', 'g2', 'be2', 'Wf1', 'bf1', 'Wf2', 'bf2')}
    del _L0_gnn_all

    def _L1_gnn_setup():
        import jax, jax.numpy as jnp
        import numpy as np
        N_NODES = 50000
        N_EDGES = 25000
        D = 128
        key = jax.random.key(seed)
        k1, k2, k3, k4, k5 = jax.random.split(key, 5)
        N = jax.random.normal(k1, (N_NODES, D), dtype=jnp.float32)
        W1 = jax.random.normal(k2, (D, D), dtype=jnp.float32) * (1.0 / np.sqrt(D))
        w2 = jax.random.normal(k3, (D,), dtype=jnp.float32) * (1.0 / np.sqrt(D))
        src = jax.random.randint(k4, (N_EDGES,), 0, N_NODES, dtype=jnp.int32)
        dst = jax.random.randint(k5, (N_EDGES,), 0, N_NODES, dtype=jnp.int32)
        return {'N': N, 'W1': W1, 'w2': w2, 'src': src, 'dst': dst}
    _L1_gnn_all = _L1_gnn_setup()
    _L1_gnn_in = {k: v for k, v in _L1_gnn_all.items() if k in ('W1', 'w2')}
    del _L1_gnn_all

    def _L2_gnn_setup():
        import jax, jax.numpy as jnp
        import numpy as np
        N = 1250
        E = 20000
        CIN = 128
        COUT = 128
        EDGE_DIM = 2
        BN_EPS = 1e-05
        key = jax.random.key(seed)
        ks = jax.random.split(key, 9)
        din = 2 * CIN + EDGE_DIM
        x = jax.random.normal(ks[0], (N, CIN), dtype=jnp.float32)
        edge_index = jax.random.randint(ks[1], (2, E), 0, N, dtype=jnp.int64)
        edge_attr = jax.random.normal(ks[2], (E, EDGE_DIM), dtype=jnp.float32)
        W1 = jax.random.normal(ks[3], (din, COUT), dtype=jnp.float32) / np.sqrt(din)
        b1 = jax.random.normal(ks[4], (COUT,), dtype=jnp.float32) * 0.01
        gamma = jnp.ones((COUT,), dtype=jnp.float32)
        beta = jnp.zeros((COUT,), dtype=jnp.float32)
        W2 = jax.random.normal(ks[5], (COUT, COUT), dtype=jnp.float32) / np.sqrt(COUT)
        b2 = jax.random.normal(ks[6], (COUT,), dtype=jnp.float32) * 0.01
        return {'x': x, 'edge_index': edge_index, 'edge_attr': edge_attr, 'W1': W1, 'b1': b1, 'gamma': gamma, 'beta': beta, 'W2': W2, 'b2': b2}
    _L2_gnn_all = _L2_gnn_setup()
    _L2_gnn_in = {k: v for k, v in _L2_gnn_all.items() if k in ('W1', 'b1', 'gamma', 'beta', 'W2', 'b2')}
    del _L2_gnn_all

    def _L3_gnn_setup():
        import jax, jax.numpy as jnp
        import numpy as np
        N, H = (50000, 128)
        E = 25000
        ETD = 32
        NUM_ET = 16
        LN_EPS = 1e-05
        key = jax.random.key(seed)
        ks = jax.random.split(key, 9)
        x = jax.random.normal(ks[0], (N, H), dtype=jnp.float32)
        edge_index = jax.random.randint(ks[1], (2, E), 0, N, dtype=jnp.int64)
        edge_type = jax.random.randint(ks[2], (E,), 0, NUM_ET, dtype=jnp.int64)
        edge_emb_W = jax.random.normal(ks[3], (NUM_ET, ETD), dtype=jnp.float32)
        lim_msg = 1.0 / np.sqrt(H + ETD)
        msg_W = jax.random.uniform(ks[4], (H, H + ETD), jnp.float32, -lim_msg, lim_msg)
        msg_b = jax.random.uniform(ks[5], (H,), jnp.float32, -lim_msg, lim_msg)
        lim_upd = 1.0 / np.sqrt(H)
        upd_W = jax.random.uniform(ks[6], (H, H), jnp.float32, -lim_upd, lim_upd)
        upd_b = jax.random.uniform(ks[7], (H,), jnp.float32, -lim_upd, lim_upd)
        ln_g = jnp.ones((H,), jnp.float32)
        ln_b = jnp.zeros((H,), jnp.float32)
        return {'x': x, 'edge_index': edge_index, 'edge_type': edge_type, 'edge_emb_W': edge_emb_W, 'msg_W': msg_W, 'msg_b': msg_b, 'upd_W': upd_W, 'upd_b': upd_b, 'ln_g': ln_g, 'ln_b': ln_b}
    _L3_gnn_all = _L3_gnn_setup()
    _L3_gnn_in = {k: v for k, v in _L3_gnn_all.items() if k in ('edge_emb_W', 'msg_W', 'msg_b', 'upd_W', 'upd_b', 'ln_g', 'ln_b')}
    del _L3_gnn_all
    return {'x': x, 'src': src, 'dst': dst, 'edge_attr_2': edge_attr_2, 'edge_attr_32': edge_attr_32, 'edge_type_16': edge_type_16, 'edge_type_2': edge_type_2, 'edge_weight': edge_weight, 'L0_gnn_Wq': _L0_gnn_in['Wq'], 'L0_gnn_Wk': _L0_gnn_in['Wk'], 'L0_gnn_Wv': _L0_gnn_in['Wv'], 'L0_gnn_rel_q': _L0_gnn_in['rel_q'], 'L0_gnn_rel_k': _L0_gnn_in['rel_k'], 'L0_gnn_rel_v': _L0_gnn_in['rel_v'], 'L0_gnn_Wt': _L0_gnn_in['Wt'], 'L0_gnn_bt': _L0_gnn_in['bt'], 'L0_gnn_Wd1': _L0_gnn_in['Wd1'], 'L0_gnn_bd1': _L0_gnn_in['bd1'], 'L0_gnn_Wd2': _L0_gnn_in['Wd2'], 'L0_gnn_bd2': _L0_gnn_in['bd2'], 'L0_gnn_decay_scale': _L0_gnn_in['decay_scale'], 'L0_gnn_c_mag': _L0_gnn_in['c_mag'], 'L0_gnn_hyp_beta': _L0_gnn_in['hyp_beta'], 'L0_gnn_logit_alpha': _L0_gnn_in['logit_alpha'], 'L0_gnn_Wo': _L0_gnn_in['Wo'], 'L0_gnn_bo': _L0_gnn_in['bo'], 'L0_gnn_g1': _L0_gnn_in['g1'], 'L0_gnn_be1': _L0_gnn_in['be1'], 'L0_gnn_g2': _L0_gnn_in['g2'], 'L0_gnn_be2': _L0_gnn_in['be2'], 'L0_gnn_Wf1': _L0_gnn_in['Wf1'], 'L0_gnn_bf1': _L0_gnn_in['bf1'], 'L0_gnn_Wf2': _L0_gnn_in['Wf2'], 'L0_gnn_bf2': _L0_gnn_in['bf2'], 'L1_gnn_W1': _L1_gnn_in['W1'], 'L1_gnn_w2': _L1_gnn_in['w2'], 'L2_gnn_W1': _L2_gnn_in['W1'], 'L2_gnn_b1': _L2_gnn_in['b1'], 'L2_gnn_gamma': _L2_gnn_in['gamma'], 'L2_gnn_beta': _L2_gnn_in['beta'], 'L2_gnn_W2': _L2_gnn_in['W2'], 'L2_gnn_b2': _L2_gnn_in['b2'], 'L3_gnn_edge_emb_W': _L3_gnn_in['edge_emb_W'], 'L3_gnn_msg_W': _L3_gnn_in['msg_W'], 'L3_gnn_msg_b': _L3_gnn_in['msg_b'], 'L3_gnn_upd_W': _L3_gnn_in['upd_W'], 'L3_gnn_upd_b': _L3_gnn_in['upd_b'], 'L3_gnn_ln_g': _L3_gnn_in['ln_g'], 'L3_gnn_ln_b': _L3_gnn_in['ln_b']}

def reference(x, src, dst, edge_attr_2, edge_attr_32, edge_type_16, edge_type_2, edge_weight, L0_gnn_Wq, L0_gnn_Wk, L0_gnn_Wv, L0_gnn_rel_q, L0_gnn_rel_k, L0_gnn_rel_v, L0_gnn_Wt, L0_gnn_bt, L0_gnn_Wd1, L0_gnn_bd1, L0_gnn_Wd2, L0_gnn_bd2, L0_gnn_decay_scale, L0_gnn_c_mag, L0_gnn_hyp_beta, L0_gnn_logit_alpha, L0_gnn_Wo, L0_gnn_bo, L0_gnn_g1, L0_gnn_be1, L0_gnn_g2, L0_gnn_be2, L0_gnn_Wf1, L0_gnn_bf1, L0_gnn_Wf2, L0_gnn_bf2, L1_gnn_W1, L1_gnn_w2, L2_gnn_W1, L2_gnn_b1, L2_gnn_gamma, L2_gnn_beta, L2_gnn_W2, L2_gnn_b2, L3_gnn_edge_emb_W, L3_gnn_msg_W, L3_gnn_msg_b, L3_gnn_upd_W, L3_gnn_upd_b, L3_gnn_ln_g, L3_gnn_ln_b):
    import jax
    import jax.numpy as jnp

    def _L0_gnn_ref(x, edge_index, time_emb, edge_type, edge_time, Wq, Wk, Wv, rel_q, rel_k, rel_v, Wt, bt, Wd1, bd1, Wd2, bd2, decay_scale, c_mag, hyp_beta, logit_alpha, Wo, bo, g1, be1, g2, be2, Wf1, bf1, Wf2, bf2):
        import jax, jax.numpy as jnp
        import numpy as np
        N = 3125
        E = 18750
        D = 128
        H = 8
        DH = D // H
        T = 32
        NET = 2

        def _ln(x, g, b, eps=1e-05):
            mu = jnp.mean(x, axis=-1, keepdims=True)
            var = jnp.mean((x - mu) ** 2, axis=-1, keepdims=True)
            return (x - mu) * jax.lax.rsqrt(var + eps) * g + b

        def _expmap(e, c):
            abs_c = jnp.maximum(jnp.abs(c), 1e-15)
            sq = jnp.sqrt(abs_c)
            n = jnp.maximum(jnp.linalg.norm(e, axis=-1, keepdims=True), 1e-15)
            tanh_p = jnp.tanh(sq * n) * e / (sq * n)
            tan_p = jnp.tan(sq * n) * e / (sq * n)
            return jnp.where(c < 0, tanh_p, tan_p)

        def _proj(x, c, eps=1e-05):
            abs_c = jnp.maximum(jnp.abs(c), 1e-15)
            maxnorm = (1.0 - eps) / jnp.sqrt(abs_c)
            norm = jnp.linalg.norm(x, axis=-1, keepdims=True)
            scale = jnp.where(norm > maxnorm, maxnorm / norm, jnp.ones_like(norm))
            return x * scale

        def _forward(x, time_emb, edge_time, Wq, Wk, Wv, rel_q, rel_k, rel_v, Wt, bt, Wd1, bd1, Wd2, bd2, decay_scale, c_mag, hyp_beta, logit_alpha, Wo, bo, g1, be1, g2, be2, Wf1, bf1, Wf2, bf2, src, dst, edge_type):
            n = x.shape[0]
            Q = (x @ Wq).reshape(n, H, DH)
            K = (x @ Wk).reshape(n, H, DH)
            V = (x @ Wv).reshape(n, H, DH)
            q_dst = Q[dst] + rel_q[edge_type].reshape(-1, H, DH)
            k_src = K[src] + rel_k[edge_type].reshape(-1, H, DH)
            v_src = V[src] + rel_v[edge_type].reshape(-1, H, DH)
            k_src = k_src + (time_emb @ Wt + bt).reshape(-1, H, DH)
            euclid = jnp.sum(q_dst * k_src, axis=-1) / np.float32(np.sqrt(DH))
            denom_t = jnp.maximum(1.0, edge_type.max().astype(jnp.float32) + 1.0)
            et = edge_type.astype(jnp.float32)[:, None] / denom_t
            dec_in = jnp.concatenate([edge_time[:, None], et], axis=-1)
            decay_raw = jnp.tanh(jax.nn.relu(dec_in @ Wd1 + bd1) @ Wd2 + bd2)
            decay = jnp.exp(decay_scale[None, :] * decay_raw)
            euclid = euclid * decay
            c = -jnp.abs(c_mag)
            m = _proj(_expmap(x, c), c)
            man_dist = jnp.linalg.norm(m[src] - m[dst], axis=-1)[:, None]
            hyp = -hyp_beta[None, :] * man_dist * decay
            alpha = jax.nn.sigmoid(logit_alpha)[None, :]
            logits = alpha * euclid + (1.0 - alpha) * hyp
            seg_max = jax.ops.segment_max(logits, dst, num_segments=n)
            ex = jnp.exp(logits - seg_max[dst])
            denom = jax.ops.segment_sum(ex, dst, num_segments=n)
            attn = ex / denom[dst]
            agg = jax.ops.segment_sum(v_src * attn[..., None], dst, num_segments=n).reshape(n, D)
            out = agg @ Wo + bo
            x = _ln(x + out, g1, be1)
            ffn = jax.nn.gelu(x @ Wf1 + bf1, approximate=False) @ Wf2 + bf2
            x = _ln(x + ffn, g2, be2)
            return x
        src, dst = (edge_index[0], edge_index[1])
        return _forward(x, time_emb, edge_time, Wq, Wk, Wv, rel_q, rel_k, rel_v, Wt, bt, Wd1, bd1, Wd2, bd2, decay_scale, c_mag, hyp_beta, logit_alpha, Wo, bo, g1, be1, g2, be2, Wf1, bf1, Wf2, bf2, src, dst, edge_type)

    def _L1_gnn_ref(N, W1, w2, src, dst):
        import jax, jax.numpy as jnp
        import numpy as np
        N_NODES = 50000
        N_EDGES = 25000
        D = 128
        n_nodes = N.shape[0]
        logit = jnp.tanh(N @ W1.T) @ w2
        e = logit[src]
        seg_max = jax.ops.segment_max(e, dst, num_segments=n_nodes)
        seg_max = jnp.where(jnp.isfinite(seg_max), seg_max, 0.0)
        ex = jnp.exp(e - seg_max[dst])
        denom = jax.ops.segment_sum(ex, dst, num_segments=n_nodes)
        a = ex / denom[dst]
        Np = jax.ops.segment_sum(a[:, None] * N[src], dst, num_segments=n_nodes)
        return Np

    def _L2_gnn_ref(x, edge_index, edge_attr, W1, b1, gamma, beta, W2, b2):
        import jax, jax.numpy as jnp
        import numpy as np
        N = 1250
        E = 20000
        CIN = 128
        COUT = 128
        EDGE_DIM = 2
        BN_EPS = 1e-05
        n_nodes = x.shape[0]
        row, col = (edge_index[0], edge_index[1])
        ef = jnp.concatenate([x[row], x[col], edge_attr], axis=-1)
        h = ef @ W1 + b1
        mu = jnp.mean(h, axis=0)
        var = jnp.mean((h - mu) ** 2, axis=0)
        h = (h - mu) * jax.lax.rsqrt(var + BN_EPS) * gamma + beta
        h = jax.nn.relu(h)
        msgs = h @ W2 + b2
        sums = jax.ops.segment_sum(msgs, row, num_segments=n_nodes)
        counts = jax.ops.segment_sum(jnp.ones((msgs.shape[0],), dtype=msgs.dtype), row, num_segments=n_nodes)
        out = sums / (counts + 1.0)[:, None]
        return out + x

    def _L3_gnn_ref(x, edge_index, edge_type, edge_emb_W, msg_W, msg_b, upd_W, upd_b, ln_g, ln_b):
        import jax, jax.numpy as jnp
        import numpy as np
        N, H = (50000, 128)
        E = 25000
        ETD = 32
        NUM_ET = 16
        LN_EPS = 1e-05
        src = edge_index[0]
        dst = edge_index[1]
        et = edge_emb_W[edge_type]
        m_in = jnp.concatenate([x[src], et], axis=-1)
        m = jax.nn.relu(m_in @ msg_W.T + msg_b)
        agg = jax.ops.segment_sum(m, dst, num_segments=x.shape[0])
        deg = jax.ops.segment_sum(jnp.ones_like(dst, dtype=x.dtype), dst, num_segments=x.shape[0])
        agg = agg / jnp.clip(deg, 1.0)[:, None]
        out = agg @ upd_W.T + upd_b
        h = x + out
        mu = jnp.mean(h, axis=-1, keepdims=True)
        var = jnp.mean((h - mu) ** 2, axis=-1, keepdims=True)
        return (h - mu) * jax.lax.rsqrt(var + LN_EPS) * ln_g + ln_b
    edge_index = jnp.stack([src, dst])
    h = jnp.maximum(_layernorm(x, axis=-1), 0.0)
    x = x + _L0_gnn_ref(h, edge_index, edge_attr_32, edge_type_2, edge_weight, L0_gnn_Wq, L0_gnn_Wk, L0_gnn_Wv, L0_gnn_rel_q, L0_gnn_rel_k, L0_gnn_rel_v, L0_gnn_Wt, L0_gnn_bt, L0_gnn_Wd1, L0_gnn_bd1, L0_gnn_Wd2, L0_gnn_bd2, L0_gnn_decay_scale, L0_gnn_c_mag, L0_gnn_hyp_beta, L0_gnn_logit_alpha, L0_gnn_Wo, L0_gnn_bo, L0_gnn_g1, L0_gnn_be1, L0_gnn_g2, L0_gnn_be2, L0_gnn_Wf1, L0_gnn_bf1, L0_gnn_Wf2, L0_gnn_bf2)
    h = jnp.maximum(_layernorm(x, axis=-1), 0.0)
    x = x + _L1_gnn_ref(h, L1_gnn_W1, L1_gnn_w2, src, dst)
    h = jnp.maximum(_layernorm(x, axis=-1), 0.0)
    x = x + _L2_gnn_ref(h, edge_index, edge_attr_2, L2_gnn_W1, L2_gnn_b1, L2_gnn_gamma, L2_gnn_beta, L2_gnn_W2, L2_gnn_b2)
    h = jnp.maximum(_layernorm(x, axis=-1), 0.0)
    x = x + _L3_gnn_ref(h, edge_index, edge_type_16, L3_gnn_edge_emb_W, L3_gnn_msg_W, L3_gnn_msg_b, L3_gnn_upd_W, L3_gnn_upd_b, L3_gnn_ln_g, L3_gnn_ln_b)
    return x

_drawn_inputs = setup_inputs


def setup_inputs(seed=0):
    import zlib

    import numpy as np

    out = dict(_drawn_inputs(seed))
    spreads = {'L0_gnn_bt': (0.0, 2.0),
     'L0_gnn_bd1': (0.0, 0.8),
     'L0_gnn_bd2': (0.0, 2.0),
     'L0_gnn_decay_scale': (0.5, 0.6),
     'L0_gnn_hyp_beta': (1.0, 0.6),
     'L0_gnn_logit_alpha': (0.0, 0.8),
     'L0_gnn_bo': (0.0, 0.1),
     'L0_gnn_g1': (1.0, 0.2),
     'L0_gnn_be1': (0.0, 0.1),
     'L0_gnn_g2': (1.0, 0.2),
     'L0_gnn_be2': (0.0, 0.1),
     'L0_gnn_bf1': (0.0, 0.1),
     'L0_gnn_bf2': (0.0, 0.1),
     'L2_gnn_gamma': (1.0, 0.2),
     'L2_gnn_beta': (0.0, 0.378),
     'L3_gnn_ln_g': (1.0, 0.2),
     'L3_gnn_ln_b': (0.0, 0.282)}
    factors = {'edge_attr_2': 8.0,
     'edge_weight': 8.0,
     'L0_gnn_Wk': 3.125,
     'L0_gnn_rel_q': 8.0,
     'L0_gnn_rel_k': 8.0,
     'L0_gnn_Wd1': 8.0,
     'L0_gnn_Wd2': 8.0,
     'L2_gnn_b1': 64.0,
     'L2_gnn_b2': 8.0,
     'L3_gnn_edge_emb_W': 5.169,
     'L3_gnn_msg_b': 8.0,
     'L3_gnn_upd_b': 2.868}
    for name, (base, spread) in spreads.items():
        noise = np.random.default_rng([zlib.crc32(name.encode()), seed]).standard_normal(out[name].shape)
        drawn = base * np.exp(spread * noise) if base else spread * noise
        out[name] = jnp.asarray(drawn.astype(out[name].dtype))
    for name, factor in factors.items():
        out[name] = (out[name] * factor).astype(out[name].dtype)
    return out
```

```python
from contextlib import ExitStack

import numpy as np

import concourse.bass as bass
from concourse import mybir

F32 = mybir.dt.float32
I32 = mybir.dt.int32
BF16 = mybir.dt.bfloat16
ALU = mybir.AluOpType
ACT = mybir.ActivationFunctionType
AX = mybir.AxisListType.X

P = 128
N, D = 3125, 128
E = 103125
H, DH = 8, 16
NET, T_DIM, HID = 2, 32, 64
NT16 = 16
NB = -(-N // P)
NLAST = N - (NB - 1) * P
TPB = 8
NBLK = -(-E // (P * TPB))
TT = NBLK * TPB
TC = -(-TT // P)
FULL = E // P
TAIL = E - FULL * P
PADKEY = 4095.0
BIG = float(2.0 ** 126)
EPS = 1e-5
NACC = 8
EW = TT * P


class Lane:

    def __init__(self, sem):
        self.sem, self.n = sem, 0

    def at(self):
        return (self.sem, self.n)


class Stream:

    def __init__(self, sem):
        self.sem, self.n, self.steps, self.reached = sem, 0, [], {}

    def wait(self, *events):
        for ev in events:
            if ev is None or self.reached.get(id(ev[0]), 0) >= ev[1]:
                continue
            self.reached[id(ev[0])] = ev[1]
            self.steps.append(lambda e, ev=ev: e.wait_ge(ev[0], ev[1]))

    def do(self, fn):
        self.n += 1
        self.steps.append(lambda e: fn(e).then_inc(self.sem, 1))
        return (self.sem, self.n)

    def quiet(self, fn):
        self.steps.append(fn)

    def chain(self, fn):
        ev = self.do(fn)
        self.wait(ev)
        return ev

    def dma(self, lane, out, in_, **kw):
        lane.n += 16
        self.steps.append(lambda e: e.dma_start(out, in_, **kw).then_inc(lane.sem, 16))
        return (lane.sem, lane.n)

    def gather(self, lane, out, table, idx):
        lane.n += 16
        self.steps.append(lambda e: e.indirect_dma_start(
            out, None, table, bass.IndirectOffsetOnAxis(ap=idx, axis=0)).then_inc(lane.sem, 16))
        return (lane.sem, lane.n)

    def scatter_add(self, lane, table, idx, in_):
        lane.n += 16
        self.steps.append(lambda e: e.indirect_dma_start(
            table, bass.IndirectOffsetOnAxis(ap=idx, axis=0), in_, None,
            compute_op=ALU.add).then_inc(lane.sem, 16))
        return (lane.sem, lane.n)

    def play(self, eng):
        for step in self.steps:
            step(eng)


def bc(ap, axis, n):
    shape = list(ap.shape)
    return ap.unsqueeze(axis).broadcast_to(shape[:axis] + [n] + shape[axis:])


def program(nc, a, out):
    ctx = ExitStack()
    with ctx:
        def sb(name, shape, dt=F32):
            return ctx.enter_context(nc.sbuf_tensor(name, shape, dt))

        def dram(name, shape, dt=F32):
            return nc.dram_tensor(name, shape, dt).ap()

        def lane(name):
            return Lane(ctx.enter_context(nc.semaphore(name)))

        def stream(name):
            return Stream(ctx.enter_context(nc.semaphore(name)))

        SP, PL, AC, VE, PE = (stream(n) for n in ("sp_done", "pool_done", "act_done", "dve_done", "pe_done"))

        bank = [ctx.enter_context(nc.psum_tensor(f"bank{i}", [P, 512], F32)) for i in range(8)]

        src0 = dram("src_table0", [NET * N, 3 * D])
        dst0 = dram("dst_table0", [NET * N, 2 * D])
        tab1 = dram("table1", [N, D + 1])
        tab2a = dram("table2a", [N, D])
        tab2b = dram("table2b", [N, D])
        tab3 = dram("table3", [N, D])
        W_Y = (D + 2 * H, D + 2, None, D)
        y_rows = {L: dram(f"y_rows{L}", [EW, W_Y[L]]) for L in (0, 1, 3)}
        c_rows = {L: dram(f"carry_rows{L}", [TT, W_Y[L]]) for L in (0, 1, 3)}
        h_rows = dram("h_rows", [EW, D])
        acc_rows = [dram(f"acc_rows{i}", [N + P, D + 1]) for i in range(NACC)]
        dst_keys = dram("dst_keys", [TC * P, P])
        dst_hl = dram("dst_hl", [2, TC * P * P], BF16)
        src_hl = dram("src_hl", [2, TC * P * P], BF16)
        dec_rows = dram("dec_rows", [4, TC * P * P])
        run_rows = dram("run_rows", [2, TC * P, P])
        t16_row = dram("t16_row", [1, TC * P * P])
        ea2_rows = dram("ea2_rows", [2, TC * P * P])
        first_last = dram("first_last", [2, TC * P])
        end_pos = dram("end_pos", [NB * P + 1])

        ident = sb("ident", [P, P])
        lower = sb("lower", [P, P])
        ones = sb("ones", [P, P])
        hilo_w = sb("hilo_w", [2, P], BF16)
        junk = sb("junk", [P, 1])
        node_id = sb("node_id", [P, NB])
        iota16 = sb("iota16", [NT16, 1])
        rep8 = sb("rep8", [H, D])
        edge_ok = sb("edge_ok", [P, TPB])

        X = sb("X", [P, NB, D])
        Hn = sb("Hn", [P, NB, D])
        stat = sb("stat", [P, 8, NB])

        src_col = sb("src_col", [P, TC * P])
        dst_col = sb("dst_col", [P, TC * P])
        src_ix = sb("src_ix", [P, TC * P], I32)
        dst_ix = sb("dst_ix", [P, TC * P], I32)
        src_tix = sb("src_tix", [P, TC * P], I32)
        dst_tix = sb("dst_tix", [P, TC * P], I32)

        RING = 4
        arena_a = sb("arena_a", [P, RING * TPB * 3 * D])
        arena_b = sb("arena_b", [P, 2 * NB * D])
        HT = arena_a[:, RING * TPB * 3 * D - NB * P:RING * TPB * 3 * D]
        GS = [arena_a[:, s * TPB * 3 * D:(s + 1) * TPB * 3 * D].rearrange("p (t w) -> p t w", t=TPB) for s in range(RING)]
        RING_D = 3
        GD = [arena_b[:, s * TPB * 2 * D:(s + 1) * TPB * 2 * D].rearrange("p (t w) -> p t w", t=TPB) for s in range(RING_D)]
        WMAX = D + 2 * H
        YE_flat = arena_a[:, 0:NB * WMAX]
        CE_flat = arena_a[:, NB * WMAX:2 * NB * WMAX]
        S1 = arena_b[:, 0:NB * D].rearrange("p (b d) -> p b d", b=NB)
        S2 = arena_b[:, NB * D:2 * NB * D].rearrange("p (b d) -> p b d", b=NB)

        same = [sb(f"same{s}", [P, TPB, P]) for s in range(2)]
        msg = [sb(f"msg{s}", [P, TPB, D + H]) for s in range(2)]
        ybuf = [sb(f"ybuf{s}", [P, TPB, WMAX]) for s in range(2)]
        hl = [sb(f"hl{s}", [2, TPB * P], BF16) for s in range(2)]
        rows4 = [sb(f"rows4_{s}", [NT16, TPB * P]) for s in range(2)]
        ea = [sb(f"ea{s}", [P, TPB, T_DIM]) for s in range(2)]
        eat = [sb(f"eat{s}", [P, 2, P]) for s in range(2)]
        runs = [sb(f"runs{s}", [TPB * H, 2, P]) for s in range(2)]
        hid = [sb(f"hid{s}", [HID + 1, TPB * P]) for s in range(2)]
        small = [sb(f"small{s}", [P, 8, TPB * H]) for s in range(2)]
        tlog = [sb(f"tlog{s}", [TPB * H, 4, P]) for s in range(2)]
        add_ix = [sb(f"add_ix{s}", [P, TPB], I32) for s in range(2)]

        Wqkv = sb("Wqkv", [P, 3 * D])
        relb = sb("relb", [P, NET, 3 * D])
        btb = sb("btb", [P, D])
        Wt4 = sb("Wt4", [P, 4 * D])
        Wd1a = sb("Wd1a", [4, HID])
        Wd2a = sb("Wd2a", [HID + 1, H])
        hrow = sb("hrow", [P, 4, H])
        wsq = sb("wsq", [P, 6, D])
        wtmp = sb("wtmp", [P, D + 2 * T_DIM])
        frow = sb("frow", [P, 8, D])
        Wf1 = sb("Wf1", [P, 4 * D])
        Wf2 = sb("Wf2", [P, 4, D])
        bf1 = sb("bf1", [P, 4])
        We3 = sb("We3", [T_DIM, D])
        emb = sb("emb", [NT16, T_DIM])
        embT = sb("embT", [T_DIM, NT16])
        Em = sb("Em", [NT16, D])
        W1c = sb("W1c", [2, D])
        cmag = sb("cmag", [P, 8])

        end_ix = sb("end_ix", [P, NB], I32)
        tile_ix = sb("tile_ix", [P, NB], I32)
        npos = sb("npos", [P, 8, NB])
        has_carry, degree, valid = npos[:, 5, :], npos[:, 6, :], npos[:, 7, :]
        chain_row = sb("chain_row", [P, TT])
        first_row = src_tix[:, 0:TT].bitcast(F32)
        last_row = dst_tix[:, 0:TT].bitcast(F32)

        l_w = lane("d_weights")
        l_w2 = lane("d_weights_later")
        l_frow = lane("d_feature_rows")
        l_stage = [lane(f"d_stage{s}") for s in range(2)]
        l_x = lane("d_x")
        l_prep = lane("d_prep")
        l_tab = lane("d_tables")
        l_rows = [lane(f"d_rows{s}") for s in range(2)]
        l_hl = [lane(f"d_hl{s}") for s in range(2)]
        l_runs = [lane(f"d_runs{s}") for s in range(2)]
        l_gs = [lane(f"d_src_rows{s}") for s in range(RING)]
        l_gd = [lane(f"d_dst_rows{s}") for s in range(RING_D)]
        l_y = [lane(f"d_y{s}") for s in range(2)]
        l_node = lane("d_node")
        l_nodeg = lane("d_node_gathers")
        l_hin = [lane(f"d_h_rows{s}") for s in range(RING)]
        l_acc = [lane(f"d_acc{i}") for i in range(NACC)]
        l_zero = lane("d_zero")
        l_out = lane("d_out")

        def row_bc(ap, parts=P):
            return ap.unsqueeze(0).broadcast_to([parts] + list(ap.shape))

        def col(ap):
            return ap.unsqueeze(1)

        c = []
        c.append(VE.do(lambda e: e.memset(ident[:, :], 0.0)))
        c.append(VE.do(lambda e: e.memset(lower[:, :], 1.0)))
        c.append(VE.do(lambda e: e.memset(ones[:, :], 1.0)))
        c.append(VE.do(lambda e: e.memset(hilo_w[:, :], 1.0)))
        c.append(VE.do(lambda e: e.memset(rep8[:, :], 1.0)))
        c.append(VE.do(lambda e: e.memset(edge_ok[:, :], 1.0)))
        PL.wait(c[-1])
        PL.do(lambda e: e.affine_select(out=ident[:, :], in_=ident[:, :], compare_op=ALU.not_equal, fill=1.0,
                                        base=0, pattern=[[-1, P]], channel_multiplier=1))
        PL.do(lambda e: e.affine_select(out=lower[:, :], in_=lower[:, :], compare_op=ALU.is_gt, fill=0.0,
                                        base=0, pattern=[[-1, P]], channel_multiplier=1))
        PL.do(lambda e: e.affine_select(out=hilo_w[:, :], in_=hilo_w[:, :], compare_op=ALU.is_gt, fill=64.0,
                                        base=0, pattern=[[0, P]], channel_multiplier=1))
        k = PL.do(lambda e: e.affine_select(out=rep8[:, :], in_=rep8[:, :], compare_op=ALU.is_ge, fill=0.0,
                                            base=0, pattern=[[1, D]], channel_multiplier=-DH))
        PL.wait(k)
        PL.do(lambda e: e.affine_select(out=rep8[:, :], in_=rep8[:, :], compare_op=ALU.is_ge, fill=0.0,
                                        base=DH - 1, pattern=[[-1, D]], channel_multiplier=DH))
        PL.do(lambda e: e.affine_select(out=edge_ok[:, :], in_=edge_ok[:, :], compare_op=ALU.is_ge, fill=0.0,
                                        base=E - 1 - (NBLK - 1) * TPB * P, pattern=[[-P, TPB]], channel_multiplier=-1))
        PL.do(lambda e: e.iota(junk[:, :], [[0, 1]], base=N, channel_multiplier=1, allow_small_or_imprecise_dtypes=True))
        PL.do(lambda e: e.iota(node_id[:, :], [[P, NB]], base=0, channel_multiplier=1, allow_small_or_imprecise_dtypes=True))
        const_ready = PL.do(lambda e: e.iota(iota16[:, :], [[0, 1]], base=0, channel_multiplier=1, allow_small_or_imprecise_dtypes=True))

        pad = [VE.do(lambda e: e.memset(X[:, NB - 1, :], 0.0))]
        SP.wait(pad[0])
        x_in = a["x"]
        SP.dma(l_x, X[:, 0:NB - 1, :], x_in[0:(NB - 1) * P, :].rearrange("(b p) d -> p b d", p=P))
        x_ready = SP.dma(l_x, X[0:NLAST, NB - 1, :], x_in[(NB - 1) * P:N, :])

        keys_i = arena_a[:, 0:5 * TC * P].bitcast(I32).rearrange("p (k c f) -> p k c f", k=5, c=TC)
        keys_f = arena_a[:, 5 * TC * P:10 * TC * P].rearrange("p (k c f) -> p k c f", k=5, c=TC)
        tmp_f = arena_b[:, 0:6 * TC * P].rearrange("p (k c f) -> p k c f", k=6, c=TC)
        SRC, DST, TY2, TY16, WGT = range(5)

        def load_tiled(lane_, dst_view, ap, w):
            c6 = (TC - 1) * P * P
            SP.dma(lane_, dst_view[:, 0:TC - 1, :], ap[0:c6 * w].rearrange("(c p f) -> p c f", p=P, f=P * w))
            rest = FULL - (TC - 1) * P
            SP.dma(lane_, dst_view[0:rest, TC - 1, :],
                   ap[c6 * w:FULL * P * w].rearrange("(p f) -> p f", f=P * w))
            return SP.dma(lane_, dst_view[rest:rest + 1, TC - 1, 0:TAIL * w],
                          ap[FULL * P * w:E * w].unsqueeze(0))

        pads = []
        for k_, v_ in ((SRC, int(PADKEY)), (DST, int(PADKEY)), (TY2, 0), (TY16, 0)):
            pads.append(VE.do(lambda e, k_=k_, v_=v_: e.memset(keys_i[:, k_, TC - 1, :], v_)))
        pads.append(VE.do(lambda e: e.memset(keys_f[:, WGT, TC - 1, :], 0.0)))
        SP.wait(pads[-1])
        load_tiled(l_prep, keys_i[:, SRC], a["src"], 1)
        load_tiled(l_prep, keys_i[:, DST], a["dst"], 1)
        load_tiled(l_prep, keys_i[:, TY2], a["edge_type_2"], 1)
        load_tiled(l_prep, keys_i[:, TY16], a["edge_type_16"], 1)
        lists_in = load_tiled(l_prep, keys_f[:, WGT], a["edge_weight"], 1)

        def w_dma(dst_, src_):
            return SP.dma(l_w, dst_, src_)

        for i, n_ in enumerate(("Wq", "Wk", "Wv")):
            w_dma(Wqkv[:, i * D:(i + 1) * D], a["L0_gnn_" + n_])
        for i, n_ in enumerate(("rel_q", "rel_k", "rel_v")):
            w_dma(relb[:, :, i * D:(i + 1) * D], row_bc(a["L0_gnn_" + n_]))
        w_dma(btb[:, :], row_bc(a["L0_gnn_bt"]))
        SP.wait(VE.do(lambda e: e.memset(Wt4[:, :], 0.0)))
        for i in range(4):
            w_dma(Wt4[i * T_DIM:(i + 1) * T_DIM, i * D:(i + 1) * D], a["L0_gnn_Wt"])
        w_dma(Wd1a[0:2, :], a["L0_gnn_Wd1"])
        w_dma(Wd1a[2:4, :], row_bc(a["L0_gnn_bd1"], 2))
        w_dma(Wd2a[0:HID, :], a["L0_gnn_Wd2"])
        w_dma(Wd2a[HID:HID + 1, :], row_bc(a["L0_gnn_bd2"], 1))
        w_dma(hrow[:, 0, :], row_bc(a["L0_gnn_decay_scale"]))
        w_dma(hrow[:, 1, :], row_bc(a["L0_gnn_logit_alpha"]))
        w_dma(hrow[:, 2, :], row_bc(a["L0_gnn_hyp_beta"]))
        w_dma(cmag[:, 0:1], a["L0_gnn_c_mag"].unsqueeze(0).broadcast_to([P, 1]))
        weights_first = w_dma(wsq[:, 0, :], a["L0_gnn_Wo"])

        VE.wait(lists_in)
        AC.wait(lists_in)
        k = VE.do(lambda e: e.tensor_copy(keys_f[:, 0:4], keys_i[:, 0:4]))
        VE.wait(k)
        hi_i, lo_i = tmp_f[:, 0:1].bitcast(I32), tmp_f[:, 1:2].bitcast(I32)
        hb = arena_b[:, 2 * TC * P:4 * TC * P].bitcast(BF16).rearrange("p (k c f) -> p k c f", k=4, c=TC)
        halves_out = []
        for j, key in enumerate((SRC, DST)):
            VE.do(lambda e, key=key: e.tensor_scalar(hi_i[:, 0], keys_i[:, key], 6, None, ALU.arith_shift_right))
            k = VE.do(lambda e, key=key: e.tensor_scalar(lo_i[:, 0], keys_i[:, key], 63, None, ALU.bitwise_and))
            VE.wait(k)
            VE.do(lambda e, j=j: e.tensor_copy(hb[:, 2 * j], hi_i[:, 0]))
            k = VE.chain(lambda e, j=j: e.tensor_copy(hb[:, 2 * j + 1], lo_i[:, 0]))
            SP.wait(k)
            for i in range(2):
                SP.dma(l_tab, (src_hl, dst_hl)[j][i, :].rearrange("(c p f) -> p c f", p=P, f=P), hb[:, 2 * j + i])
        src_c, dst_c, src_t, dst_t = (tmp_f[:, i] for i in (4, 5, 0, 1))
        for o_, key in ((src_c, SRC), (dst_c, DST)):
            k = VE.do(lambda e, o_=o_, key=key: e.scalar_tensor_tensor(
                out=o_, in0=keys_f[:, key], scalar=float(N), in1=keys_f[:, key], op0=ALU.is_lt, op1=ALU.mult))
        VE.wait(k)
        VE.do(lambda e: e.scalar_tensor_tensor(out=src_t, in0=keys_f[:, TY2], scalar=float(N), in1=src_c, op0=ALU.mult, op1=ALU.add))
        lists_ready = VE.do(lambda e: e.scalar_tensor_tensor(out=dst_t, in0=keys_f[:, TY2], scalar=float(N), in1=dst_c, op0=ALU.mult, op1=ALU.add))
        PE.wait(const_ready, lists_ready)
        bank_free = [None] * 8
        cols_ready = None
        for n_, (view, outs_) in enumerate(((keys_f[:, SRC], src_col), (keys_f[:, DST], dst_col), (src_c, src_ix),
                                            (dst_c, dst_ix), (src_t, src_tix), (dst_t, dst_tix))):
            for half in range(2):
                bk = (2 * n_ + half) % 4
                cs = range(4 * half, min(4 * half + 4, TC))
                PE.wait(bank_free[bk])
                for q in cs[:-1]:
                    PE.quiet(lambda e, bk=bk, q=q, view=view: e.transpose(bank[bk][:, (q % 4) * P:(q % 4 + 1) * P], view[:, q, :], ident[:, :]))
                q = cs[-1]
                k = PE.do(lambda e, bk=bk, q=q, view=view: e.transpose(bank[bk][:, (q % 4) * P:(q % 4 + 1) * P], view[:, q, :], ident[:, :]))
                eng = AC if half else VE
                eng.wait(k)
                w_ = len(cs) * P
                if half:
                    bank_free[bk] = AC.do(lambda e, bk=bk, w_=w_, outs_=outs_: e.activation(outs_[:, 4 * P:4 * P + w_], bank[bk][:, 0:w_], ACT.Copy))
                else:
                    bank_free[bk] = VE.do(lambda e, bk=bk, w_=w_, outs_=outs_: e.tensor_copy(outs_[:, 0:w_], bank[bk][:, 0:w_]))
        cols_ready = (bank_free[0], bank_free[1], bank_free[2], bank_free[3])
        pe_lists_done = k

        k = VE.do(lambda e: e.tensor_reduce(cmag[:, 1:2], keys_f[:, TY2], mybir.AxisListType.XY, ALU.max))
        PE.wait(k, bank_free[0])
        k = PE.do(lambda e: e.transpose(bank[4][0:1, 0:P], cmag[:, 1:2], ident[:, :]))
        VE.wait(k)
        VE.chain(lambda e: e.tensor_reduce(cmag[0:1, 2:3], bank[4][0:1, 0:P], AX, ALU.max))
        k = VE.do(lambda e: e.tensor_scalar(cmag[0:1, 3:4], cmag[0:1, 2:3], 1.0, 1.0, ALU.add, ALU.max))
        PE.wait(k)
        k = PE.do(lambda e: e.matmul(bank[4][:, 256:257], ones[0:1, :], cmag[0:1, 3:4], start=True, stop=True))
        VE.wait(k)
        VE.chain(lambda e: e.reciprocal(cmag[:, 4:5], bank[4][:, 256:257]))
        VE.wait(pe_lists_done)
        et, oh0, rF, rB = (tmp_f[:, i] for i in (0, 1, 4, 5))
        VE.do(lambda e: e.tensor_scalar(et, keys_f[:, TY2], cmag[:, 4:5], None, ALU.mult))
        k = VE.do(lambda e: e.tensor_scalar(oh0, keys_f[:, TY2], 0.0, None, ALU.is_equal))
        SP.wait(k)
        for i, v_ in enumerate((keys_f[:, WGT], et, oh0, keys_f[:, TY2])):
            SP.dma(l_tab, dec_rows[i, :].rearrange("(c p f) -> p c f", p=P, f=P), v_)
        SP.dma(l_tab, t16_row[0, :].rearrange("(c p f) -> p c f", p=P, f=P), keys_f[:, TY16])
        SP.dma(l_tab, dst_keys.rearrange("(c p) f -> p c f", p=P), keys_f[:, DST])
        SP.dma(l_tab, first_last[0, :].rearrange("(c p) -> p c", p=P), keys_f[:, DST, :, 0], allow_slow_non_contiguous=True)
        SP.dma(l_tab, first_last[1, :].rearrange("(c p) -> p c", p=P), keys_f[:, DST, :, P - 1], allow_slow_non_contiguous=True)
        VE.do(lambda e: e.memset(rF[:, :, 0:1], 1.0))
        VE.do(lambda e: e.memset(rB[:, :, P - 1:P], 1.0))
        VE.do(lambda e: e.tensor_tensor(rF[:, :, 1:P], keys_f[:, DST, :, 1:P], keys_f[:, DST, :, 0:P - 1], ALU.is_equal))
        k = VE.do(lambda e: e.tensor_tensor(rB[:, :, 0:P - 1], keys_f[:, DST, :, 1:P], keys_f[:, DST, :, 0:P - 1], ALU.is_equal))
        VE.wait(k)
        VE.do(lambda e: e.tensor_scalar(rF, rF, BIG, -BIG, ALU.mult, ALU.add))
        k = VE.do(lambda e: e.tensor_scalar(rB, rB, BIG, -BIG, ALU.mult, ALU.add))
        SP.wait(k)
        SP.dma(l_tab, run_rows[0].rearrange("(c p) f -> p c f", p=P), rF)
        lists_out = SP.dma(l_tab, run_rows[1].rearrange("(c p) f -> p c f", p=P), rB)

        def norm_rows(src_v, dst_v, ready, scratch):
            mu, var = stat[:, 0, :], stat[:, 1, :]
            VE.wait(*ready)
            VE.chain(lambda e: e.tensor_reduce(mu, src_v, AX, ALU.add))
            VE.chain(lambda e: e.tensor_scalar(mu, mu, 1.0 / D, None, ALU.mult))
            k = VE.chain(lambda e: e.tensor_tensor(dst_v, src_v, bc(mu, 2, D), ALU.subtract))
            AC.wait(k)
            k = AC.do(lambda e: e.activation(scratch, dst_v, ACT.Square))
            VE.wait(k)
            VE.chain(lambda e: e.tensor_reduce(var, scratch, AX, ALU.add))
            VE.chain(lambda e: e.tensor_scalar(var, var, 1.0 / D, EPS, ALU.mult, ALU.add))
            k = VE.chain(lambda e: e.reciprocal(var, var))
            AC.wait(k)
            k = AC.do(lambda e: e.activation(var, var, ACT.Sqrt))
            VE.wait(k)
            return VE.chain(lambda e: e.tensor_tensor(dst_v, dst_v, bc(var, 2, D), ALU.mult))

        def relu_norm(ready):
            norm_rows(X[:, :, :], Hn[:, :, :], ready, S2)
            return VE.chain(lambda e: e.tensor_scalar(Hn[:, :, :], Hn[:, :, :], 0.0, None, ALU.max))

        def transpose_nodes(src_v, dst_, ready):
            PE.wait(*ready)
            free = [None, None]
            last = None
            for g in range(-(-NB // 4)):
                bs = list(range(4 * g, min(4 * g + 4, NB)))
                bk = 4 + g % 2
                PE.wait(free[g % 2])
                for b in bs:
                    fn = lambda e, b=b, bk=bk: e.transpose(bank[bk][:, (b % 4) * P:(b % 4 + 1) * P], src_v[:, b, :], ident[:, :])
                    if b == bs[-1]:
                        k = PE.do(fn)
                    else:
                        PE.quiet(fn)
                w_ = len(bs) * P
                if g % 2:
                    VE.wait(k)
                    last = free[1] = VE.do(lambda e, bk=bk, w_=w_, g=g: e.tensor_copy(dst_[:, 4 * g * P:4 * g * P + w_], bank[bk][:, 0:w_]))
                else:
                    AC.wait(k)
                    last = free[0] = AC.do(lambda e, bk=bk, w_=w_, g=g: e.activation(dst_[:, 4 * g * P:4 * g * P + w_], bank[bk][:, 0:w_], ACT.Copy))
            return (free[0], free[1])

        def transpose_weight(src_, dst_, ready, parts=P, width=P):
            PE.wait(*ready)
            k = PE.do(lambda e: e.transpose(bank[6][0:width, 0:parts], src_, ident[0:parts, 0:parts]))
            VE.wait(k)
            k = VE.do(lambda e: e.tensor_copy(dst_, bank[6][0:width, 0:parts]))
            PE.wait(k)
            return k

        def store_nodes(tab, view, lane_):
            SP.dma(lane_, tab[0:(NB - 1) * P, :].rearrange("(b p) w -> p b w", p=P), view[:, 0:NB - 1, :])
            return SP.dma(lane_, tab[(NB - 1) * P:N, :], view[0:NLAST, NB - 1, :])

        h_ready = relu_norm((x_ready, lists_out))
        ht_ready = transpose_nodes(Hn, HT, (h_ready,))
        VE.wait(weights_first)
        AC.wait(weights_first)
        s_ = lambda i: stat[:, i, :]
        AC.do(lambda e: e.activation(S2, Hn[:, :, :], ACT.Square))
        k = (AC.sem, AC.n)
        VE.wait(k)
        VE.chain(lambda e: e.tensor_scalar(cmag[:, 1:2], cmag[:, 0:1], -1.0, None, ALU.mult))
        VE.chain(lambda e: e.tensor_tensor(cmag[:, 1:2], cmag[:, 0:1], cmag[:, 1:2], ALU.max))
        VE.chain(lambda e: e.tensor_scalar(cmag[:, 5:6], cmag[:, 1:2], 0.0, None, ALU.is_gt))
        k = VE.chain(lambda e: e.tensor_scalar(cmag[:, 1:2], cmag[:, 1:2], 1e-15, None, ALU.max))
        AC.wait(k)
        k = AC.do(lambda e: e.activation(cmag[:, 2:3], cmag[:, 1:2], ACT.Sqrt))
        VE.wait(k)
        VE.chain(lambda e: e.reciprocal(cmag[:, 3:4], cmag[:, 2:3]))
        VE.chain(lambda e: e.tensor_scalar(cmag[:, 3:4], cmag[:, 3:4], 1.0 - 1e-5, None, ALU.mult))
        k = VE.chain(lambda e: e.tensor_reduce(s_(2), S2, AX, ALU.add))
        AC.wait(k)
        k = AC.do(lambda e: e.activation(s_(2), s_(2), ACT.Sqrt))
        VE.wait(k)
        VE.chain(lambda e: e.tensor_scalar(s_(2), s_(2), 1e-15, None, ALU.max))
        k = VE.chain(lambda e: e.tensor_scalar(s_(3), s_(2), cmag[:, 2:3], None, ALU.mult))
        AC.wait(k)
        k = AC.do(lambda e: e.activation(s_(4), s_(3), ACT.Tanh))
        VE.chain(lambda e: e.reciprocal(s_(5), s_(3)))
        VE.wait(k)
        VE.chain(lambda e: e.tensor_tensor(s_(4), s_(4), s_(5), ALU.mult))
        VE.chain(lambda e: e.tensor_tensor(s_(5), s_(3), s_(3), ALU.mult))
        VE.chain(lambda e: e.tensor_scalar(s_(5), s_(5), 1.0 / 3.0, 1.0, ALU.mult, ALU.add))
        VE.chain(lambda e: e.tensor_tensor(s_(4), s_(4), s_(5), ALU.subtract))
        VE.chain(lambda e: e.scalar_tensor_tensor(out=s_(4), in0=s_(4), scalar=cmag[:, 5:6], in1=s_(5), op0=ALU.mult, op1=ALU.add))
        VE.chain(lambda e: e.tensor_tensor(s_(5), s_(4), s_(2), ALU.mult))
        VE.chain(lambda e: e.tensor_scalar(s_(6), s_(5), 1e-30, None, ALU.max))
        VE.chain(lambda e: e.reciprocal(s_(6), s_(6)))
        VE.chain(lambda e: e.tensor_scalar(s_(6), s_(6), cmag[:, 3:4], -1.0, ALU.mult, ALU.add))
        VE.chain(lambda e: e.tensor_scalar(s_(5), s_(5), cmag[:, 3:4], None, ALU.is_gt))
        VE.chain(lambda e: e.tensor_tensor(s_(6), s_(6), s_(5), ALU.mult))
        VE.chain(lambda e: e.tensor_scalar(s_(6), s_(6), 1.0, None, ALU.add))
        VE.chain(lambda e: e.tensor_tensor(s_(4), s_(4), s_(6), ALU.mult))
        m_ready = VE.chain(lambda e: e.tensor_tensor(S1, Hn[:, :, :], bc(s_(4), 2, D), ALU.mult))
        k = AC.do(lambda e: e.activation(hrow[:, 3, :], hrow[:, 1, :], ACT.Exp, scale=-1.0))
        VE.wait(k)
        VE.chain(lambda e: e.tensor_scalar(hrow[:, 3, :], hrow[:, 3, :], 1.0, None, ALU.add))
        VE.chain(lambda e: e.reciprocal(hrow[:, 3, :], hrow[:, 3, :]))
        VE.chain(lambda e: e.tensor_scalar(hrow[:, 1, :], hrow[:, 3, :], DH ** -0.5, None, ALU.mult))
        VE.chain(lambda e: e.tensor_scalar(hrow[:, 3, :], hrow[:, 3, :], -1.0, 1.0, ALU.mult, ALU.add))
        VE.chain(lambda e: e.tensor_tensor(hrow[:, 2, :], hrow[:, 2, :], hrow[:, 3, :], ALU.mult))
        VE.chain(lambda e: e.tensor_tensor(relb[:, :, D:2 * D], relb[:, :, D:2 * D], bc(btb[:, :], 1, NET), ALU.add))
        PE.wait(ht_ready[0], ht_ready[1], weights_first)
        free, sent = [None, None], [None, None]
        AC.wait(m_ready)
        for b in range(NB):
            s = b % 2
            stage_s = arena_a[:, s * 1280:s * 1280 + 768].rearrange("p (y w) -> p y w", y=NET)
            stage_d = arena_a[:, s * 1280 + 768:s * 1280 + 1280].rearrange("p (y w) -> p y w", y=NET)
            PE.wait(free[s])
            k = PE.do(lambda e, b=b, s=s: e.matmul(bank[s][:, 0:3 * D], HT[:, b * P:(b + 1) * P], Wqkv[:, :], start=True, stop=True))
            VE.wait(k, sent[s])
            VE.do(lambda e, s=s, st=stage_s: e.tensor_tensor(st[:, :, 0:2 * D], bc(bank[s][:, D:3 * D], 1, NET), relb[:, :, D:3 * D], ALU.add))
            free[s] = VE.do(lambda e, s=s, st=stage_d: e.tensor_tensor(st[:, :, 0:D], bc(bank[s][:, 0:D], 1, NET), relb[:, :, 0:D], ALU.add))
            AC.wait(sent[s])
            AC.do(lambda e, b=b, st=stage_s: e.activation(st[:, :, 2 * D:3 * D], bc(S1[:, b, :], 1, NET), ACT.Copy))
            k = AC.do(lambda e, b=b, st=stage_d: e.activation(st[:, :, D:2 * D], bc(S1[:, b, :], 1, NET), ACT.Copy))
            SP.wait(k, free[s])
            np_ = P if b < NB - 1 else NLAST
            SP.dma(l_stage[s], src0.rearrange("(y n) w -> n y w", y=NET)[b * P:b * P + np_], stage_s[0:np_])
            sent[s] = SP.dma(l_stage[s], dst0.rearrange("(y n) w -> n y w", y=NET)[b * P:b * P + np_], stage_d[0:np_])
        tables0 = sent

        def w_dma2(dst_, src_):
            return SP.dma(l_w2, dst_, src_)

        for i, n_ in ((1, "L1_gnn_W1"), (2, "L2_gnn_W2"), (5, "L3_gnn_upd_W")):
            w_dma2(wsq[:, i, :], a[n_])
        w_dma2(wsq[:, 3, :], a["L2_gnn_W1"][0:D, :])
        w_dma2(wsq[:, 4, :], a["L2_gnn_W1"][D:2 * D, :])
        w_dma2(W1c[:, :], a["L2_gnn_W1"][2 * D:2 * D + 2, :])
        w_dma2(wtmp[:, 0:D + T_DIM], a["L3_gnn_msg_W"])
        w_dma2(emb[:, :], a["L3_gnn_edge_emb_W"])
        w_dma2(Wf1[:, :], a["L0_gnn_Wf1"])
        w_dma2(Wf2[:, :, :], a["L0_gnn_Wf2"].rearrange("(c p) n -> p c n", p=P))
        weights_rest = SP.dma(
            l_w2, bf1[:, :], a["L0_gnn_bf1"].rearrange("(c p) -> p c", p=P), allow_slow_non_contiguous=True)

        frow_sets = {
            0: ("L0_gnn_bo", "L0_gnn_g1", "L0_gnn_be1", "L0_gnn_bf2", "L0_gnn_g2", "L0_gnn_be2"),
            1: ("L1_gnn_w2",),
            2: ("L2_gnn_b1", "L2_gnn_b2"),
            3: ("L3_gnn_msg_b", "L3_gnn_upd_b", "L3_gnn_ln_g", "L3_gnn_ln_b"),
        }

        def load_frow(L, after):
            SP.wait(*after)
            for i, n_ in enumerate(frow_sets[L]):
                k = SP.dma(l_frow, frow[:, i, :], row_bc(a[n_]))
            return k

        frow_ready = load_frow(0, ())

        ev = {}

        def got(name, k_):
            return ev.get((name, k_))

        def load_keys(L, k_, rows):
            s = k_ % 2
            SP.wait(got("keys_read", (L, k_ - 2)))
            ev[("keys", (L, k_))] = SP.dma(l_hl[s], hl[s][:, :], rows[:, k_ * TPB * P:(k_ + 1) * TPB * P])

        def load_runs(L, k_, nh):
            s = k_ % 2
            SP.wait(got("scan", (L, k_ - 2)))
            for i in range(2):
                src_ = run_rows[i, k_ * TPB:(k_ + 1) * TPB, :]
                ev[("runs", (L, k_))] = SP.dma(l_runs[s], runs[s][0:TPB * nh, i, :], bc(src_, 1, nh) if nh > 1 else src_)

        def same_matrix(L, k_, key_col):
            s = k_ % 2
            for hf in range(2):
                PE.wait(got("keys", (L, k_)), ev.get("bank2_free"))
                kk = PE.do(lambda e, hf=hf: e.matmul(bank[2][:, :], hilo_w[:, :], hl[s][:, hf * 512:(hf + 1) * 512], start=True, stop=True))
                VE.wait(kk, got("pe_y", (L, k_ - 2)))
                cols_ = key_col[:, k_ * TPB + 4 * hf:k_ * TPB + 4 * hf + 4]
                ev["bank2_free"] = VE.do(lambda e, hf=hf, cols_=cols_: e.tensor_tensor(
                    same[s][:, 4 * hf:4 * hf + 4, :], bank[2][:, :].rearrange("p (t f) -> p t f", t=4), bc(cols_, 2, P), ALU.is_equal))
            ev[("keys_read", (L, k_))] = kk
            ev[("same", (L, k_))] = ev["bank2_free"]

        def logits_to_rows(L, k_, nh, logits):
            PE.wait(ev[("logits", (L, k_))], ev.get("bank6_free"))
            ev[("rows", (L, k_))] = PE.do(lambda e: e.transpose(bank[6][0:TPB * nh, 0:P], logits, ident[:, :]))

        def run_scans(L, k_, nh):
            s, R = k_ % 2, TPB * nh
            tl = tlog[s]
            VE.wait(ev[("rows", (L, k_))], got("runs", (L, k_)), got("max_cols", (L, k_ - 2)))
            VE.do(lambda e: e.tensor_tensor_scan(tl[0:R, 0, :], runs[s][0:R, 0, :], bank[6][0:R, 0:P], -BIG, ALU.add, ALU.max))
            k2 = ev[("scan", (L, k_))] = VE.do(lambda e: e.tensor_tensor_scan(
                tl[0:R, 1, ::-1], runs[s][0:R, 1, ::-1], bank[6][0:R, 0:P][:, ::-1], -BIG, ALU.add, ALU.max))
            VE.wait(k2)
            k2 = VE.do(lambda e: e.tensor_tensor(tl[0:R, 2, :], tl[0:R, 0, :], tl[0:R, 1, :], ALU.max))
            PE.wait(k2)
            ev[("max_cols", (L, k_))] = PE.do(lambda e: e.transpose(bank[6][:, 128:128 + R], tl[0:R, 2, :], ident[0:R, 0:R]))

        def less_max(L, k_, nh, logits):
            s, R = k_ % 2, TPB * nh
            VE.wait(ev[("max_cols", (L, k_))], got("exp", (L, k_ - 2)))
            ev[("less", (L, k_))] = VE.do(lambda e: e.tensor_tensor(small[s][:, 7, 0:R], logits, bank[6][:, 128:128 + R], ALU.subtract))

        def exponentials(L, k_, nh):
            s, R = k_ % 2, TPB * nh
            AC.wait(ev[("less", (L, k_))], got("ydma", (L, k_ - 2)))
            ev["bank6_free"] = AC.do(lambda e: e.activation(ybuf[s][:, :, D + nh:D + 2 * nh], bank[6][:, 128:128 + R].rearrange("p (t h) -> p t h", t=TPB), ACT.Copy))
            AC.wait(got("pe_y", (L, k_ - 2)))
            ev[("exp", (L, k_))] = AC.do(lambda e: e.activation(msg[s][:, :, D:D + nh], small[s][:, 7, 0:R].rearrange("p (t h) -> p t h", t=TPB), ACT.Exp))

        def sum_runs(L, k_, w, msg_ready, consume=None):
            s = k_ % 2
            for pair in range(TPB // 2):
                bk = (5, 7)[pair % 2]
                PE.wait(*msg_ready, ev[("same", (L, k_))], ev.get(f"bank{bk}_free"))
                for j in range(2):
                    t = 2 * pair + j
                    fn = lambda e, t=t, bk=bk, j=j: e.matmul(bank[bk][:, j * w:(j + 1) * w], same[s][:, t, :], msg[s][:, t, 0:w], start=True, stop=True)
                    if j:
                        kk = PE.do(fn)
                    else:
                        PE.quiet(fn)
                AC.wait(kk, *got_all("ydma", (L, k_ - 2)))
                ka = AC.do(lambda e, pair=pair, bk=bk: e.activation(
                    ybuf[s][:, 2 * pair:2 * pair + 2, 0:w], bank[bk][:, 0:2 * w].rearrange("p (t f) -> p t f", t=2), ACT.Copy))
                ev[f"bank{bk}_free"] = ka
            ev[("pe_y", (L, k_))] = kk
            if consume is not None:
                ev[("ydma", (L, k_))] = consume(ka)
                return
            SP.wait(ka)
            ev[("ydma", (L, k_))] = SP.dma(l_y[s], y_rows[L][k_ * TPB * P:(k_ + 1) * TPB * P, :].rearrange("(t p) w -> p t w", p=P),
                                            ybuf[s][:, :, 0:W_Y[L]])

        def got_all(name, k_):
            e_ = ev.get((name, k_))
            return () if e_ is None else tuple(e_) if isinstance(e_, list) else (e_,)

        def gather_block(name, L, k_, lanes, ring, w, table, ix, *free):
            r = k_ % len(ring)
            PL.wait(*free)
            for t in range(TPB):
                c_ = k_ * TPB + t
                kk = PL.gather(lanes[r], ring[r][:, t, 0:w], table, ix[:, c_:c_ + 1])
            ev[(name, (L, k_))] = kk

        def v3(ap):
            return ap.rearrange("p (t h) -> p t h", t=TPB)

        hid_one = [VE.do(lambda e, s=s: e.memset(hid[s][HID:HID + 1, :], 1.0)) for s in range(2)]
        ea_view = a["edge_attr_32"]
        ea_pad = [VE.do(lambda e, s=s: e.memset(ea[s][:, :, :], 0.0)) for s in range(2)]
        PL.wait(*tables0, *cols_ready)
        SP.wait(lists_out, hid_one[1], ea_pad[1])
        AC.wait(hid_one[1])

        def l0_loads(k_):
            s = k_ % 2
            SP.wait(got("hid_in", k_ - 2), got("ea_read", k_ - 2))
            SP.dma(l_rows[s], rows4[s][0:4, :], dec_rows[:, k_ * TPB * P:(k_ + 1) * TPB * P])
            t0 = k_ * TPB
            if k_ < NBLK - 1:
                kk = SP.dma(l_rows[s], ea[s][:, :, :], ea_view[t0 * P:(t0 + TPB) * P, :].rearrange("(t p) c -> p t c", p=P))
            else:
                nf = FULL - t0
                SP.dma(l_rows[s], ea[s][:, 0:nf, :], ea_view[t0 * P:FULL * P, :].rearrange("(t p) c -> p t c", p=P))
                kk = SP.dma(l_rows[s], ea[s][0:TAIL, nf, :], ea_view[FULL * P:E, :])
            ev[("in", k_)] = kk

        def l0_time_cols(k_):
            s = k_ % 2
            PE.wait(ev[("in", k_)], ev.get("bank4_free"))
            for hf in range(2):
                kk = PE.do(lambda e, hf=hf: e.transpose(bank[4][:, hf * P:(hf + 1) * P], ea[s][:, 4 * hf:4 * hf + 4, :].rearrange("p t c -> p (t c)"), ident[:, :]))
            ev[("ea_read", k_)] = kk
            AC.wait(kk, got("time_part", k_ - 2))
            ev[("eat", k_)] = AC.do(lambda e: e.activation(eat[s][:, :, :], bank[4][:, 0:2 * P].rearrange("p (h f) -> p h f", h=2), ACT.Copy))

        def l0_hidden(k_):
            s = k_ % 2
            for hf in range(2):
                PE.wait(ev.get("bank3_free"))
                kk = PE.do(lambda e, hf=hf: e.matmul(bank[3][0:HID, :], Wd1a[:, :], rows4[s][0:4, hf * 512:(hf + 1) * 512], start=True, stop=True))
                AC.wait(kk, got("decay_mm", k_ - 2))
                ev["bank3_free"] = AC.do(lambda e, hf=hf: e.activation(hid[s][0:HID, hf * 512:(hf + 1) * 512], bank[3][0:HID, :], ACT.Relu))
            ev[("hid_in", k_)] = kk

        def l0_time_part(k_):
            s = k_ % 2
            PE.wait(ev[("eat", k_)])
            for hf in range(2):
                PE.wait(ev.get(f"bank{hf}_free"))
                ev[("time", (k_, hf))] = ev[("time_part", k_)] = PE.do(
                    lambda e, hf=hf: e.matmul(bank[hf][:, :], eat[s][:, hf, :], Wt4[:, :], start=True, stop=True))

        def l0_decay(k_):
            s = k_ % 2
            dec = small[s][:, 2, :]
            PE.wait(ev["bank3_free"], ev[("eat", k_)])
            for t in range(TPB):
                fn = lambda e, t=t: e.matmul(bank[4][:, 256 + t * H:256 + (t + 1) * H], hid[s][:, t * P:(t + 1) * P], Wd2a[:, :], start=True, stop=True)
                if t == TPB - 1:
                    kk = PE.do(fn)
                else:
                    PE.quiet(fn)
            ev[("decay_mm", k_)] = kk
            AC.wait(kk, got("logits", (0, k_ - 2)))
            kt = ev["bank4_free"] = AC.do(lambda e: e.activation(dec, bank[4][:, 256:256 + TPB * H], ACT.Tanh))
            VE.wait(kt)
            kd = VE.do(lambda e: e.tensor_tensor(v3(dec), v3(dec), bc(hrow[:, 0, :], 1, TPB), ALU.mult))
            AC.wait(kd)
            ev[("decay", k_)] = AC.do(lambda e: e.activation(dec, dec, ACT.Exp))

        def l0_distance(k_):
            s, r, rd = k_ % 2, k_ % RING, k_ % RING_D
            d2 = small[s][:, 1, 0:TPB]
            VE.wait(ev[("gs", (0, k_))], ev[("gd", (0, k_))])
            kdf = VE.do(lambda e: e.tensor_tensor(GS[r][:, :, 2 * D:3 * D], GS[r][:, :, 2 * D:3 * D], GD[rd][:, :, D:2 * D], ALU.subtract))
            AC.wait(kdf, got("logits", (0, k_ - 2)))
            for t in range(TPB):
                ksq = AC.do(lambda e, t=t: e.activation(GS[r][:, t, 2 * D:3 * D], GS[r][:, t, 2 * D:3 * D], ACT.Square, accum_out=d2[:, t:t + 1]))
            AC.wait(ksq)
            ev[("dist", k_)] = AC.do(lambda e: e.activation(d2, d2, ACT.Sqrt))

        def l0_scores(k_):
            s, r, rd = k_ % 2, k_ % RING, k_ % RING_D
            eu = small[s][:, 0, :]
            for hf in range(2):
                VE.wait(ev[("time", (k_, hf))])
                g_ = GS[r][:, 4 * hf:4 * hf + 4, 0:D]
                ev[f"bank{hf}_free"] = k2 = VE.do(lambda e, g_=g_, hf=hf: e.tensor_tensor(g_, g_, bank[hf][:, :].rearrange("p (t f) -> p t f", t=4), ALU.add))
            VE.wait(k2)
            ev[("gd_used", (0, k_))] = VE.chain(lambda e: e.tensor_tensor(GS[r][:, :, 0:D], GS[r][:, :, 0:D], GD[rd][:, :, 0:D], ALU.mult))
            ev[("scores", k_)] = VE.do(lambda e: e.tensor_reduce(v3(eu), GS[r][:, :, 0:D].rearrange("p t (h w) -> p t h w", h=H), AX, ALU.add))

        def l0_logits(k_):
            s = k_ % 2
            eu, d2, dec, lg, t1 = small[s][:, 0, :], small[s][:, 1, 0:TPB], small[s][:, 2, :], small[s][:, 3, :], small[s][:, 4, :]
            VE.wait(ev[("dist", k_)], ev[("scores", k_)])
            VE.do(lambda e: e.tensor_tensor(v3(t1), bc(d2, 2, H), bc(hrow[:, 2, :], 1, TPB), ALU.mult))
            VE.chain(lambda e: e.tensor_tensor(v3(eu), v3(eu), bc(hrow[:, 1, :], 1, TPB), ALU.mult))
            VE.chain(lambda e: e.tensor_tensor(eu, eu, t1, ALU.subtract))
            VE.wait(ev[("decay", k_)])
            ev[("logits", (0, k_))] = VE.do(lambda e: e.tensor_tensor(lg, eu, dec, ALU.mult))

        def l0_messages(k_):
            s, r = k_ % 2, k_ % RING
            VE.wait(ev[("exp", (0, k_))])
            km = ev[("gs_used", (0, k_))] = VE.do(lambda e: e.tensor_tensor(
                msg[s][:, :, 0:D].rearrange("p t (h w) -> p t h w", h=H), GS[r][:, :, D:2 * D].rearrange("p t (h w) -> p t h w", h=H),
                bc(msg[s][:, :, D:D + H], 3, DH), ALU.mult))
            sum_runs(0, k_, D + H, (km,))

        def lg0(k_):
            return small[k_ % 2][:, 3, :]

        for n in range(NBLK + 3):
            i0, i1, i2, i3 = n, n - 1, n - 2, n - 3
            b0, b1, b2, b3 = n < NBLK, 0 <= n - 1 < NBLK, 0 <= n - 2 < NBLK, 0 <= n - 3
            if b0:
                gather_block("gd", 0, i0, l_gd, GD, 2 * D, dst0, dst_tix, got("gd_used", (0, i0 - RING_D)))
                gather_block("gs", 0, i0, l_gs, GS, 3 * D, src0, src_tix, got("gs_used", (0, i0 - RING)), got("dist", i0 - RING))
            for j in (0, 1) if n == 0 else (n + 1,):
                if j < NBLK:
                    l0_loads(j)
            if b1:
                load_runs(0, i1, H)
            if b2:
                load_keys(0, i2, dst_hl)
                logits_to_rows(0, i2, H, lg0(i2))
            if b0:
                l0_time_cols(i0)
            if b1:
                l0_distance(i1)
            if b2:
                run_scans(0, i2, H)
            if b0:
                l0_hidden(i0)
            if b1:
                l0_scores(i1)
            if b2:
                less_max(0, i2, H, lg0(i2))
                exponentials(0, i2, H)
            if b3:
                same_matrix(0, i3, dst_col)
            if b0:
                l0_time_part(i0)
            if b3:
                l0_messages(i3)
            if b1:
                l0_logits(i1)
            if b0:
                l0_decay(i0)

        def node_positions():
            SP.dma(l_tab, first_row[:, :], row_bc(first_last[0, 0:TT]))
            rows_in = SP.dma(l_tab, last_row[:, :], row_bc(first_last[1, 0:TT]))
            VE.wait(rows_in)
            VE.do(lambda e: e.memset(chain_row[:, 0:2], 0.0))
            VE.chain(lambda e: e.tensor_tensor(chain_row[:, 2:TT], first_row[:, 1:TT - 1], last_row[:, 1:TT - 1], ALU.is_equal))
            k_ = VE.do(lambda e: e.tensor_tensor(first_row[:, 1:TT], first_row[:, 1:TT], last_row[:, 0:TT - 1], ALU.is_equal))
            VE.wait(k_)
            VE.chain(lambda e: e.tensor_tensor(chain_row[:, 2:TT], chain_row[:, 2:TT], first_row[:, 1:TT - 1], ALU.mult))
            te, cnt, end, start, lastp, tl = (npos[:, i, :] for i in range(6))
            for b in range(NB):
                VE.chain(lambda e, b=b: e.tensor_scalar(first_row[:, :], last_row[:, :], node_id[:, b:b + 1], None, ALU.is_le))
                VE.chain(lambda e, b=b: e.tensor_reduce(te[:, b:b + 1], first_row[:, :], AX, ALU.add))
            k_ = VE.do(lambda e: e.tensor_copy(end_ix[:, :], te))
            PL.wait(k_)
            for b in range(NB):
                k_ = PL.gather(l_nodeg, S1[:, b, :], dst_keys, end_ix[:, b:b + 1])
            VE.wait(k_)
            VE.chain(lambda e: e.tensor_tensor(S1, S1, bc(node_id[:, :], 2, P), ALU.is_le))
            VE.chain(lambda e: e.tensor_reduce(cnt, S1, AX, ALU.add))
            k_ = VE.chain(lambda e: e.scalar_tensor_tensor(out=end, in0=te, scalar=float(P), in1=cnt, op0=ALU.mult, op1=ALU.add))
            VE.chain(lambda e: e.memset(start, 0.0))
            SP.wait((VE.sem, VE.n))
            k_ = SP.dma(l_tab, end_pos[1:NB * P + 1].rearrange("(b p) -> p b", p=P), end, allow_slow_non_contiguous=True)
            SP.wait(k_)
            k_ = SP.dma(l_tab, start[1:P, :], end_pos[1:NB * P + 1].rearrange("(b p) -> p b", p=P)[0:P - 1, :], allow_slow_non_contiguous=True)
            k_ = SP.dma(l_tab, start[0:1, 1:NB], end_pos[1:NB * P + 1].rearrange("(b p) -> p b", p=P)[P - 1:P, 0:NB - 1], allow_slow_non_contiguous=True)
            VE.wait(k_)
            VE.chain(lambda e: e.tensor_tensor(degree, end, start, ALU.subtract))
            VE.chain(lambda e: e.tensor_scalar(valid, degree, 0.0, None, ALU.is_gt))
            VE.chain(lambda e: e.tensor_scalar(lastp, end, -1.0, 0.0, ALU.add, ALU.max))
            VE.chain(lambda e: e.tensor_copy(end_ix[:, :], lastp))
            VE.chain(lambda e: e.tensor_scalar(tile_ix[:, :], end_ix[:, :], 7, None, ALU.arith_shift_right))
            VE.chain(lambda e: e.tensor_copy(te, tile_ix[:, :]))
            VE.chain(lambda e: e.scalar_tensor_tensor(out=has_carry, in0=te, scalar=float(P), in1=start, op0=ALU.mult, op1=ALU.is_gt))
            return VE.chain(lambda e: e.tensor_tensor(has_carry, has_carry, valid, ALU.mult))

        VE.wait((l_y[0].sem, l_y[0].n), (l_y[1].sem, l_y[1].n))
        SP.wait((VE.sem, VE.n))
        pos_ready = node_positions()

        def join_runs(L, nh):
            wy = W_Y[L]
            YE = YE_flat[:, 0:NB * wy].rearrange("p (b w) -> p b w", b=NB)
            CE = CE_flat[:, 0:NB * wy].rearrange("p (b w) -> p b w", b=NB)
            LR = arena_b[:, 0:TC * wy].rearrange("p (c w) -> p c w", c=TC)
            work = arena_b[:, TC * WMAX:TC * WMAX + 5 * TT].rearrange("p (k t) -> p k t", k=5)
            y_out = ((l_y[0].sem, l_y[0].n), (l_y[1].sem, l_y[1].n))
            PL.wait(*y_out, pos_ready, (VE.sem, VE.n))
            for b in range(NB):
                ye_ready = PL.gather(l_nodeg, YE[:, b, :], y_rows[L], end_ix[:, b:b + 1])
            lasts = y_rows[L].rearrange("(t e) w -> t e w", e=P)[:, P - 1, :]
            SP.wait(*y_out, (VE.sem, VE.n))
            SP.dma(l_tab, LR[:, 0:TC - 1, :], lasts[0:(TC - 1) * P, :].rearrange("(c p) w -> p c w", p=P))
            rest = TT - (TC - 1) * P
            k_ = SP.dma(l_tab, LR[0:rest, TC - 1, :], lasts[(TC - 1) * P:TT, :])
            PE.wait(k_, (VE.sem, VE.n), (AC.sem, AC.n))
            parts = [(0, D, P)] + ([(D, D + nh, nh), (D + nh, D + 2 * nh, nh)] if nh else [])
            rows = [work[:, i, :] for i in range(5)]
            for i, (lo, hi, m_) in enumerate(parts):
                for g in range(2):
                    bk = 2 * (i % 2) + g
                    cs = range(4 * g, min(4 * g + 4, TC))
                    PE.wait((VE.sem, VE.n), (AC.sem, AC.n))
                    for q in cs:
                        np_ = P if q < TC - 1 else rest
                        k_ = PE.do(lambda e, bk=bk, q=q, np_=np_, lo=lo, hi=hi, m_=m_: e.transpose(
                            bank[bk][0:m_, (q % 4) * P:(q % 4) * P + np_], LR[0:np_, q, lo:hi], ident[0:np_, 0:np_]))
                    w_ = min(TT - 4 * g * P, 4 * P)
                    VE.wait(k_)
                    VE.do(lambda e, bk=bk, g=g, w_=w_, i=i, m_=m_: e.tensor_copy(rows[i][0:m_, 4 * g * P:4 * g * P + w_], bank[bk][0:m_, 0:w_]))
            VE.wait((VE.sem, VE.n))
            num, den, mx, gg, ff = rows
            S_num, S_den, S_mx = first_row, last_row, gg
            VE.chain(lambda e: e.memset(S_num[:, 0:1], 0.0))
            if nh:
                cr = chain_row[0:nh, 1:TT]
                sm_, ex_g, ex_f, sd_ = rows4[0][:, 0:TT], rows4[1][:, 0:TT], hid[0][:, 0:TT], hid[1][:, 0:TT]
                VE.chain(lambda e: e.memset(sm_[0:nh, 0:1], -BIG))
                VE.chain(lambda e: e.memset(sd_[0:nh, 0:1], 0.0))
                VE.chain(lambda e: e.tensor_scalar(ex_g[0:nh, 1:TT], cr, BIG, -BIG, ALU.mult, ALU.add))
                VE.chain(lambda e: e.tensor_tensor_scan(sm_[0:nh, 1:TT], ex_g[0:nh, 1:TT], mx[0:nh, 0:TT - 1], -BIG, ALU.add, ALU.max))
                VE.chain(lambda e: e.tensor_tensor(ex_g[0:nh, 1:TT], sm_[0:nh, 0:TT - 1], sm_[0:nh, 1:TT], ALU.subtract))
                k_ = VE.chain(lambda e: e.tensor_tensor(ex_f[0:nh, 1:TT], mx[0:nh, 0:TT - 1], sm_[0:nh, 1:TT], ALU.subtract))
                AC.wait(k_)
                AC.do(lambda e: e.activation(ex_g[0:nh, 1:TT], ex_g[0:nh, 1:TT], ACT.Exp))
                k_ = AC.do(lambda e: e.activation(ex_f[0:nh, 1:TT], ex_f[0:nh, 1:TT], ACT.Exp))
                VE.wait(k_)
                VE.chain(lambda e: e.tensor_tensor(ex_g[0:nh, 1:TT], ex_g[0:nh, 1:TT], cr, ALU.mult))
                VE.chain(lambda e: e.tensor_tensor(den[0:nh, 0:TT - 1], den[0:nh, 0:TT - 1], ex_f[0:nh, 1:TT], ALU.mult))
                k_ = VE.chain(lambda e: e.tensor_tensor_scan(sd_[0:nh, 1:TT], ex_g[0:nh, 1:TT], den[0:nh, 0:TT - 1], 0.0, ALU.mult, ALU.add))
                PE.wait(k_)
                rp = rep8[:, :] if nh == H else ones[0:1, :]
                HALF = TT // 2
                for i, src_ in enumerate((ex_g, ex_f)):
                    for g in range(2):
                        lo_ = max(1, g * HALF)
                        k_ = PE.do(lambda e, i=i, g=g, src_=src_, lo_=lo_: e.matmul(
                            bank[2 * i + g][:, lo_ - g * HALF:HALF], rp, src_[0:nh, lo_:(g + 1) * HALF], start=True, stop=True))
                VE.wait(k_)
                for g in range(2):
                    lo_ = max(1, g * HALF)
                    VE.do(lambda e, g=g, lo_=lo_: e.tensor_copy(gg[:, lo_:(g + 1) * HALF], bank[g][:, lo_ - g * HALF:HALF]))
                    VE.do(lambda e, g=g, lo_=lo_: e.tensor_tensor(ff[:, lo_:(g + 1) * HALF], num[:, lo_ - 1:(g + 1) * HALF - 1], bank[2 + g][:, lo_ - g * HALF:HALF], ALU.mult))
                VE.wait((VE.sem, VE.n))
                k_ = VE.chain(lambda e: e.tensor_tensor_scan(S_num[:, 1:TT], gg[:, 1:TT], ff[:, 1:TT], 0.0, ALU.mult, ALU.add))
                outs_ = [(S_num, 0, D, P), (sd_, D, D + nh, nh), (sm_, D + nh, D + 2 * nh, nh)]
            else:
                k_ = VE.chain(lambda e: e.tensor_tensor_scan(S_num[:, 1:TT], chain_row[:, 1:TT], num[:, 0:TT - 1], 0.0, ALU.mult, ALU.add))
                outs_ = [(S_num, 0, D, P)]
            PE.wait(k_)
            for src_, lo, hi, m_ in outs_:
                for g in range(2):
                    PE.wait((VE.sem, VE.n))
                    cs = range(4 * g, min(4 * g + 4, TC))
                    for q in cs:
                        np_ = P if q < TC - 1 else rest
                        k_ = PE.do(lambda e, g=g, q=q, np_=np_, m_=m_, src_=src_: e.transpose(
                            bank[g][0:np_, (q % 4) * m_:(q % 4 + 1) * m_], src_[0:m_, q * P:q * P + np_], ident[0:m_, 0:m_]))
                    VE.wait(k_)
                    nf = len([q for q in cs if q < TC - 1])
                    VE.do(lambda e, g=g, nf=nf, m_=m_, lo=lo, hi=hi: e.tensor_copy(
                        LR[:, 4 * g:4 * g + nf, lo:hi], bank[g][:, 0:nf * m_].rearrange("p (c w) -> p c w", c=nf)))
                    if g:
                        VE.do(lambda e, g=g, nf=nf, m_=m_, lo=lo, hi=hi: e.tensor_copy(
                            LR[0:rest, TC - 1, lo:hi], bank[g][0:rest, nf * m_:(nf + 1) * m_]))
            SP.wait((VE.sem, VE.n))
            SP.dma(l_tab, c_rows[L][0:(TC - 1) * P, :].rearrange("(c p) w -> p c w", p=P), LR[:, 0:TC - 1, :])
            k_ = SP.dma(l_tab, c_rows[L][(TC - 1) * P:TT, :], LR[0:rest, TC - 1, :])
            PL.wait(k_)
            for b in range(NB):
                ce_ready = PL.gather(l_nodeg, CE[:, b, :], c_rows[L], tile_ix[:, b:b + 1])
            VE.wait(ce_ready, ye_ready)
            return YE, CE

        def softmax_rows(L, nh):
            YE, CE = join_runs(L, nh)
            w_h = D // nh
            fE, fC, M, dn = (nodeh[:, i, :].rearrange("p (b h) -> p b h", b=NB)[:, :, 0:nh] for i in range(4))
            mE, mC = YE[:, :, D + nh:D + 2 * nh], CE[:, :, D + nh:D + 2 * nh]
            hc = bc(has_carry, 2, nh)
            VE.chain(lambda e: e.tensor_tensor(mC, mC, hc, ALU.mult))
            VE.chain(lambda e: e.tensor_scalar(stat[:, 0, :], has_carry, BIG, -BIG, ALU.mult, ALU.add))
            VE.chain(lambda e: e.tensor_tensor(mC, mC, bc(stat[:, 0, :], 2, nh), ALU.add))
            VE.chain(lambda e: e.tensor_tensor(M, mE, mC, ALU.max))
            VE.chain(lambda e: e.tensor_tensor(fE, mE, M, ALU.subtract))
            k_ = VE.chain(lambda e: e.tensor_tensor(fC, mC, M, ALU.subtract))
            AC.wait(k_)
            AC.do(lambda e: e.activation(fE, fE, ACT.Exp))
            k_ = AC.do(lambda e: e.activation(fC, fC, ACT.Exp))
            VE.wait(k_)
            VE.chain(lambda e: e.tensor_tensor(dn, fE, YE[:, :, D:D + nh], ALU.mult))
            VE.chain(lambda e: e.tensor_tensor(M, fC, CE[:, :, D:D + nh], ALU.mult))
            VE.chain(lambda e: e.tensor_tensor(dn, dn, M, ALU.add))
            VE.chain(lambda e: e.tensor_scalar(dn, dn, 1e-30, None, ALU.max))
            VE.chain(lambda e: e.reciprocal(dn, dn))
            VE.chain(lambda e: e.tensor_tensor(dn, dn, bc(valid, 2, nh), ALU.mult))
            VE.chain(lambda e: e.tensor_tensor(fE, fE, dn, ALU.mult))
            VE.chain(lambda e: e.tensor_tensor(fC, fC, dn, ALU.mult))
            for b in range(NB):
                o_ = S1[:, b, :].rearrange("p (h w) -> p h w", h=nh)
                VE.do(lambda e, b=b, o_=o_: e.tensor_tensor(o_, YE[:, b, 0:D].rearrange("p (h w) -> p h w", h=nh), bc(fE[:, b, :], 2, w_h), ALU.mult))
                c_ = CE[:, b, 0:D].rearrange("p (h w) -> p h w", h=nh)
                VE.do(lambda e, b=b, c_=c_: e.tensor_tensor(c_, c_, bc(fC[:, b, :], 2, w_h), ALU.mult))
            VE.wait((VE.sem, VE.n))
            return VE.chain(lambda e: e.tensor_tensor(S1, S1, CE[:, :, 0:D], ALU.add))

        nodeh = same[0][:, :, :].rearrange("p t f -> p (t f)")[:, 0:4 * NB * H].rearrange("p (k n) -> p k n", k=4)

        def project(dstT, weight, ready, consume):
            PE.wait(*ready)
            for g in range(-(-NB // 4)):
                bs = list(range(4 * g, min(4 * g + 4, NB)))
                bk = g % 2
                PE.wait(ev.get(("proj", bk)))
                for b in bs:
                    k_ = PE.do(lambda e, b=b, bk=bk: e.matmul(bank[bk][:, (b % 4) * P:(b % 4 + 1) * P], dstT[:, b * P:(b + 1) * P], weight, start=True, stop=True))
                VE.wait(k_)
                AC.wait(k_)
                ev[("proj", bk)] = consume(bs, bank[bk][:, 0:len(bs) * P].rearrange("p (b f) -> p b f", b=len(bs)))

        def affine(v, g_row, b_row):
            VE.chain(lambda e: e.tensor_tensor(v, v, bc(g_row, 1, NB), ALU.mult))
            return VE.chain(lambda e: e.tensor_tensor(v, v, bc(b_row, 1, NB), ALU.add))

        agg = softmax_rows(0, H)
        aggT = transpose_nodes(S1, HT, (agg,))
        VE.wait(frow_ready, weights_rest)
        PE.wait(weights_rest)
        AC.wait(weights_rest)

        def add_out(bs, ps):
            o_ = S1[:, bs[0]:bs[-1] + 1, :]
            VE.do(lambda e: e.tensor_tensor(o_, ps, bc(frow[:, 0, :], 1, len(bs)), ALU.add))
            return (VE.sem, VE.n)

        project(HT, wsq[:, 0, :], aggT, add_out)
        VE.wait((VE.sem, VE.n))
        k = VE.chain(lambda e: e.tensor_tensor(Hn[:, :, :], Hn[:, :, :], S1, ALU.add))
        norm_rows(Hn[:, :, :], Hn[:, :, :], (k,), S2)
        y1 = affine(Hn[:, :, :], frow[:, 1, :], frow[:, 2, :])
        y1T = transpose_nodes(Hn, HT, (y1,))
        PE.wait(*y1T, frow_ready)
        AC.wait(frow_ready, y1)
        hidT = [arena_a[:, s * 2048:(s + 1) * 2048].rearrange("p (c n) -> p c n", c=4) for s in range(2)]
        for g in range(-(-NB // 4)):
            bs = list(range(4 * g, min(4 * g + 4, NB)))
            w_ = len(bs) * P
            s = g % 2
            for c_ in range(4):
                bk = 4 + c_ % 2
                PE.wait(ev.get(("ff", bk)))
                k_ = PE.do(lambda e, c_=c_, bk=bk, g=g, w_=w_: e.matmul(bank[bk][:, 0:w_], Wf1[:, c_ * P:(c_ + 1) * P], HT[:, 4 * g * P:4 * g * P + w_], start=True, stop=True))
                AC.wait(k_, ev.get(("ff2", g - 2)))
                ev[("ff", bk)] = AC.do(lambda e, c_=c_, bk=bk, w_=w_, s=s: e.activation(hidT[s][:, c_, 0:w_], bank[bk][:, 0:w_], ACT.Gelu, bias=bf1[:, c_:c_ + 1]))
            PE.wait(ev[("ff", bk)], ev.get(("proj", s)))
            for j, b in enumerate(bs):
                for c_ in range(4):
                    k_ = PE.do(lambda e, c_=c_, j=j, s=s: e.matmul(bank[s][:, j * P:(j + 1) * P], hidT[s][:, c_, j * P:(j + 1) * P], Wf2[:, c_, :], start=(c_ == 0), stop=(c_ == 3)))
            ev[("ff2", g)] = k_
            VE.wait(k_)
            ev[("proj", s)] = VE.do(lambda e, bs=bs, s=s, w_=w_: e.tensor_tensor(
                S1[:, bs[0]:bs[-1] + 1, :], bank[s][:, 0:w_].rearrange("p (b f) -> p b f", b=len(bs)), bc(frow[:, 3, :], 1, len(bs)), ALU.add))
        VE.wait(ev[("proj", s)])
        k = VE.chain(lambda e: e.tensor_tensor(Hn[:, :, :], Hn[:, :, :], S1, ALU.add))
        norm_rows(Hn[:, :, :], Hn[:, :, :], (k,), S2)
        affine(Hn[:, :, :], frow[:, 4, :], frow[:, 5, :])
        x1 = VE.chain(lambda e: e.tensor_tensor(X[:, :, :], X[:, :, :], Hn[:, :, :], ALU.add))

        frow_ready = load_frow(1, (x1,))
        h_ready = relu_norm((x1,))
        hT = transpose_nodes(Hn, HT, (h_ready,))
        w1T = transpose_weight(wsq[:, 1, :], wsq[:, 1, :], (frow_ready,))

        def tanh_out(bs, ps):
            return AC.do(lambda e: e.activation(S1[:, bs[0]:bs[-1] + 1, :], ps, ACT.Tanh))

        AC.wait(x1)
        project(HT, wsq[:, 1, :], hT, tanh_out)
        VE.wait((AC.sem, AC.n), frow_ready)
        TB = arena_a[:, 0:NB * (D + 1)].rearrange("p (b w) -> p b w", b=NB)
        VE.chain(lambda e: e.tensor_tensor(S1, S1, bc(frow[:, 0, :], 1, NB), ALU.mult))
        VE.chain(lambda e: e.tensor_reduce(stat[:, 0, :], S1, AX, ALU.add))
        VE.do(lambda e: e.tensor_copy(TB[:, :, D], stat[:, 0, :]))
        k = VE.do(lambda e: e.tensor_copy(TB[:, :, 0:D], Hn[:, :, :]))
        SP.wait(k)
        tables1 = store_nodes(tab1, TB, l_node)

        def lg1(k_):
            return small[k_ % 2][:, 3, 0:TPB]

        def l1_logits(k_):
            VE.wait(ev[("gs", (1, k_))], got("less", (1, k_ - 2)), got("rows", (1, k_ - 2)))
            ev[("logits", (1, k_))] = VE.do(lambda e: e.tensor_copy(lg1(k_), GS[k_ % RING][:, :, D]))

        def l1_messages(k_):
            s, r = k_ % 2, k_ % RING
            VE.wait(ev[("exp", (1, k_))])
            km = ev[("gs_used", (1, k_))] = VE.do(lambda e: e.tensor_tensor(
                msg[s][:, :, 0:D], GS[r][:, :, 0:D], msg[s][:, :, D:D + 1].broadcast_to([P, TPB, D]), ALU.mult))
            sum_runs(1, k_, D + 1, (km,))

        PL.wait(tables1)
        SP.wait((PE.sem, PE.n), (VE.sem, VE.n))
        for n in range(NBLK + 2):
            i0, i1, i2 = n, n - 1, n - 2
            b0, b1, b2 = n < NBLK, 0 <= n - 1 < NBLK, 0 <= n - 2
            if b0:
                gather_block("gs", 1, i0, l_gs, GS, D + 1, tab1, src_ix, got("gs_used", (1, i0 - RING)), got("logits", (1, i0 - RING)))
                load_runs(1, i0, 1)
            if b1:
                load_keys(1, i1, dst_hl)
                logits_to_rows(1, i1, 1, lg1(i1))
                run_scans(1, i1, 1)
            if b2:
                same_matrix(1, i2, dst_col)
            if b1:
                less_max(1, i1, 1, lg1(i1))
                exponentials(1, i1, 1)
            if b2:
                l1_messages(i2)
            if b0:
                l1_logits(i0)
        agg = softmax_rows(1, 1)
        x2 = VE.chain(lambda e: e.tensor_tensor(X[:, :, :], X[:, :, :], S1, ALU.add))

        e2 = arena_a[:, 0:TC * 2 * P].rearrange("p (c f) -> p c f", c=TC)
        e2s = arena_a[:, TC * 2 * P:2 * TC * 2 * P].rearrange("p (k c f) -> p k c f", k=2, c=TC)
        k = VE.do(lambda e: e.memset(e2[:, TC - 1, :], 0.0))
        SP.wait(k, x2)
        k = load_tiled(l_prep, e2, a["edge_attr_2"].rearrange("e k -> (e k)"), 2)
        VE.wait(k)
        VE.do(lambda e: e.tensor_copy(e2s[:, 0], e2.rearrange("p c (f k) -> p c f k", k=2)[:, :, :, 0]))
        k = VE.do(lambda e: e.tensor_copy(e2s[:, 1], e2.rearrange("p c (f k) -> p c f k", k=2)[:, :, :, 1]))
        SP.wait(k)
        for i in range(2):
            k = SP.dma(l_tab, ea2_rows[i, :].rearrange("(c p f) -> p c f", p=P, f=P), e2s[:, i])
        e2_ready = k
        frow_ready = load_frow(2, (x2,))
        h_ready = relu_norm((x2,))
        hT = transpose_nodes(Hn, HT, (h_ready,))
        VE.wait(*hT)
        VE.chain(lambda e: e.tensor_reduce(cmag[:, 0:1], HT[:, 0:N], AX, ALU.add))
        VE.chain(lambda e: e.tensor_scalar(cmag[:, 0:1], cmag[:, 0:1], 1.0 / N, None, ALU.mult))
        k = VE.chain(lambda e: e.tensor_scalar(HT[:, :], HT[:, :], cmag[:, 0:1], None, ALU.subtract))
        VE.wait(frow_ready)

        def a_out(bs, ps):
            return VE.do(lambda e: e.tensor_tensor(S1[:, bs[0]:bs[-1] + 1, :], ps, bc(frow[:, 0, :], 1, len(bs)), ALU.add))

        def b_out(bs, ps):
            return AC.do(lambda e: e.activation(S2[:, bs[0]:bs[-1] + 1, :], ps, ACT.Copy))

        project(HT, wsq[:, 3, :], (k,), a_out)
        project(HT, wsq[:, 4, :], (k,), b_out)
        SP.wait((VE.sem, VE.n), (AC.sem, AC.n))
        store_nodes(tab2a, S1, l_node)
        tables2 = store_nodes(tab2b, S2, l_node)
        Z = arena_a[:, 0:NB * (D + 1)].rearrange("p (b w) -> p b w", b=NB)
        VE.wait(e2_ready)
        k = VE.do(lambda e: e.memset(arena_a[:, 0:(NB + 1) * (D + 1)], 0.0))
        SP.wait(k)
        for i in range(NACC):
            SP.dma(l_zero, acc_rows[i][0:NB * P, :].rearrange("(b p) w -> p b w", p=P), Z)
            zeroed = SP.dma(l_zero, acc_rows[i][NB * P:N + P, :], Z[0:N + P - NB * P, 0, :])
        PL.wait(tables2, zeroed)
        def e2_load(k_, s):
            return SP.dma(l_rows[s], rows4[s][0:2, :], ea2_rows[:, k_ * TPB * P:(k_ + 1) * TPB * P])

        hb_ = [ybuf[s][:, :, 0:D] for s in range(2)]
        sums, squares = bank[6][0:1, :], bank[7][0:1, :]
        n_groups = NBLK * 2

        def l2_attr_part(i):
            s = i % 2
            PE.wait(ev[("in2", i)])
            for hf in range(2):
                PE.wait(ev.get(f"bank{hf}_free"))
                for t in range(4):
                    tt = 4 * hf + t
                    fn = lambda e, hf=hf, t=t, tt=tt: e.matmul(bank[hf][:, t * P:(t + 1) * P], rows4[s][0:2, tt * P:(tt + 1) * P], W1c[:, :], start=True, stop=True)
                    if t == 3:
                        kk = PE.do(fn)
                    else:
                        PE.quiet(fn)
                ev[("attr", (i, hf))] = kk
            ev[("t2", i)] = kk

        def l2_sum(i):
            s, r, rd = i % 2, i % RING, i % RING_D
            VE.wait(ev[("gs", (2, i))], ev[("gd", (2, i))], got("hdma", i - 2), got("st2", i - 2))
            kg = ev[("gd_used", (2, i))] = VE.do(lambda e: e.tensor_tensor(GS[r][:, :, 0:D], GS[r][:, :, 0:D], GD[rd][:, :, 0:D], ALU.add))
            VE.wait(kg)
            for hf in range(2):
                VE.wait(ev[("attr", (i, hf))])
                kh = VE.do(lambda e, hf=hf: e.tensor_tensor(
                    hb_[s][:, 4 * hf:4 * hf + 4, :], GS[r][:, 4 * hf:4 * hf + 4, 0:D], bank[hf][:, :].rearrange("p (t f) -> p t f", t=4), ALU.add))
                ev[f"bank{hf}_free"] = kh
            ev[("h_used", i)] = kh
            AC.wait(kh, got("st2", i - 2))
            ev[("square", i)] = AC.do(lambda e: e.activation(msg[s][:, :, 0:D], hb_[s], ACT.Square))
            SP.wait(kh)
            ev[("hdma", i)] = SP.dma(l_y[s], h_rows[i * TPB * P:(i + 1) * TPB * P, :].rearrange("(t p) w -> p t w", p=P), hb_[s])

        def l2_stats(i):
            s = i % 2
            PE.wait(ev[("square", i)])
            if i < NBLK - 1:
                for hf in range(2):
                    for dst_, v_ in ((sums, hb_[s]), (squares, msg[s][:, :, 0:D])):
                        kk = PE.do(lambda e, dst_=dst_, v_=v_, hf=hf: e.matmul(dst_, ones[:, 0:1], v_[:, 4 * hf:4 * hf + 4, :], start=(i == 0 and hf == 0), stop=False, skip_group_check=True))
            else:
                for t in range(TPB):
                    for dst_, v_ in ((sums, hb_[s]), (squares, msg[s][:, :, 0:D])):
                        kk = PE.do(lambda e, dst_=dst_, v_=v_, t=t: e.matmul(dst_[:, (t % 4) * P:(t % 4 + 1) * P], edge_ok[:, t:t + 1], v_[:, t, :], start=False, stop=(t >= TPB - 4), skip_group_check=True))
            ev[("st2", i)] = kk

        for n in range(NBLK + 2):
            if n < NBLK:
                gather_block("gs", 2, n, l_gs, GS, D, tab2a, src_ix, got("h_used", n - RING))
                gather_block("gd", 2, n, l_gd, GD, D, tab2b, dst_ix, got("gd_used", (2, n - RING_D)))
            for j in (0, 1) if n == 0 else (n + 1,):
                if j < NBLK:
                    SP.wait(got("t2", j - 2))
                    ev[("in2", j)] = e2_load(j, j % 2)
            if 0 <= n - 1 < NBLK:
                l2_sum(n - 1)
            if n < NBLK:
                l2_attr_part(n)
            if n >= 2:
                l2_stats(n - 2)
        kk = ev[("st2", NBLK - 1)]
        bn = relb[0:1, :, :].rearrange("p y (k f) -> p (y k) f", f=D)
        gb = Wqkv[0:1, 0:2 * D].rearrange("p (k f) -> p k f", k=2)
        gb_in = [SP.dma(l_w2, gb[:, 0, :], a["L2_gnn_gamma"].unsqueeze(0)), SP.dma(l_w2, gb[:, 1, :], a["L2_gnn_beta"].unsqueeze(0))][-1]
        VE.wait(kk, gb_in)
        mu_, ms_, va_ = bn[:, 0, :], bn[:, 1, :], bn[:, 2, :]
        VE.chain(lambda e: e.tensor_reduce(mu_, sums.rearrange("p (t f) -> p f t", t=4), AX, ALU.add))
        VE.chain(lambda e: e.tensor_reduce(ms_, squares.rearrange("p (t f) -> p f t", t=4), AX, ALU.add))
        VE.chain(lambda e: e.tensor_scalar(bn[:, 0:2, :], bn[:, 0:2, :], 1.0 / E, None, ALU.mult))
        VE.chain(lambda e: e.tensor_tensor(va_, mu_, mu_, ALU.mult))
        VE.chain(lambda e: e.tensor_tensor(va_, ms_, va_, ALU.subtract))
        VE.chain(lambda e: e.tensor_scalar(va_, va_, 0.0, EPS, ALU.max, ALU.add))
        k = VE.chain(lambda e: e.reciprocal(va_, va_))
        AC.wait(k)
        k = AC.do(lambda e: e.activation(va_, va_, ACT.Sqrt))
        VE.wait(k)
        VE.chain(lambda e: e.tensor_tensor(bn[:, 3, :], va_, gb[:, 0, :], ALU.mult))
        VE.chain(lambda e: e.tensor_tensor(bn[:, 5, :], mu_, bn[:, 3, :], ALU.mult))
        k = VE.chain(lambda e: e.tensor_tensor(bn[:, 4, :], gb[:, 1, :], bn[:, 5, :], ALU.subtract))
        PE.wait(k)
        k = PE.do(lambda e: e.matmul(bank[4][:, 0:2 * D], ones[0:1, :], bn[:, 3:5, :].rearrange("p k f -> p (k f)"), start=True, stop=True))
        bnr = Wf1[:, 0:2 * D].rearrange("p (k f) -> p k f", k=2)
        VE.wait(k)
        bn_ready = VE.chain(lambda e: e.tensor_copy(bnr[:, :, :], bank[4][:, 0:2 * D].rearrange("p (k f) -> p k f", k=2)))
        for s in range(2):
            VE.do(lambda e, s=s: e.memset(msg[s][:, :, D:D + 1], 1.0))
        VE.wait((VE.sem, VE.n))
        SP.wait((l_y[0].sem, l_y[0].n), (l_y[1].sem, l_y[1].n), ev[("h_used", NBLK - 1)])

        def l2_h_in(i):
            r = i % RING
            SP.wait(got("m2", i - RING))
            ev[("hin", i)] = SP.dma(l_hin[r], GS[r][:, :, 0:D], h_rows[i * TPB * P:(i + 1) * TPB * P, :].rearrange("(t p) w -> p t w", p=P))

        def l2_targets(i):
            s = i % 2
            tri = GD[s][:, :, 0:P]
            cnt_, tgt = small[s][:, 0, 0:TPB], small[s][:, 1, 0:TPB]
            sc_ = src_col[:, i * TPB:(i + 1) * TPB]
            VE.wait(ev[("same", (2, i))])
            VE.chain(lambda e: e.tensor_tensor(tri, same[s][:, :, :], bc(lower[:, :], 1, TPB), ALU.mult))
            VE.chain(lambda e: e.tensor_reduce(cnt_, tri, AX, ALU.add))
            VE.chain(lambda e: e.tensor_scalar(cnt_, cnt_, 0.0, None, ALU.is_equal))
            VE.do(lambda e: e.tensor_scalar(tgt, sc_, junk[:, 0:1], None, ALU.subtract))
            VE.chain(lambda e: e.scalar_tensor_tensor(out=cnt_, in0=sc_, scalar=float(N), in1=cnt_, op0=ALU.is_lt, op1=ALU.mult))
            VE.chain(lambda e: e.tensor_tensor(tgt, tgt, cnt_, ALU.mult))
            VE.wait(*got_all("ydma", (2, i - 2)))
            ev[("targets", i)] = VE.do(lambda e: e.tensor_scalar(add_ix[s][:, :], tgt, junk[:, 0:1], None, ALU.add))

        def l2_relu(i):
            s, r = i % 2, i % RING
            g_ = GS[r][:, :, 0:D]
            VE.wait(ev[("hin", i)])
            VE.chain(lambda e: e.tensor_tensor(g_, g_, bc(bnr[:, 0, :], 1, TPB), ALU.mult))
            kb = VE.do(lambda e: e.tensor_tensor(g_, g_, bc(bnr[:, 1, :], 1, TPB), ALU.add))
            AC.wait(kb, got("pe_y", (2, i - 2)))
            ev[("m2", i)] = AC.do(lambda e: e.activation(msg[s][:, :, 0:D], g_, ACT.Relu))

        def l2_add(i, ready):
            s = i % 2
            PL.wait(ev[("targets", i)], ready)
            for t in range(TPB):
                PL.wait(l_acc[t].at() if l_acc[t].n else None)
                PL.scatter_add(l_acc[t], acc_rows[t], add_ix[s][:, t:t + 1], ybuf[s][:, t, 0:D + 1])
            return [l_acc[t].at() for t in range(TPB)]

        for n in range(NBLK + 1):
            if n < NBLK:
                for j in (0, 1) if n == 0 else (n + 1,):
                    if j < NBLK:
                        load_keys(2, j, src_hl)
                for j in (0, 1, 2) if n == 0 else (n + 2,):
                    if j < NBLK:
                        l2_h_in(j)
                same_matrix(2, n, src_col)
                l2_relu(n)
            if n >= 1:
                sum_runs(2, n - 1, D + 1, (ev[("m2", n - 1)],), lambda ready, i=n - 1: l2_add(i, ready))
            if n < NBLK:
                l2_targets(n)
        ev[("acc", NBLK - 1)] = ev[("ydma", (2, NBLK - 1))]
        SP.wait((VE.sem, VE.n), (PE.sem, PE.n), (AC.sem, AC.n), *ev[("acc", NBLK - 1)])
        AB = [arena_a[:, j * NB * (D + 1):(j + 1) * NB * (D + 1)].rearrange("p (b w) -> p b w", b=NB) for j in range(2)]
        A_done = [None, None]
        for t in range(NACC):
            j = 0 if t == 0 else 1
            SP.wait(A_done[j])
            k = SP.dma(l_node, AB[j], acc_rows[t][0:NB * P, :].rearrange("(b p) w -> p b w", p=P))
            if t:
                VE.wait(k)
                A_done[1] = VE.chain(lambda e: e.tensor_tensor(AB[0], AB[0], AB[1], ALU.add))
        cnts, rc = stat[:, 2, :], stat[:, 3, :]
        VE.chain(lambda e: e.tensor_copy(cnts, AB[0][:, :, D]))
        VE.chain(lambda e: e.tensor_scalar(rc, cnts, 1.0, None, ALU.add))
        VE.chain(lambda e: e.reciprocal(rc, rc))
        k = VE.chain(lambda e: e.tensor_copy(S1, AB[0][:, :, 0:D]))
        sT = transpose_nodes(S1, HT, (k,))
        VE.do(lambda e: e.tensor_tensor(S2, bc(cnts, 2, D), bc(frow[:, 1, :], 1, NB), ALU.mult))
        VE.wait((VE.sem, VE.n))

        def w2_out(bs, ps):
            return VE.do(lambda e: e.tensor_tensor(S1[:, bs[0]:bs[-1] + 1, :], ps, S2[:, bs[0]:bs[-1] + 1, :], ALU.add))

        project(HT, wsq[:, 2, :], sT, w2_out)
        VE.wait((VE.sem, VE.n))
        VE.chain(lambda e: e.tensor_tensor(S1, S1, bc(rc, 2, D), ALU.mult))
        VE.chain(lambda e: e.tensor_tensor(S1, S1, Hn[:, :, :], ALU.add))
        x3 = VE.chain(lambda e: e.tensor_tensor(X[:, :, :], X[:, :, :], S1, ALU.add))

        frow_ready = load_frow(3, (x3,))
        h_ready = relu_norm((x3,))
        hT = transpose_nodes(Hn, HT, (h_ready,))
        transpose_weight(wtmp[:, D:D + T_DIM], We3[:, :], (frow_ready,), width=T_DIM)
        transpose_weight(emb[:, :], embT[:, :], (), parts=NT16, width=T_DIM)
        transpose_weight(wtmp[:, 0:D], wsq[:, 3, :], ())
        transpose_weight(wsq[:, 5, :], wsq[:, 4, :], ())
        k = PE.do(lambda e: e.matmul(bank[6][0:NT16, 0:D], embT[:, :], We3[:, :], start=True, stop=True))
        VE.wait(k, frow_ready)
        em_ready = VE.do(lambda e: e.tensor_tensor(Em[:, :], bank[6][0:NT16, 0:D], frow[0:NT16, 0, :], ALU.add))

        def xm_out(bs, ps):
            return VE.do(lambda e: e.tensor_copy(S1[:, bs[0]:bs[-1] + 1, :], ps))

        project(HT, wsq[:, 3, :], hT, xm_out)
        SP.wait((VE.sem, VE.n))
        tables3 = store_nodes(tab3, S1, l_node)
        L = 3
        PL.wait(tables3)
        PE.wait(em_ready)


        def l3_type_part(i):
            s = i % 2
            VE.wait(ev[("types", i)])
            k1 = VE.do(lambda e: e.tensor_scalar(rows4[s][:, :], rows4[s][:, :], iota16[:, 0:1], None, ALU.is_equal))
            PE.wait(k1)
            for hf in range(2):
                PE.wait(ev.get(f"bank{hf}_free"))
                for t in range(4):
                    tt = 4 * hf + t
                    fn = lambda e, hf=hf, t=t, tt=tt: e.matmul(bank[hf][:, t * P:(t + 1) * P], rows4[s][:, tt * P:(tt + 1) * P], Em[:, :], start=True, stop=True)
                    if t == 3:
                        kk = PE.do(fn)
                    else:
                        PE.quiet(fn)
                ev[("type", (i, hf))] = kk
            ev[("types_used", i)] = kk

        def l3_relu(i):
            s, r = i % 2, i % RING
            VE.wait(ev[("gs", (3, i))])
            for hf in range(2):
                VE.wait(ev[("type", (i, hf))])
                g_ = GS[r][:, 4 * hf:4 * hf + 4, 0:D]
                kg = VE.do(lambda e, g_=g_, hf=hf: e.tensor_tensor(g_, g_, bank[hf][:, :].rearrange("p (t f) -> p t f", t=4), ALU.add))
                ev[f"bank{hf}_free"] = kg
            AC.wait(kg, got("pe_y", (3, i - 2)))
            ev[("gs_used", (3, i))] = AC.do(lambda e: e.activation(msg[s][:, :, 0:D], GS[r][:, :, 0:D], ACT.Relu))

        for n in range(NBLK + 2):
            if n < NBLK:
                gather_block("gs", 3, n, l_gs, GS, D, tab3, src_ix, got("gs_used", (3, n - RING)))
            for j in (0, 1) if n == 0 else (n + 1,):
                if j < NBLK:
                    SP.wait(got("types_used", j - 2))
                    ev[("types", j)] = SP.dma(l_rows[j % 2], rows4[j % 2][:, :], t16_row[:, j * TPB * P:(j + 1) * TPB * P].broadcast_to([NT16, TPB * P]))
            if 0 <= n - 1 < NBLK:
                load_keys(3, n - 1, dst_hl)
                l3_relu(n - 1)
            if n < NBLK:
                l3_type_part(n)
            if n >= 2:
                same_matrix(3, n - 2, dst_col)
                sum_runs(3, n - 2, D, (ev[("gs_used", (3, n - 2))],))
        YE, CE = join_runs(3, 0)
        VE.chain(lambda e: e.tensor_tensor(CE, CE, bc(has_carry, 2, D), ALU.mult))
        VE.chain(lambda e: e.tensor_tensor(YE, YE, CE, ALU.add))
        VE.chain(lambda e: e.tensor_scalar(stat[:, 0, :], degree, 1.0, None, ALU.max))
        VE.chain(lambda e: e.reciprocal(stat[:, 0, :], stat[:, 0, :]))
        VE.chain(lambda e: e.tensor_tensor(stat[:, 0, :], stat[:, 0, :], valid, ALU.mult))
        k = VE.chain(lambda e: e.tensor_tensor(S1, YE, bc(stat[:, 0, :], 2, D), ALU.mult))
        aT = transpose_nodes(S1, HT, (k,))

        def upd_out(bs, ps):
            return VE.do(lambda e: e.tensor_tensor(S1[:, bs[0]:bs[-1] + 1, :], ps, bc(frow[:, 1, :], 1, len(bs)), ALU.add))

        project(HT, wsq[:, 4, :], aT, upd_out)
        VE.wait((VE.sem, VE.n))
        k = VE.chain(lambda e: e.tensor_tensor(Hn[:, :, :], Hn[:, :, :], S1, ALU.add))
        norm_rows(Hn[:, :, :], Hn[:, :, :], (k,), S2)
        affine(Hn[:, :, :], frow[:, 2, :], frow[:, 3, :])
        k = VE.chain(lambda e: e.tensor_tensor(X[:, :, :], X[:, :, :], Hn[:, :, :], ALU.add))
        SP.wait(k)
        done = store_nodes(out, X, l_out)
        SP.wait(done)

        block = ctx.enter_context(nc.Block())
        block.sync(SP.play)
        block.gpsimd(PL.play)
        block.scalar(AC.play)
        block.vector(VE.play)
        block.tensor(PE.play)


def kernel(**inputs):
    import concourse.bacc as bacc
    from concourse.bass_utils import run_bass_kernel_spmd

    nc = bacc.Bacc("TRN2", target_bir_lowering=False, num_devices=1)
    arrays, aps = {}, {}
    for name, value in inputs.items():
        v = np.ascontiguousarray(value).reshape(np.shape(value) or (1,))
        arrays[name] = v
        aps[name] = nc.dram_tensor(name, v.shape, mybir.dt.from_np(v.dtype), kind="ExternalInput").ap()
    out = nc.dram_tensor("out", (N, D), F32, kind="ExternalOutput").ap()
    program(nc, aps, out)
    r = run_bass_kernel_spmd(nc, [arrays], core_ids=[0])
    return r.results[0]["out"]
```

```python
from contextlib import ExitStack

import numpy as np

import concourse.bass as bass
from concourse import mybir

F32 = mybir.dt.float32
I32 = mybir.dt.int32
BF16 = mybir.dt.bfloat16
ALU = mybir.AluOpType
ACT = mybir.ActivationFunctionType
AX = mybir.AxisListType.X

P = 128
N, D = 3125, 128
E = 103125
H, DH = 8, 16
NET, T_DIM, HID = 2, 32, 64
NT16 = 16
NB = -(-N // P)
NLAST = N - (NB - 1) * P
TPB = 8
NBLK = -(-E // (P * TPB))
TT = NBLK * TPB
TC = -(-TT // P)
FULL = E // P
TAIL = E - FULL * P
PADKEY = 4095.0
BIG = float(2.0 ** 126)
EPS = 1e-5
NACC = 4
EW = TT * P
TIME_PARTS, WEIGHT_PARTS = (0, 0, 0, 1, 1, 2), (0, 1, 2, 0, 1, 0)
NDEC = len(TIME_PARTS) + 3 * NET
WIN = P - NET


class Lane:

    def __init__(self, sem):
        self.sem, self.n = sem, 0

    def at(self):
        return (self.sem, self.n)


class Stream:

    def __init__(self, sem):
        self.sem, self.n, self.steps, self.reached = sem, 0, [], {}

    def wait(self, *events):
        for ev in events:
            if ev is None or self.reached.get(id(ev[0]), 0) >= ev[1]:
                continue
            self.reached[id(ev[0])] = ev[1]
            self.steps.append(lambda e, ev=ev: e.wait_ge(ev[0], ev[1]))

    def do(self, fn):
        self.n += 1
        self.steps.append(lambda e: fn(e).then_inc(self.sem, 1))
        return (self.sem, self.n)

    def quiet(self, fn):
        self.steps.append(fn)

    def chain(self, fn):
        ev = self.do(fn)
        self.wait(ev)
        return ev

    def dma(self, lane, out, in_, **kw):
        lane.n += 16
        self.steps.append(lambda e: e.dma_start(out, in_, **kw).then_inc(lane.sem, 16))
        return (lane.sem, lane.n)

    def gather(self, lane, out, table, idx):
        lane.n += 16
        self.steps.append(lambda e: e.indirect_dma_start(
            out, None, table, bass.IndirectOffsetOnAxis(ap=idx, axis=0)).then_inc(lane.sem, 16))
        return (lane.sem, lane.n)

    def scatter_add(self, lane, table, idx, in_):
        lane.n += 16
        self.steps.append(lambda e: e.indirect_dma_start(
            table, bass.IndirectOffsetOnAxis(ap=idx, axis=0), in_, None,
            compute_op=ALU.add).then_inc(lane.sem, 16))
        return (lane.sem, lane.n)

    def play(self, eng):
        for step in self.steps:
            step(eng)


def either(streams, lanes, own_lanes, ev, flag, emit_if_set, emit_if_clear):
    before = [(st.n, dict(st.reached), st.steps) for st in streams]
    lanes_before, ev_before = [l.n for l in lanes], dict(ev)
    paths, counts, lane_counts = [], [], []
    for emit in (emit_if_set, emit_if_clear):
        for st, (n, reached, _) in zip(streams, before):
            st.n, st.reached, st.steps = n, dict(reached), []
        for l, n in zip(lanes, lanes_before):
            l.n = n if l not in own_lanes else l.n
        ev.clear()
        ev.update(ev_before)
        emit()
        paths.append([st.steps for st in streams])
        counts.append([st.n for st in streams])
        lane_counts.append([l.n for l in lanes if l not in own_lanes])
    assert lane_counts[0] == lane_counts[1]
    ev.clear()
    ev.update(ev_before)
    level = [max(c) for c in zip(*counts)]
    for i, (st, (_, reached, steps)) in enumerate(zip(streams, before)):
        for path, count in zip(paths, counts):
            if count[i] < level[i]:
                path[i].append(lambda e, st=st, d=level[i] - count[i]: e.drain().then_inc(st.sem, d))

        def branch(e, taken=paths[0][i], other=paths[1][i]):
            value = e.value_load(flag, min_val=0, max_val=1)
            with e.If(value != 0):
                for step in taken:
                    step(e)
            with e.If(value != 1):
                for step in other:
                    step(e)

        st.steps, st.n, st.reached = steps + [branch], level[i], reached
    for st in streams:
        st.wait(*((o.sem, o.n) for o in streams))


def bc(ap, axis, n):
    shape = list(ap.shape)
    return ap.unsqueeze(axis).broadcast_to(shape[:axis] + [n] + shape[axis:])


def program(nc, a, out):
    ctx = ExitStack()
    with ctx:
        def sb(name, shape, dt=F32):
            return ctx.enter_context(nc.sbuf_tensor(name, shape, dt))

        def dram(name, shape, dt=F32):
            return nc.dram_tensor(name, shape, dt).ap()

        def lane(name):
            return Lane(ctx.enter_context(nc.semaphore(name)))

        def stream(name):
            return Stream(ctx.enter_context(nc.semaphore(name)))

        SP, PL, AC, VE, PE = (stream(n) for n in ("sp_done", "pool_done", "act_done", "dve_done", "pe_done"))

        bank = [ctx.enter_context(nc.psum_tensor(f"bank{i}", [P, 512], F32)) for i in range(8)]

        src0 = dram("src_table0", [NET * N, 3 * D])
        dst0 = dram("dst_table0", [NET * N, 2 * D])
        tab1 = dram("table1", [N, D + 1])
        tab2a = dram("table2a", [N, D])
        tab2b = dram("table2b", [N + NET, D])
        dst_win = dram("dst_window_table", [N + NET, 2 * D])
        tab3 = dram("table3", [N, D])
        W_Y = (D + 2 * H, D + 2, None, D)
        y_rows = {L: dram(f"y_rows{L}", [EW, W_Y[L]]) for L in (0, 1, 3)}
        c_rows = {L: dram(f"carry_rows{L}", [TT, W_Y[L]]) for L in (0, 1, 3)}
        h_rows = dram("h_rows", [EW, D])
        acc_rows = [dram(f"acc_rows{i}", [N + P, D + 1]) for i in range(NACC)]
        dst_keys = dram("dst_keys", [TC * P, P])
        dst_hl = dram("dst_hl", [3, TC * P * P], BF16)
        src_hl = dram("src_hl", [2, TC * P * P], BF16)
        dec_rows = dram("dec_rows", [NDEC, TC * P * P], BF16)
        run_rows = dram("run_rows", [2, TC * P, P])
        t16_row = dram("t16_row", [1, TC * P * P])
        ea2_rows = dram("ea2_rows", [2, TC * P * P])
        first_last = dram("first_last", [2, TC * P])
        end_pos = dram("end_pos", [NB * P + 1])

        ident = sb("ident", [P, P])
        lower = sb("lower", [P, P])
        ones = sb("ones", [P, P])
        hilo_w = sb("hilo_w", [2, P], BF16)
        win_w = sb("win_w", [3, P], BF16)
        win_node = sb("win_node", [P, NBLK])
        win_ix = sb("win_ix", [P, NBLK], I32)
        is_node = sb("is_node", [P, 1])
        all_near = sb("all_near", [1, 2], I32)
        junk = sb("junk", [P, 1])
        node_id = sb("node_id", [P, NB])
        iota16 = sb("iota16", [NT16, 1])
        rep8 = sb("rep8", [H, D])
        edge_ok = sb("edge_ok", [P, TPB])

        X = sb("X", [P, NB, D])
        Hn = sb("Hn", [P, NB, D])
        stat = sb("stat", [P, 8, NB])

        src_col = sb("src_col", [P, TC * P])
        dst_col = sb("dst_col", [P, TC * P])
        src_ix = sb("src_ix", [P, TC * P], I32)
        dst_ix = sb("dst_ix", [P, TC * P], I32)
        src_tix = sb("src_tix", [P, TC * P], I32)
        dst_tix = sb("dst_tix", [P, TC * P], I32)

        RING = 4
        arena_a = sb("arena_a", [P, RING * TPB * 3 * D])
        arena_b = sb("arena_b", [P, 2 * NB * D])
        HT = arena_a[:, RING * TPB * 3 * D - NB * P:RING * TPB * 3 * D]
        GS = [arena_a[:, s * TPB * 3 * D:(s + 1) * TPB * 3 * D].rearrange("p (t w) -> p t w", t=TPB) for s in range(RING)]
        RING_D = 3
        RING_W = 3
        win = [arena_b[:, s * 2 * D:(s + 1) * 2 * D] for s in range(RING_W)]
        o_ = RING_W * 2 * D
        pick = [arena_b[:, o_ + s * TPB * P:o_ + (s + 1) * TPB * P].rearrange("p (t f) -> p t f", t=TPB) for s in range(2)]
        o_ += 2 * TPB * P
        w_ = o_ + TPB * P
        wd2_wide = arena_b[:, w_:w_ + (2 * TPB - 1) * H]
        wd1_2 = arena_b[0:2 * NDEC, w_ + 2 * TPB * H:w_ + 2 * TPB * H + HID].bitcast(BF16)
        bias_col = arena_b[0:TPB * H, w_ + 2 * TPB * H + HID:w_ + 2 * TPB * H + HID + 1]
        hid_2 = [arena_b[:, 2 * NB * D - (2 - s) * 512:2 * NB * D - (1 - s) * 512] for s in range(2)]
        hlt = [arena_b[0:3, o_ + s * TPB * P // 2:o_ + (s + 1) * TPB * P // 2].bitcast(BF16) for s in range(2)]
        GD = [arena_b[:, s * TPB * 2 * D:(s + 1) * TPB * 2 * D].rearrange("p (t w) -> p t w", t=TPB) for s in range(RING_D)]
        WMAX = D + 2 * H
        YE_flat = arena_a[:, 0:NB * WMAX]
        CE_flat = arena_a[:, NB * WMAX:2 * NB * WMAX]
        S1 = arena_b[:, 0:NB * D].rearrange("p (b d) -> p b d", b=NB)
        S2 = arena_b[:, NB * D:2 * NB * D].rearrange("p (b d) -> p b d", b=NB)

        same = [sb(f"same{s}", [P, TPB, P]) for s in range(2)]
        msg = [sb(f"msg{s}", [P, TPB, D + H]) for s in range(2)]
        ybuf = [sb(f"ybuf{s}", [P, TPB, WMAX]) for s in range(2)]
        hl = [sb(f"hl{s}", [2, TPB * P], BF16) for s in range(2)]
        rows4 = [sb(f"rows4_{s}", [NT16, TPB * P]) for s in range(2)]
        ea = [sb(f"ea{s}", [P, TPB, T_DIM]) for s in range(2)]
        eat = [sb(f"eat{s}", [P, 2, P]) for s in range(2)]
        runs = [sb(f"runs{s}", [TPB * H, 2, P]) for s in range(2)]
        hid = [sb(f"hid{s}", [HID + 1, TPB * P]) for s in range(2)]
        small = [sb(f"small{s}", [P, 8, TPB * H]) for s in range(2)]
        tlog = [sb(f"tlog{s}", [TPB * H, 4, P]) for s in range(2)]
        RING_IX = 3
        dec_2 = [hid[s][0:2 * NDEC, 0:256].bitcast(BF16) for s in range(2)]
        add_ix = [sb(f"add_ix{s}", [P, TPB], I32) for s in range(RING_IX)]

        Wqkv = sb("Wqkv", [P, 3 * D])
        relb = sb("relb", [P, NET, 3 * D])
        btb = sb("btb", [P, D])
        Wt4 = sb("Wt4", [P, 4 * D])
        Wd1a = sb("Wd1a", [NDEC, HID], BF16)
        Wd2a = sb("Wd2a", [HID + 1, H])
        scale_col = sb("scale_col", [TPB * H, 1])
        hrow = sb("hrow", [P, 4, H])
        wsq = sb("wsq", [P, 6, D])
        wtmp = sb("wtmp", [P, D + 2 * T_DIM])
        frow = sb("frow", [P, 8, D])
        Wf1 = sb("Wf1", [P, 4 * D])
        Wf2 = sb("Wf2", [P, 4, D])
        bf1 = sb("bf1", [P, 4])
        We3 = sb("We3", [T_DIM, D])
        emb = sb("emb", [NT16, T_DIM])
        embT = sb("embT", [T_DIM, NT16])
        Em = sb("Em", [NT16, D])
        W1c = Em[0:2, :]
        cmag = sb("cmag", [P, 8])

        end_ix = sb("end_ix", [P, NB], I32)
        tile_ix = sb("tile_ix", [P, NB], I32)
        npos = sb("npos", [P, 8, NB])
        has_carry, degree, valid = npos[:, 5, :], npos[:, 6, :], npos[:, 7, :]
        chain_row = sb("chain_row", [P, TT])
        first_row = src_tix[:, 0:TT].bitcast(F32)
        last_row = dst_tix[:, 0:TT].bitcast(F32)

        l_w = lane("d_weights")
        l_w2 = lane("d_weights_later")
        l_frow = lane("d_feature_rows")
        l_stage = [lane(f"d_stage{s}") for s in range(4)]
        l_dst = lane("d_dst_table")
        l_dec = lane("d_decay_weights")
        l_x = lane("d_x")
        l_prep = lane("d_prep")
        l_tab = lane("d_tables")
        l_rows = [lane(f"d_rows{s}") for s in range(2)]
        l_hl = [lane(f"d_hl{s}") for s in range(2)]
        l_runs = [lane(f"d_runs{s}") for s in range(2)]
        l_gs = [lane(f"d_src_rows{s}") for s in range(RING)]
        l_gd = [lane(f"d_dst_rows{s}") for s in range(RING_D)]
        l_y = [lane(f"d_y{s}") for s in range(2)]
        l_node = lane("d_node")
        l_nodeg = lane("d_node_gathers")
        l_pos = lane("d_positions")
        l_pos_keys = [lane(f"d_position_keys{s}") for s in range(2)]
        l_win = [lane(f"d_window{s}") for s in range(RING_W)]
        l_hlt = [lane(f"d_hlt{s}") for s in range(2)]
        l_hin = [lane(f"d_h_rows{s}") for s in range(RING)]
        l_acc = [lane(f"d_acc{i}") for i in range(NACC)]
        l_zero = lane("d_zero")
        l_out = lane("d_out")

        win_rows = small[1][:, :, :].rearrange("p k f -> p (k f)")[:, 0:NBLK]

        def row_bc(ap, parts=P):
            return ap.unsqueeze(0).broadcast_to([parts] + list(ap.shape))

        def col(ap):
            return ap.unsqueeze(1)

        c = []
        c.append(VE.do(lambda e: e.memset(ident[:, :], 0.0)))
        c.append(VE.do(lambda e: e.memset(lower[:, :], 1.0)))
        c.append(VE.do(lambda e: e.memset(ones[:, :], 1.0)))
        c.append(VE.do(lambda e: e.memset(hilo_w[:, :], 1.0)))
        c.append(VE.do(lambda e: e.memset(rep8[:, :], 1.0)))
        c.append(VE.do(lambda e: e.memset(win_w[:, :], 1.0)))
        c.append(VE.do(lambda e: e.memset(is_node[:, :], 1.0)))
        c.append(VE.do(lambda e: e.memset(edge_ok[:, :], 1.0)))
        PL.wait(c[-1])
        PL.do(lambda e: e.affine_select(out=ident[:, :], in_=ident[:, :], compare_op=ALU.not_equal, fill=1.0,
                                        base=0, pattern=[[-1, P]], channel_multiplier=1))
        PL.do(lambda e: e.affine_select(out=lower[:, :], in_=lower[:, :], compare_op=ALU.is_gt, fill=0.0,
                                        base=0, pattern=[[-1, P]], channel_multiplier=1))
        PL.do(lambda e: e.affine_select(out=hilo_w[:, :], in_=hilo_w[:, :], compare_op=ALU.is_gt, fill=64.0,
                                        base=0, pattern=[[0, P]], channel_multiplier=1))
        PL.do(lambda e: e.affine_select(out=is_node[:, :], in_=is_node[:, :], compare_op=ALU.is_ge, fill=0.0,
                                        base=WIN - 1, pattern=[[0, 1]], channel_multiplier=-1))
        PL.do(lambda e: e.affine_select(out=win_w[:, WIN:P], in_=win_w[:, WIN:P], compare_op=ALU.is_ge, fill=0.0,
                                        base=-2, pattern=[[0, NET]], channel_multiplier=1))
        k = PL.do(lambda e: e.affine_select(out=win_w[:, 0:WIN], in_=win_w[:, 0:WIN], compare_op=ALU.is_ge, fill=0.0,
                                        base=1, pattern=[[0, WIN]], channel_multiplier=-1))
        PL.wait(k)
        PL.do(lambda e: e.affine_select(out=win_w[:, 0:WIN], in_=win_w[:, 0:WIN], compare_op=ALU.is_gt, fill=64.0,
                                        base=0, pattern=[[0, WIN]], channel_multiplier=1))
        k = PL.do(lambda e: e.affine_select(out=rep8[:, :], in_=rep8[:, :], compare_op=ALU.is_ge, fill=0.0,
                                            base=0, pattern=[[1, D]], channel_multiplier=-DH))
        PL.wait(k)
        PL.do(lambda e: e.affine_select(out=rep8[:, :], in_=rep8[:, :], compare_op=ALU.is_ge, fill=0.0,
                                        base=DH - 1, pattern=[[-1, D]], channel_multiplier=DH))
        PL.do(lambda e: e.affine_select(out=edge_ok[:, :], in_=edge_ok[:, :], compare_op=ALU.is_ge, fill=0.0,
                                        base=E - 1 - (NBLK - 1) * TPB * P, pattern=[[-P, TPB]], channel_multiplier=-1))
        PL.do(lambda e: e.iota(junk[:, :], [[0, 1]], base=N, channel_multiplier=1, allow_small_or_imprecise_dtypes=True))
        PL.do(lambda e: e.iota(node_id[:, :], [[P, NB]], base=0, channel_multiplier=1, allow_small_or_imprecise_dtypes=True))
        const_ready = PL.do(lambda e: e.iota(iota16[:, :], [[0, 1]], base=0, channel_multiplier=1, allow_small_or_imprecise_dtypes=True))

        pad = [VE.do(lambda e: e.memset(X[:, NB - 1, :], 0.0))]
        SP.wait(pad[0])
        x_in = a["x"]
        SP.dma(l_x, X[:, 0:NB - 1, :], x_in[0:(NB - 1) * P, :].rearrange("(b p) d -> p b d", p=P))
        x_ready = SP.dma(l_x, X[0:NLAST, NB - 1, :], x_in[(NB - 1) * P:N, :])

        keys_i = arena_a[:, 0:5 * TC * P].bitcast(I32).rearrange("p (k c f) -> p k c f", k=5, c=TC)
        keys_f = arena_a[:, 5 * TC * P:10 * TC * P].rearrange("p (k c f) -> p k c f", k=5, c=TC)
        tmp_f = arena_b[:, 0:6 * TC * P].rearrange("p (k c f) -> p k c f", k=6, c=TC)
        SRC, DST, TY2, TY16, WGT = range(5)

        def load_tiled(lane_, dst_view, ap, w):
            c6 = (TC - 1) * P * P
            SP.dma(lane_, dst_view[:, 0:TC - 1, :], ap[0:c6 * w].rearrange("(c p f) -> p c f", p=P, f=P * w))
            rest = FULL - (TC - 1) * P
            SP.dma(lane_, dst_view[0:rest, TC - 1, :],
                   ap[c6 * w:FULL * P * w].rearrange("(p f) -> p f", f=P * w))
            return SP.dma(lane_, dst_view[rest:rest + 1, TC - 1, 0:TAIL * w],
                          ap[FULL * P * w:E * w].unsqueeze(0))

        pads = []
        for k_, v_ in ((SRC, int(PADKEY)), (DST, int(PADKEY)), (TY2, 0), (TY16, 0)):
            pads.append(VE.do(lambda e, k_=k_, v_=v_: e.memset(keys_i[:, k_, TC - 1, :], v_)))
        pads.append(VE.do(lambda e: e.memset(keys_f[:, WGT, TC - 1, :], 0.0)))
        SP.wait(pads[-1])
        load_tiled(l_prep, keys_i[:, SRC], a["src"], 1)
        load_tiled(l_prep, keys_i[:, DST], a["dst"], 1)
        load_tiled(l_prep, keys_i[:, TY2], a["edge_type_2"], 1)
        load_tiled(l_prep, keys_i[:, TY16], a["edge_type_16"], 1)
        lists_in = load_tiled(l_prep, keys_f[:, WGT], a["edge_weight"], 1)

        def w_dma(dst_, src_):
            return SP.dma(l_w, dst_, src_)

        for i, n_ in enumerate(("Wq", "Wk", "Wv")):
            w_dma(Wqkv[:, i * D:(i + 1) * D], a["L0_gnn_" + n_])
        for i, n_ in enumerate(("rel_q", "rel_k", "rel_v")):
            w_dma(relb[:, :, i * D:(i + 1) * D], row_bc(a["L0_gnn_" + n_]))
        w_dma(btb[:, :], row_bc(a["L0_gnn_bt"]))
        SP.wait(VE.do(lambda e: e.memset(Wt4[:, :], 0.0)))
        for i in range(4):
            w_dma(Wt4[i * T_DIM:(i + 1) * T_DIM, i * D:(i + 1) * D], a["L0_gnn_Wt"])
        wd = tlog[0][0:1, :, :].rearrange("p k f -> p (k f)")[:, 0:3 * HID].rearrange("p (k f) -> p k f", k=3)
        w_dma(wd[:, 0, :], a["L0_gnn_Wd1"][0:1, :])
        w_dma(wd[:, 1, :], row_bc(a["L0_gnn_bd1"], 1))
        w_dma(wd[:, 2, :], a["L0_gnn_Wd1"][1:2, :])
        w_dma(Wd2a[0:HID, :], a["L0_gnn_Wd2"])
        w_dma(Wd2a[HID:HID + 1, :], row_bc(a["L0_gnn_bd2"], 1))
        w_dma(hrow[:, 0, :], row_bc(a["L0_gnn_decay_scale"]))
        for t in range(TPB):
            w_dma(scale_col[t * H:(t + 1) * H, :], col(a["L0_gnn_decay_scale"]))
        w_dma(hrow[:, 1, :], row_bc(a["L0_gnn_logit_alpha"]))
        w_dma(hrow[:, 2, :], row_bc(a["L0_gnn_hyp_beta"]))
        w_dma(cmag[:, 0:1], a["L0_gnn_c_mag"].unsqueeze(0).broadcast_to([P, 1]))
        weights_first = w_dma(wsq[:, 0, :], a["L0_gnn_Wo"])

        NH_ = NB // 2

        def norm_rows(src_v, dst_v, ready, scratch, relu=False):
            mu, var, neg, shift = (stat[:, i, :] for i in (0, 1, 6, 7))
            VE.wait(*ready)
            VE.chain(lambda e: e.tensor_reduce(mu, src_v, AX, ALU.add))
            k = VE.chain(lambda e: e.tensor_scalar(neg, mu, -1.0 / D, None, ALU.mult))
            AC.wait(k)
            for b in range(NH_):
                k = AC.do(lambda e, b=b: e.activation(scratch[:, b, :], src_v[:, b, :], ACT.Square, bias=neg[:, b:b + 1], accum_out=var[:, b:b + 1]))
            rest = scratch[:, NH_:NB, :]
            VE.chain(lambda e: e.tensor_tensor(rest, src_v[:, NH_:NB, :], bc(neg[:, NH_:NB], 2, D), ALU.add))
            VE.chain(lambda e: e.tensor_tensor(rest, rest, rest, ALU.mult))
            VE.chain(lambda e: e.tensor_reduce(var[:, NH_:NB], rest, AX, ALU.add))
            VE.wait(k)
            VE.chain(lambda e: e.tensor_scalar(var, var, 1.0 / D, EPS, ALU.mult, ALU.add))
            k = VE.chain(lambda e: e.reciprocal(var, var))
            AC.wait(k)
            k = AC.do(lambda e: e.activation(var, var, ACT.Sqrt))
            VE.wait(k)
            k = VE.chain(lambda e: e.tensor_tensor(shift, neg, var, ALU.mult))
            AC.wait(k)
            for b in range(NB):
                if b < NH_:
                    k = AC.do(lambda e, b=b: e.activation(dst_v[:, b, :], src_v[:, b, :], ACT.Relu if relu else ACT.Identity,
                                                          bias=shift[:, b:b + 1], scale=var[:, b:b + 1]))
                else:
                    VE.do(lambda e, b=b: e.tensor_scalar(dst_v[:, b, :], src_v[:, b, :], var[:, b:b + 1], shift[:, b:b + 1], ALU.mult, ALU.add))
            VE.wait((VE.sem, VE.n))
            if relu:
                VE.chain(lambda e: e.tensor_scalar(dst_v[:, NH_:NB, :], dst_v[:, NH_:NB, :], 0.0, None, ALU.max))
            VE.wait(k)
            return VE.chain(lambda e: e.tensor_copy(stat[:, 5, 0:1], stat[:, 6, 0:1]))

        def relu_norm(ready):
            return norm_rows(X[:, :, :], Hn[:, :, :], ready, S2, relu=True)

        def transpose_nodes(src_v, dst_, ready):
            PE.wait(*ready)
            free = [None, None]
            last = None
            for g in range(-(-NB // 4)):
                bs = list(range(4 * g, min(4 * g + 4, NB)))
                bk = 4 + g % 2
                PE.wait(free[g % 2])
                for b in bs:
                    fn = lambda e, b=b, bk=bk: e.transpose(bank[bk][:, (b % 4) * P:(b % 4 + 1) * P], src_v[:, b, :], ident[:, :])
                    if b == bs[-1]:
                        k = PE.do(fn)
                    else:
                        PE.quiet(fn)
                w_ = len(bs) * P
                if g % 2:
                    VE.wait(k)
                    last = free[1] = VE.do(lambda e, bk=bk, w_=w_, g=g: e.tensor_copy(dst_[:, 4 * g * P:4 * g * P + w_], bank[bk][:, 0:w_]))
                else:
                    AC.wait(k)
                    last = free[0] = AC.do(lambda e, bk=bk, w_=w_, g=g: e.activation(dst_[:, 4 * g * P:4 * g * P + w_], bank[bk][:, 0:w_], ACT.Copy))
            return (free[0], free[1])

        def transpose_weight(src_, dst_, ready, parts=P, width=P):
            PE.wait(*ready)
            k = PE.do(lambda e: e.transpose(bank[6][0:width, 0:parts], src_, ident[0:parts, 0:parts]))
            VE.wait(k)
            k = VE.do(lambda e: e.tensor_copy(dst_, bank[6][0:width, 0:parts]))
            PE.wait(k)
            return k

        def store_nodes(tab, view, lane_):
            SP.dma(lane_, tab[0:(NB - 1) * P, :].rearrange("(b p) w -> p b w", p=P), view[:, 0:NB - 1, :])
            return SP.dma(lane_, tab[(NB - 1) * P:N, :], view[0:NLAST, NB - 1, :])

        h_ready = relu_norm((x_ready,))
        PE.wait(const_ready)
        ht_ready = transpose_nodes(Hn, HT, (h_ready,))
        VE.wait(weights_first)
        AC.wait(weights_first)
        s_ = lambda i: stat[:, i, :]
        AC.do(lambda e: e.activation(S2, Hn[:, :, :], ACT.Square))
        k = (AC.sem, AC.n)
        VE.wait(k)
        VE.chain(lambda e: e.tensor_scalar(cmag[:, 1:2], cmag[:, 0:1], -1.0, None, ALU.mult))
        VE.chain(lambda e: e.tensor_tensor(cmag[:, 1:2], cmag[:, 0:1], cmag[:, 1:2], ALU.max))
        VE.chain(lambda e: e.tensor_scalar(cmag[:, 5:6], cmag[:, 1:2], 0.0, None, ALU.is_gt))
        k = VE.chain(lambda e: e.tensor_scalar(cmag[:, 1:2], cmag[:, 1:2], 1e-15, None, ALU.max))
        AC.wait(k)
        k = AC.do(lambda e: e.activation(cmag[:, 2:3], cmag[:, 1:2], ACT.Sqrt))
        VE.wait(k)
        VE.chain(lambda e: e.reciprocal(cmag[:, 3:4], cmag[:, 2:3]))
        VE.chain(lambda e: e.tensor_scalar(cmag[:, 3:4], cmag[:, 3:4], 1.0 - 1e-5, None, ALU.mult))
        k = VE.chain(lambda e: e.tensor_reduce(s_(2), S2, AX, ALU.add))
        AC.wait(k)
        k = AC.do(lambda e: e.activation(s_(2), s_(2), ACT.Sqrt))
        VE.wait(k)
        VE.chain(lambda e: e.tensor_scalar(s_(2), s_(2), 1e-15, None, ALU.max))
        k = VE.chain(lambda e: e.tensor_scalar(s_(3), s_(2), cmag[:, 2:3], None, ALU.mult))
        AC.wait(k)
        k = AC.do(lambda e: e.activation(s_(4), s_(3), ACT.Tanh))
        VE.chain(lambda e: e.reciprocal(s_(5), s_(3)))
        VE.wait(k)
        VE.chain(lambda e: e.tensor_tensor(s_(4), s_(4), s_(5), ALU.mult))
        VE.chain(lambda e: e.tensor_tensor(s_(5), s_(3), s_(3), ALU.mult))
        VE.chain(lambda e: e.tensor_scalar(s_(5), s_(5), 1.0 / 3.0, 1.0, ALU.mult, ALU.add))
        VE.chain(lambda e: e.tensor_tensor(s_(4), s_(4), s_(5), ALU.subtract))
        VE.chain(lambda e: e.scalar_tensor_tensor(out=s_(4), in0=s_(4), scalar=cmag[:, 5:6], in1=s_(5), op0=ALU.mult, op1=ALU.add))
        VE.chain(lambda e: e.tensor_tensor(s_(5), s_(4), s_(2), ALU.mult))
        VE.chain(lambda e: e.tensor_scalar(s_(6), s_(5), 1e-30, None, ALU.max))
        VE.chain(lambda e: e.reciprocal(s_(6), s_(6)))
        VE.chain(lambda e: e.tensor_scalar(s_(6), s_(6), cmag[:, 3:4], -1.0, ALU.mult, ALU.add))
        VE.chain(lambda e: e.tensor_scalar(s_(5), s_(5), cmag[:, 3:4], None, ALU.is_gt))
        VE.chain(lambda e: e.tensor_tensor(s_(6), s_(6), s_(5), ALU.mult))
        VE.chain(lambda e: e.tensor_scalar(s_(6), s_(6), 1.0, None, ALU.add))
        m_scale = VE.chain(lambda e: e.tensor_tensor(s_(4), s_(4), s_(6), ALU.mult))
        PE.wait(*ht_ready)
        VE.wait(lists_in)
        AC.wait(lists_in)
        k = VE.do(lambda e: e.tensor_copy(keys_f[:, 0:4], keys_i[:, 0:4]))
        VE.wait(k)
        hi_i, lo_i = tmp_f[:, 0:1].bitcast(I32), tmp_f[:, 1:2].bitcast(I32)
        hb = arena_b[:, 2 * TC * P:4 * TC * P].bitcast(BF16).rearrange("p (k c f) -> p k c f", k=4, c=TC)
        halves_out = []
        for j, key in enumerate((SRC, DST)):
            VE.do(lambda e, key=key: e.tensor_scalar(hi_i[:, 0], keys_i[:, key], 6, None, ALU.arith_shift_right))
            k = VE.do(lambda e, key=key: e.tensor_scalar(lo_i[:, 0], keys_i[:, key], 63, None, ALU.bitwise_and))
            VE.wait(k)
            VE.do(lambda e, j=j: e.tensor_copy(hb[:, 2 * j], hi_i[:, 0]))
            k = VE.chain(lambda e, j=j: e.tensor_copy(hb[:, 2 * j + 1], lo_i[:, 0]))
            SP.wait(k)
            for i in range(2):
                SP.dma(l_tab, (src_hl, dst_hl)[j][i, :].rearrange("(c p f) -> p c f", p=P, f=P), hb[:, 2 * j + i])
        type_h = arena_b[:, 6 * TC * P:6 * TC * P + TC * P // 2].bitcast(BF16).rearrange("p (c f) -> p c f", c=TC)
        types_out = VE.do(lambda e: e.tensor_copy(type_h, keys_f[:, TY2]))
        SP.wait(types_out)
        types_out = SP.dma(l_tab, dst_hl[2, :].rearrange("(c p f) -> p c f", p=P, f=P), type_h)
        src_c, dst_c, src_t, dst_t = (tmp_f[:, i] for i in (4, 5, 0, 1))
        for o_, key in ((src_c, SRC), (dst_c, DST)):
            k = VE.do(lambda e, o_=o_, key=key: e.scalar_tensor_tensor(
                out=o_, in0=keys_f[:, key], scalar=float(N), in1=keys_f[:, key], op0=ALU.is_lt, op1=ALU.mult))
        VE.wait(k)
        VE.do(lambda e: e.scalar_tensor_tensor(out=src_t, in0=keys_f[:, TY2], scalar=float(N), in1=src_c, op0=ALU.mult, op1=ALU.add))
        lists_ready = VE.do(lambda e: e.scalar_tensor_tensor(out=dst_t, in0=keys_f[:, TY2], scalar=float(N), in1=dst_c, op0=ALU.mult, op1=ALU.add))
        PE.wait(const_ready, lists_ready)
        bank_free = [None] * 8
        cols_ready = None
        for n_, (view, outs_) in enumerate(((keys_f[:, SRC], src_col), (keys_f[:, DST], dst_col), (src_c, src_ix),
                                            (dst_c, dst_ix), (src_t, src_tix), (dst_t, dst_tix))):
            for half in range(2):
                bk = (2 * n_ + half) % 4
                cs = range(4 * half, min(4 * half + 4, TC))
                PE.wait(bank_free[bk])
                for q in cs[:-1]:
                    PE.quiet(lambda e, bk=bk, q=q, view=view: e.transpose(bank[bk][:, (q % 4) * P:(q % 4 + 1) * P], view[:, q, :], ident[:, :]))
                q = cs[-1]
                k = PE.do(lambda e, bk=bk, q=q, view=view: e.transpose(bank[bk][:, (q % 4) * P:(q % 4 + 1) * P], view[:, q, :], ident[:, :]))
                eng = AC if half else VE
                eng.wait(k)
                w_ = len(cs) * P
                if half:
                    bank_free[bk] = AC.do(lambda e, bk=bk, w_=w_, outs_=outs_: e.activation(outs_[:, 4 * P:4 * P + w_], bank[bk][:, 0:w_], ACT.Copy))
                else:
                    bank_free[bk] = VE.do(lambda e, bk=bk, w_=w_, outs_=outs_: e.tensor_copy(outs_[:, 0:w_], bank[bk][:, 0:w_]))
        cols_ready = (bank_free[0], bank_free[1], bank_free[2], bank_free[3])
        pe_lists_done = k

        k = VE.do(lambda e: e.tensor_reduce(cmag[:, 1:2], keys_f[:, TY2], mybir.AxisListType.XY, ALU.max))
        PE.wait(k, bank_free[0])
        k = PE.do(lambda e: e.transpose(bank[4][0:1, 0:P], cmag[:, 1:2], ident[:, :]))
        VE.wait(k)
        VE.chain(lambda e: e.tensor_reduce(cmag[0:1, 2:3], bank[4][0:1, 0:P], AX, ALU.max))
        k = VE.do(lambda e: e.tensor_scalar(cmag[0:1, 3:4], cmag[0:1, 2:3], 1.0, 1.0, ALU.add, ALU.max))
        PE.wait(k)
        k = PE.do(lambda e: e.matmul(bank[4][:, 256:257], ones[0:1, :], cmag[0:1, 3:4], start=True, stop=True))
        VE.wait(k)
        VE.chain(lambda e: e.reciprocal(cmag[:, 4:5], bank[4][:, 256:257]))
        VE.wait(pe_lists_done)
        rF, rB = (tmp_f[:, i] for i in (4, 5))
        VE.wait(types_out)
        parts_v = arena_b[:, 2 * TC * P:4 * TC * P].bitcast(BF16).rearrange("p (k c f) -> p k c f", k=4, c=TC)
        VE.chain(lambda e: e.tensor_copy(parts_v[:, 0], keys_f[:, WGT]))
        VE.chain(lambda e: e.tensor_tensor(tmp_f[:, 0], keys_f[:, WGT], parts_v[:, 0], ALU.subtract))
        VE.chain(lambda e: e.tensor_copy(parts_v[:, 1], tmp_f[:, 0]))
        VE.chain(lambda e: e.tensor_tensor(tmp_f[:, 1], tmp_f[:, 0], parts_v[:, 1], ALU.subtract))
        VE.do(lambda e: e.tensor_copy(parts_v[:, 2], tmp_f[:, 1]))
        k = VE.do(lambda e: e.tensor_scalar(parts_v[:, 3], keys_f[:, TY2], 0.0, None, ALU.is_equal))
        SP.wait(k)
        dec_in = [parts_v[:, i] for i in TIME_PARTS] + [parts_v[:, 3]] * 3 + [type_h] * 3
        for i, v_ in enumerate(dec_in):
            SP.dma(l_tab, dec_rows[i, :].rearrange("(c p f) -> p c f", p=P, f=P), v_)
        VE.wait(weights_first)
        VE.chain(lambda e: e.scalar_tensor_tensor(out=wd[:, 2, :], in0=wd[:, 2, :], scalar=cmag[0:1, 4:5], in1=wd[:, 1, :], op0=ALU.mult, op1=ALU.add))
        w_flat = tlog[1][0:1, :, :].rearrange("p k f -> p (k f)")
        w_part = w_flat[:, 0:9 * HID // 2].bitcast(BF16).rearrange("p (i k f) -> p i k f", i=3, k=3)
        w_left = tlog[0][0:1, :, :].rearrange("p k f -> p (k f)")[:, 3 * HID:6 * HID].rearrange("p (k f) -> p k f", k=3)
        VE.chain(lambda e: e.tensor_copy(w_part[:, 0], wd))
        VE.chain(lambda e: e.tensor_tensor(w_left, wd, w_part[:, 0], ALU.subtract))
        VE.chain(lambda e: e.tensor_copy(w_part[:, 1], w_left))
        VE.chain(lambda e: e.tensor_tensor(w_left, w_left, w_part[:, 1], ALU.subtract))
        k = VE.chain(lambda e: e.tensor_copy(w_part[:, 2], w_left))
        SP.wait(k)
        rows_of = [(i, 0) for i in WEIGHT_PARTS] + [(i, 1) for i in range(3)] + [(i, 2) for i in range(3)]
        for row, (i, j) in enumerate(rows_of):
            k = SP.dma(l_w, Wd1a[row:row + 1, :], w_part[:, i, j, :])
        decay_weights = k
        SP.dma(l_tab, t16_row[0, :].rearrange("(c p f) -> p c f", p=P, f=P), keys_f[:, TY16])
        SP.dma(l_tab, dst_keys.rearrange("(c p) f -> p c f", p=P), keys_f[:, DST])
        SP.dma(l_tab, first_last[0, :].rearrange("(c p) -> p c", p=P), keys_f[:, DST, :, 0], allow_slow_non_contiguous=True)
        SP.dma(l_tab, first_last[1, :].rearrange("(c p) -> p c", p=P), keys_f[:, DST, :, P - 1], allow_slow_non_contiguous=True)
        VE.do(lambda e: e.memset(rF[:, :, 0:1], 1.0))
        VE.do(lambda e: e.memset(rB[:, :, P - 1:P], 1.0))
        VE.do(lambda e: e.tensor_tensor(rF[:, :, 1:P], keys_f[:, DST, :, 1:P], keys_f[:, DST, :, 0:P - 1], ALU.is_equal))
        k = VE.do(lambda e: e.tensor_tensor(rB[:, :, 0:P - 1], keys_f[:, DST, :, 1:P], keys_f[:, DST, :, 0:P - 1], ALU.is_equal))
        VE.wait(k)
        VE.do(lambda e: e.tensor_scalar(rF, rF, BIG, -BIG, ALU.mult, ALU.add))
        k = VE.do(lambda e: e.tensor_scalar(rB, rB, BIG, -BIG, ALU.mult, ALU.add))
        SP.wait(k)
        SP.dma(l_tab, run_rows[0].rearrange("(c p) f -> p c f", p=P), rF)
        lists_out = SP.dma(l_tab, run_rows[1].rearrange("(c p) f -> p c f", p=P), rB)

        k = AC.do(lambda e: e.activation(hrow[:, 3, :], hrow[:, 1, :], ACT.Exp, scale=-1.0))
        VE.wait(k)
        VE.chain(lambda e: e.tensor_scalar(hrow[:, 3, :], hrow[:, 3, :], 1.0, None, ALU.add))
        VE.chain(lambda e: e.reciprocal(hrow[:, 3, :], hrow[:, 3, :]))
        VE.chain(lambda e: e.tensor_scalar(hrow[:, 1, :], hrow[:, 3, :], DH ** -0.5, None, ALU.mult))
        VE.chain(lambda e: e.tensor_scalar(hrow[:, 3, :], hrow[:, 3, :], -1.0, 1.0, ALU.mult, ALU.add))
        VE.chain(lambda e: e.tensor_tensor(hrow[:, 2, :], hrow[:, 2, :], hrow[:, 3, :], ALU.mult))
        VE.chain(lambda e: e.tensor_tensor(relb[:, :, D:2 * D], relb[:, :, D:2 * D], bc(btb[:, :], 1, NET), ALU.add))
        NS = 4
        PE.wait(weights_first, *cols_ready, (VE.sem, VE.n))
        free, sent = [None] * NS, [None] * NS
        AC.wait(m_scale, lists_out)
        VE.wait(lists_out)
        for b in range(NB):
            s = b % NS
            stage_s = arena_a[:, s * 1024:s * 1024 + 768].rearrange("p (y w) -> p y w", y=NET)
            stage_w = arena_a[:, s * 1024 + 768:(s + 1) * 1024]
            PE.wait(free[s])
            k = PE.do(lambda e, b=b, s=s: e.matmul(bank[s][:, 0:3 * D], HT[:, b * P:(b + 1) * P], Wqkv[:, :], start=True, stop=True))
            VE.wait(k, sent[s])
            VE.do(lambda e, s=s, st=stage_s: e.tensor_tensor(st[:, :, 0:2 * D], bc(bank[s][:, D:3 * D], 1, NET), relb[:, :, D:3 * D], ALU.add))
            free[s] = VE.do(lambda e, s=s, st=stage_w: e.tensor_copy(st[:, 0:D], bank[s][:, 0:D]))
            AC.wait(sent[s])
            for y in range(NET):
                AC.do(lambda e, b=b, y=y, st=stage_s: e.activation(st[:, y, 2 * D:3 * D], Hn[:, b, :], ACT.Identity, scale=stat[:, 4, b:b + 1]))
            k = AC.do(lambda e, b=b, st=stage_w: e.activation(st[:, D:2 * D], Hn[:, b, :], ACT.Identity, scale=stat[:, 4, b:b + 1]))
            SP.wait(k, free[s])
            np_ = P if b < NB - 1 else NLAST
            SP.dma(l_stage[s], src0.rearrange("(y n) w -> n y w", y=NET)[b * P:b * P + np_], stage_s[0:np_])
            sent[s] = SP.dma(l_stage[s], dst_win[b * P:b * P + np_, :], stage_w[0:np_])
        zero_rows = Wt4[0:1, D:3 * D].rearrange("p (y d) -> p y d", y=NET)
        SP.dma(l_stage[0], dst_win[N:N + NET, 0:D].unsqueeze(0), relb[0:1, :, 0:D])
        SP.dma(l_stage[0], dst_win[N:N + NET, D:2 * D].unsqueeze(0), zero_rows)
        sent[0] = SP.dma(l_stage[0], tab2b[N:N + NET, :].unsqueeze(0), zero_rows)
        tables0 = sent

        first_r, last_r = hid[0][0:1, 0:TC * P], hid[1][0:1, 0:TC * P]
        SP.wait(lists_out)
        SP.dma(l_tab, first_r, first_last[0:1, :])
        k = SP.dma(l_tab, last_r, first_last[1:2, :])
        VE.wait(k)
        VE.do(lambda e: e.tensor_scalar(first_r, first_r, float(N - 1), None, ALU.min))
        k = VE.do(lambda e: e.tensor_scalar(last_r, last_r, float(N - 1), None, ALU.min))
        VE.wait(k)
        base_r = first_r.rearrange("p (k t) -> p k t", t=TPB)[:, :, 0]
        PE.wait(k)
        kb = PE.do(lambda e: e.matmul(bank[4][:, 0:NBLK], ones[0:1, :], base_r[:, 0:NBLK], start=True, stop=True))
        last_v = last_r.rearrange("p (k t) -> p k t", t=TPB)
        far = cmag[0:1, 6:7]
        VE.chain(lambda e: e.tensor_tensor(last_v, last_v, bc(base_r, 2, TPB), ALU.subtract))
        VE.chain(lambda e: e.tensor_reduce(far, last_r, AX, ALU.max))
        near_ready = VE.chain(lambda e: e.tensor_scalar(all_near[:, 0:1], far, WIN - 0.5, None, ALU.is_lt))
        row_no = cmag[:, 7:8]
        VE.wait(kb, const_ready)
        VE.chain(lambda e: e.tensor_scalar(row_no, is_node[:, :], float(WIN), float(-N - WIN), ALU.mult, ALU.add))
        VE.chain(lambda e: e.tensor_tensor(row_no, row_no, junk[:, :], ALU.add))
        VE.chain(lambda e: e.tensor_scalar(win_node[:, :], bank[4][:, 0:NBLK], is_node[:, 0:1], row_no, ALU.mult, ALU.add))
        VE.chain(lambda e: e.tensor_scalar(small[0][:, 0, 0:1], is_node[:, :], float(-N), float(N), ALU.mult, ALU.add))
        k = VE.chain(lambda e: e.tensor_scalar(win_rows, win_node[:, :], float(N - 1), small[0][:, 0, 0:1], ALU.min, ALU.add))
        windows_ready = VE.chain(lambda e: e.tensor_copy(win_ix[:, :], win_rows))


        def w_dma2(dst_, src_):
            return SP.dma(l_w2, dst_, src_)

        for i, n_ in ((1, "L1_gnn_W1"), (2, "L2_gnn_W2"), (5, "L3_gnn_upd_W")):
            w_dma2(wsq[:, i, :], a[n_])
        w_dma2(wsq[:, 3, :], a["L2_gnn_W1"][0:D, :])
        w_dma2(wsq[:, 4, :], a["L2_gnn_W1"][D:2 * D, :])
        w_dma2(W1c[:, :], a["L2_gnn_W1"][2 * D:2 * D + 2, :])
        w_dma2(wtmp[:, 0:D + T_DIM], a["L3_gnn_msg_W"])
        w_dma2(emb[:, :], a["L3_gnn_edge_emb_W"])
        w_dma2(Wf1[:, :], a["L0_gnn_Wf1"])
        w_dma2(Wf2[:, :, :], a["L0_gnn_Wf2"].rearrange("(c p) n -> p c n", p=P))
        weights_rest = SP.dma(
            l_w2, bf1[:, :], a["L0_gnn_bf1"].rearrange("(c p) -> p c", p=P), allow_slow_non_contiguous=True)

        frow_sets = {
            0: ("L0_gnn_bo", "L0_gnn_g1", "L0_gnn_be1", "L0_gnn_bf2", "L0_gnn_g2", "L0_gnn_be2"),
            1: ("L1_gnn_w2",),
            2: ("L2_gnn_b1", "L2_gnn_b2"),
            3: ("L3_gnn_msg_b", "L3_gnn_upd_b", "L3_gnn_ln_g", "L3_gnn_ln_b"),
        }

        def load_frow(L, after):
            SP.wait(*after)
            for i, n_ in enumerate(frow_sets[L]):
                k = SP.dma(l_frow, frow[:, i, :], row_bc(a[n_]))
            return k

        frow_ready = load_frow(0, ())

        ev = {}

        def got(name, k_):
            return ev.get((name, k_))

        def load_keys(L, k_, rows):
            s = k_ % 2
            SP.wait(got("keys_read", (L, k_ - 2)))
            ev[("keys", (L, k_))] = SP.dma(l_hl[s], hl[s][:, :], rows[0:2, k_ * TPB * P:(k_ + 1) * TPB * P])

        def load_runs(L, k_, nh):
            s = k_ % 2
            SP.wait(got("scan", (L, k_ - 2)))
            for i in range(2):
                src_ = run_rows[i, k_ * TPB:(k_ + 1) * TPB, :]
                ev[("runs", (L, k_))] = SP.dma(l_runs[s], runs[s][0:TPB * nh, i, :], bc(src_, 1, nh) if nh > 1 else src_)

        def same_half(L, k_, key_col, hf):
            s = k_ % 2
            PE.wait(got("keys", (L, k_)), ev.get("bank2_free"))
            kk = ev[("keys_read", (L, k_))] = PE.do(lambda e: e.matmul(bank[2][:, :], hilo_w[:, :], hl[s][:, hf * 512:(hf + 1) * 512], start=True, stop=True))
            VE.wait(kk, got("pe_y", (L, k_ - 2)))
            cols_ = key_col[:, k_ * TPB + 4 * hf:k_ * TPB + 4 * hf + 4]
            ev["bank2_free"] = ev[("same", (L, k_))] = VE.do(lambda e: e.tensor_tensor(
                same[s][:, 4 * hf:4 * hf + 4, :], bank[2][:, :].rearrange("p (t f) -> p t f", t=4), bc(cols_, 2, P), ALU.is_equal))

        def same_matrix(L, k_, key_col):
            for hf in range(2):
                same_half(L, k_, key_col, hf)

        def logits_to_rows(L, k_, nh, logits):
            PE.wait(ev[("logits", (L, k_))], ev.get("bank6_free"))
            ev[("rows", (L, k_))] = PE.do(lambda e: e.transpose(bank[6][0:TPB * nh, 0:P], logits, ident[:, :]))

        def run_scans(L, k_, nh):
            s, R = k_ % 2, TPB * nh
            tl = tlog[s]
            VE.wait(ev[("rows", (L, k_))], got("runs", (L, k_)), got("max_cols", (L, k_ - 2)))
            VE.do(lambda e: e.tensor_tensor_scan(tl[0:R, 0, :], runs[s][0:R, 0, :], bank[6][0:R, 0:P], -BIG, ALU.add, ALU.max))
            k2 = ev[("scan", (L, k_))] = VE.do(lambda e: e.tensor_tensor_scan(
                tl[0:R, 1, ::-1], runs[s][0:R, 1, ::-1], bank[6][0:R, 0:P][:, ::-1], -BIG, ALU.add, ALU.max))
            VE.wait(k2)
            k2 = VE.do(lambda e: e.tensor_tensor(tl[0:R, 2, :], tl[0:R, 0, :], tl[0:R, 1, :], ALU.max))
            PE.wait(k2)
            ev[("max_cols", (L, k_))] = PE.do(lambda e: e.transpose(bank[6][:, 128:128 + R], tl[0:R, 2, :], ident[0:R, 0:R]))

        def less_max(L, k_, nh, logits):
            s, R = k_ % 2, TPB * nh
            VE.wait(ev[("max_cols", (L, k_))], got("exp", (L, k_ - 2)))
            ev[("less", (L, k_))] = VE.do(lambda e: e.tensor_tensor(small[s][:, 7, 0:R], logits, bank[6][:, 128:128 + R], ALU.subtract))

        def exponentials(L, k_, nh):
            s, R = k_ % 2, TPB * nh
            AC.wait(ev[("less", (L, k_))], got("ydma", (L, k_ - 2)))
            ev["bank6_free"] = AC.do(lambda e: e.activation(ybuf[s][:, :, D + nh:D + 2 * nh], bank[6][:, 128:128 + R].rearrange("p (t h) -> p t h", t=TPB), ACT.Copy))
            AC.wait(got("pe_y", (L, k_ - 2)))
            ev[("exp", (L, k_))] = AC.do(lambda e: e.activation(msg[s][:, :, D:D + nh], small[s][:, 7, 0:R].rearrange("p (t h) -> p t h", t=TPB), ACT.Exp))

        def sum_pair(L, k_, w, pair):
            s, bk = k_ % 2, (5, 7)[pair % 2]
            PE.wait(ev[("same", (L, k_))], ev.get(f"bank{bk}_free"))
            for j in range(2):
                t = 2 * pair + j
                fn = lambda e, t=t, j=j: e.matmul(bank[bk][:, j * w:(j + 1) * w], same[s][:, t, :], msg[s][:, t, 0:w], start=True, stop=True)
                if j:
                    kk = ev[("pe_y", (L, k_))] = PE.do(fn)
                else:
                    PE.quiet(fn)
            AC.wait(kk, *got_all("ydma", (L, k_ - 2)))
            ev[f"bank{bk}_free"] = ev[("sums", (L, k_))] = AC.do(lambda e: e.activation(
                ybuf[s][:, 2 * pair:2 * pair + 2, 0:w], bank[bk][:, 0:2 * w].rearrange("p (t f) -> p t f", t=2), ACT.Copy))

        def store_sums(L, k_):
            s = k_ % 2
            SP.wait(ev[("sums", (L, k_))])
            ev[("ydma", (L, k_))] = SP.dma(l_y[s], y_rows[L][k_ * TPB * P:(k_ + 1) * TPB * P, :].rearrange("(t p) w -> p t w", p=P),
                                            ybuf[s][:, :, 0:W_Y[L]])

        def sum_runs(L, k_, w, msg_ready, consume=None):
            PE.wait(*msg_ready)
            for pair in range(TPB // 2):
                sum_pair(L, k_, w, pair)
            if consume is not None:
                ev[("ydma", (L, k_))] = consume(ev[("sums", (L, k_))])
            else:
                store_sums(L, k_)

        def got_all(name, k_):
            e_ = ev.get((name, k_))
            return () if e_ is None else tuple(e_) if isinstance(e_, list) else (e_,)

        def gather_block(name, L, k_, lanes, ring, w, table, ix, *free):
            r = k_ % len(ring)
            PL.wait(*free)
            for t in range(TPB):
                c_ = k_ * TPB + t
                kk = PL.gather(lanes[r], ring[r][:, t, 0:w], table, ix[:, c_:c_ + 1])
            ev[(name, (L, k_))] = kk

        def v3(ap):
            return ap.rearrange("p (t h) -> p t h", t=TPB)

        VE.wait(frow_ready)
        VE.do(lambda e: e.tensor_tensor(Hn[:, :, :], Hn[:, :, :], bc(frow[:, 0, :], 1, NB), ALU.add))
        hid_one = [VE.do(lambda e, s=s: e.memset(hid[s][HID:HID + 1, :], 1.0)) for s in range(2)]
        ea_view = a["edge_attr_32"]
        ea_pad = [VE.do(lambda e, s=s: e.memset(ea[s][:, :, :], 0.0)) for s in range(2)]
        PL.wait(*tables0, *cols_ready)
        PE.wait(decay_weights)
        dec_t = [rows4[s][0:NDEC, 0:TPB * P // 2].bitcast(BF16) for s in range(2)]
        for st in (SP, PL, AC, VE, PE):
            st.wait(near_ready)
        SP.wait(lists_out, hid_one[1], ea_pad[1])
        AC.wait(hid_one[1])

        def l0_loads(k_, stacked=False):
            s = k_ % 2
            SP.wait(got("hid_in", k_ - 2), got("ea_read", k_ - 2))
            for hf in range(2):
                dec_to = dec_2[s][hf * NDEC:(hf + 1) * NDEC, :] if stacked else dec_t[s][:, hf * 512:(hf + 1) * 512]
                SP.dma(l_rows[s], dec_to, dec_rows[:, (2 * k_ + hf) * 512:(2 * k_ + hf + 1) * 512])
            t0 = k_ * TPB
            if k_ < NBLK - 1:
                kk = SP.dma(l_rows[s], ea[s][:, :, :], ea_view[t0 * P:(t0 + TPB) * P, :].rearrange("(t p) c -> p t c", p=P))
            else:
                nf = FULL - t0
                SP.dma(l_rows[s], ea[s][:, 0:nf, :], ea_view[t0 * P:FULL * P, :].rearrange("(t p) c -> p t c", p=P))
                kk = SP.dma(l_rows[s], ea[s][0:TAIL, nf, :], ea_view[FULL * P:E, :])
            ev[("in", k_)] = kk

        def l0_time_cols(k_):
            s = k_ % 2
            PE.wait(ev[("in", k_)], ev.get("bank4_free"))
            for hf in range(2):
                kk = PE.do(lambda e, hf=hf: e.transpose(bank[4][:, hf * P:(hf + 1) * P], ea[s][:, 4 * hf:4 * hf + 4, :].rearrange("p t c -> p (t c)"), ident[:, :]))
            ev[("ea_read", k_)] = kk
            AC.wait(kk, got("time_part", k_ - 2))
            ev[("eat", k_)] = AC.do(lambda e: e.activation(eat[s][:, :, :], bank[4][:, 0:2 * P].rearrange("p (h f) -> p h f", h=2), ACT.Copy))

        def l0_hidden(k_):
            s = k_ % 2
            for hf in range(2):
                PE.wait(ev.get("bank3_free"))
                kk = PE.do(lambda e, hf=hf: e.matmul(bank[3][0:HID, :], Wd1a[:, :], dec_t[s][:, hf * 512:(hf + 1) * 512], start=True, stop=True))
                AC.wait(kk, got("decay_mm", k_ - 2))
                ev["bank3_free"] = AC.do(lambda e, hf=hf: e.activation(hid[s][0:HID, hf * 512:(hf + 1) * 512], bank[3][0:HID, :], ACT.Relu))
            ev[("hid_in", k_)] = kk

        def l0_time_part(k_):
            s = k_ % 2
            PE.wait(ev[("eat", k_)])
            for hf in range(2):
                PE.wait(ev.get(f"bank{hf}_free"))
                ev[("time", (k_, hf))] = ev[("time_part", k_)] = PE.do(
                    lambda e, hf=hf: e.matmul(bank[hf][:, :], eat[s][:, hf, :], Wt4[:, :], start=True, stop=True))

        def l0_decay(k_):
            s = k_ % 2
            dec = small[s][:, 2, :]
            PE.wait(ev["bank3_free"], ev[("eat", k_)])
            for t in range(TPB):
                fn = lambda e, t=t: e.matmul(bank[4][:, 256 + t * H:256 + (t + 1) * H], hid[s][:, t * P:(t + 1) * P], Wd2a[:, :], start=True, stop=True)
                if t == TPB - 1:
                    kk = PE.do(fn)
                else:
                    PE.quiet(fn)
            ev[("decay_mm", k_)] = kk
            AC.wait(kk, got("logits", (0, k_ - 2)))
            kt = ev["bank4_free"] = AC.do(lambda e: e.activation(dec, bank[4][:, 256:256 + TPB * H], ACT.Tanh))
            VE.wait(kt)
            kd = VE.do(lambda e: e.tensor_tensor(v3(dec), v3(dec), bc(hrow[:, 0, :], 1, TPB), ALU.mult))
            AC.wait(kd)
            ev[("decay", k_)] = AC.do(lambda e: e.activation(dec, dec, ACT.Exp))

        def l0_distance(k_):
            s, r, rd = k_ % 2, k_ % RING, k_ % RING_D
            d2 = small[s][:, 1, 0:TPB]
            VE.wait(ev[("gs", (0, k_))], ev[("gd", (0, k_))])
            kdf = VE.do(lambda e: e.tensor_tensor(GS[r][:, :, 2 * D:3 * D], GS[r][:, :, 2 * D:3 * D], GD[rd][:, :, D:2 * D], ALU.subtract))
            AC.wait(kdf, got("logits", (0, k_ - 2)))
            for t in range(TPB):
                ksq = AC.do(lambda e, t=t: e.activation(GS[r][:, t, 2 * D:3 * D], GS[r][:, t, 2 * D:3 * D], ACT.Square, accum_out=d2[:, t:t + 1]))
            AC.wait(ksq)
            ev[("dist", k_)] = AC.do(lambda e: e.activation(d2, d2, ACT.Sqrt))

        def l0_scores(k_):
            s, r, rd = k_ % 2, k_ % RING, k_ % RING_D
            eu = small[s][:, 0, :]
            for hf in range(2):
                VE.wait(ev[("time", (k_, hf))])
                g_ = GS[r][:, 4 * hf:4 * hf + 4, 0:D]
                ev[f"bank{hf}_free"] = k2 = VE.do(lambda e, g_=g_, hf=hf: e.tensor_tensor(g_, g_, bank[hf][:, :].rearrange("p (t f) -> p t f", t=4), ALU.add))
            VE.wait(k2)
            ev[("gd_used", (0, k_))] = VE.chain(lambda e: e.tensor_tensor(GS[r][:, :, 0:D], GS[r][:, :, 0:D], GD[rd][:, :, 0:D], ALU.mult))
            ev[("scores", k_)] = VE.do(lambda e: e.tensor_reduce(v3(eu), GS[r][:, :, 0:D].rearrange("p t (h w) -> p t h w", h=H), AX, ALU.add))

        def l0_logits(k_):
            s = k_ % 2
            eu, d2, dec, lg, t1 = small[s][:, 0, :], small[s][:, 1, 0:TPB], small[s][:, 2, :], small[s][:, 3, :], small[s][:, 4, :]
            VE.wait(ev[("dist", k_)], ev[("scores", k_)])
            VE.do(lambda e: e.tensor_tensor(v3(t1), bc(d2, 2, H), bc(hrow[:, 2, :], 1, TPB), ALU.mult))
            VE.chain(lambda e: e.tensor_tensor(v3(eu), v3(eu), bc(hrow[:, 1, :], 1, TPB), ALU.mult))
            VE.chain(lambda e: e.tensor_tensor(eu, eu, t1, ALU.subtract))
            VE.wait(ev[("decay", k_)])
            ev[("logits", (0, k_))] = VE.do(lambda e: e.tensor_tensor(lg, eu, dec, ALU.mult))

        def l0_messages(k_):
            s, r = k_ % 2, k_ % RING
            VE.wait(ev[("exp", (0, k_))])
            km = ev[("gs_used", (0, k_))] = VE.do(lambda e: e.tensor_tensor(
                msg[s][:, :, 0:D].rearrange("p t (h w) -> p t h w", h=H), GS[r][:, :, D:2 * D].rearrange("p t (h w) -> p t h w", h=H),
                bc(msg[s][:, :, D:D + H], 3, DH), ALU.mult))
            sum_runs(0, k_, D + H, (km,))

        def lg0(k_):
            return small[k_ % 2][:, 3, :]

        def node_positions(first_row, last_row, keys_of):
            SP.dma(l_pos, first_row, row_bc(first_last[0, 0:TT]))
            rows_in = SP.dma(l_pos, last_row, row_bc(first_last[1, 0:TT]))
            yield
            VE.wait(rows_in)
            VE.do(lambda e: e.memset(chain_row[:, 0:2], 0.0))
            VE.chain(lambda e: e.tensor_tensor(chain_row[:, 2:TT], first_row[:, 1:TT - 1], last_row[:, 1:TT - 1], ALU.is_equal))
            VE.chain(lambda e: e.tensor_tensor(first_row[:, 1:TT], first_row[:, 1:TT], last_row[:, 0:TT - 1], ALU.is_equal))
            VE.chain(lambda e: e.tensor_tensor(chain_row[:, 2:TT], chain_row[:, 2:TT], first_row[:, 1:TT - 1], ALU.mult))
            te, cnt, end, start, lastp = (npos[:, i, :] for i in range(5))
            for b in range(NB):
                yield
                VE.chain(lambda e, b=b: e.tensor_scalar(first_row, last_row, node_id[:, b:b + 1], None, ALU.is_le))
                VE.chain(lambda e, b=b: e.tensor_reduce(te[:, b:b + 1], first_row, AX, ALU.add))
            copied = VE.chain(lambda e: e.tensor_copy(end_ix[:, :], te))
            PL.wait(copied)
            counted = [None, None]
            for b in range(NB):
                keys_b = keys_of[b % 2]
                PL.wait(counted[b % 2])
                keys_in = PL.gather(l_pos_keys[b % 2], keys_b, dst_keys, end_ix[:, b:b + 1])
                yield
                VE.wait(keys_in)
                VE.chain(lambda e, b=b, keys_b=keys_b: e.tensor_scalar(keys_b, keys_b, node_id[:, b:b + 1], None, ALU.is_le))
                counted[b % 2] = VE.chain(lambda e, b=b, keys_b=keys_b: e.tensor_reduce(cnt[:, b:b + 1], keys_b, AX, ALU.add))
            VE.chain(lambda e: e.scalar_tensor_tensor(out=end, in0=te, scalar=float(P), in1=cnt, op0=ALU.mult, op1=ALU.add))
            k_ = VE.chain(lambda e: e.memset(start, 0.0))
            yield
            SP.wait(k_)
            k_ = SP.dma(l_pos, end_pos[1:NB * P + 1].rearrange("(b p) -> p b", p=P), end, allow_slow_non_contiguous=True)
            yield
            SP.wait(k_)
            SP.dma(l_pos, start[1:P, :], end_pos[1:NB * P + 1].rearrange("(b p) -> p b", p=P)[0:P - 1, :], allow_slow_non_contiguous=True)
            k_ = SP.dma(l_pos, start[0:1, 1:NB], end_pos[1:NB * P + 1].rearrange("(b p) -> p b", p=P)[P - 1:P, 0:NB - 1], allow_slow_non_contiguous=True)
            yield
            VE.wait(k_)
            VE.chain(lambda e: e.tensor_tensor(degree, end, start, ALU.subtract))
            VE.chain(lambda e: e.tensor_scalar(valid, degree, 0.0, None, ALU.is_gt))
            VE.chain(lambda e: e.tensor_scalar(lastp, end, -1.0, 0.0, ALU.add, ALU.max))
            VE.chain(lambda e: e.tensor_copy(end_ix[:, :], lastp))
            VE.chain(lambda e: e.tensor_scalar(tile_ix[:, :], end_ix[:, :], 7, None, ALU.arith_shift_right))
            VE.chain(lambda e: e.tensor_copy(te, tile_ix[:, :]))
            VE.chain(lambda e: e.scalar_tensor_tensor(out=has_carry, in0=te, scalar=float(P), in1=start, op0=ALU.mult, op1=ALU.is_gt))
            VE.chain(lambda e: e.tensor_tensor(has_carry, has_carry, valid, ALU.mult))

        def load_window(L, k_, table, w):
            r = k_ % RING_W
            PL.wait(got("window_used", (L, k_ - RING_W)))
            ev[("window", (L, k_))] = PL.gather(l_win[r], win[r][:, 0:w], table, win_ix[:, k_:k_ + 1])

        def load_window_keys(L, k_):
            s = k_ % 2
            SP.wait(got("hlt_read", (L, k_ - 2)))
            ev[("hlt", (L, k_))] = SP.dma(l_hlt[s], hlt[s], dst_hl[:, k_ * TPB * P:(k_ + 1) * TPB * P])

        def pick_matrix(L, k_, hf):
            s = k_ % 2
            PE.wait(ev[("hlt", (L, k_))], ev.get("bank2_free"))
            kk = ev[("hlt_read", (L, k_))] = PE.do(lambda e: e.matmul(bank[2][:, :], win_w[:, :], hlt[s][:, hf * 512:(hf + 1) * 512], start=True, stop=True))
            VE.wait(kk, got("window_used", (L, k_ - 2)))
            ev["bank2_free"] = ev[("pick", (L, k_, hf))] = VE.do(lambda e: e.tensor_scalar(
                pick[s][:, 4 * hf:4 * hf + 4, :], bank[2][:, :].rearrange("p (t f) -> p t f", t=4), win_node[:, k_:k_ + 1], None, ALU.is_equal))

        def w_time_cols(k_):
            s = k_ % 2
            PE.wait(ev[("in", k_)], ev.get("bank3_free"))
            for hf in range(2):
                kk = PE.do(lambda e, hf=hf: e.transpose(bank[3][:, hf * P:(hf + 1) * P], ea[s][:, 4 * hf:4 * hf + 4, :].rearrange("p t c -> p (t c)"), ident[:, :]))
            ev[("ea_read", k_)] = kk
            AC.wait(kk, got("time_part", k_ - 2))
            ev["bank3_free"] = ev[("eat", k_)] = AC.do(lambda e: e.activation(eat[s][:, :, :], bank[3][:, 0:2 * P].rearrange("p (h f) -> p h f", h=2), ACT.Copy))

        def w_hidden(k_):
            s = k_ % 2
            PE.wait(ev["bank3_free"])
            kk = ev[("hid_in", k_)] = PE.do(lambda e: e.matmul(bank[3][:, :], wd1_2, dec_2[s], start=True, stop=True))
            AC.wait(kk, got("decay_mm", k_ - 2))
            ev["bank3_free"] = AC.do(lambda e: e.activation(hid_2[s], bank[3][:, :], ACT.Relu))

        def w_decay(k_):
            s = k_ % 2
            rows_ = bank[3][0:TPB * H, 0:P]
            PE.wait(ev["bank3_free"])
            for t in range(TPB // 2):
                lo = (TPB - 1 - t) * H
                kk = PE.do(lambda e, t=t, lo=lo: e.matmul(rows_, wd2_wide[:, lo:lo + TPB * H], hid_2[s][:, t * P:(t + 1) * P], start=(t == 0), stop=(t == TPB // 2 - 1)))
            ev[("decay_mm", k_)] = kk
            AC.wait(kk, got("decayed", k_ - 2))
            kt = ev["bank3_free"] = AC.do(lambda e: e.activation(tlog[s][:, 3, :], rows_, ACT.Tanh, bias=bias_col))
            AC.wait(kt)
            ev[("decay", k_)] = AC.do(lambda e: e.activation(tlog[s][:, 3, :], tlog[s][:, 3, :], ACT.Exp, scale=scale_col[:, 0:1]))

        def w_run_maxima(k_):
            s, R = k_ % 2, TPB * H
            tl = tlog[s]
            PE.wait(ev[("logits", (0, k_))], ev.get("bank6_free"))
            kr = ev[("rows", (0, k_))] = PE.do(lambda e: e.transpose(bank[6][0:R, 0:P], lg0(k_), ident[:, :]))
            VE.wait(kr, ev[("decay", k_)], got("runs", (0, k_)), got("max_cols", k_ - 2))
            k1 = ev[("decayed", k_)] = VE.do(lambda e: e.tensor_tensor(tl[:, 0, :], bank[6][0:R, 0:P], tl[:, 3, :], ALU.mult))
            VE.wait(k1)
            VE.do(lambda e: e.tensor_tensor_scan(tl[:, 1, :], runs[s][:, 0, :], tl[:, 0, :], -BIG, ALU.add, ALU.max))
            k1 = ev[("scan", (0, k_))] = VE.do(lambda e: e.tensor_tensor_scan(
                tl[:, 2, ::-1], runs[s][:, 1, ::-1], tl[:, 0, ::-1], -BIG, ALU.add, ALU.max))
            VE.wait(k1)
            VE.chain(lambda e: e.tensor_tensor(tl[:, 1, :], tl[:, 1, :], tl[:, 2, :], ALU.max))
            k1 = VE.do(lambda e: e.tensor_tensor(tl[:, 0, :], tl[:, 0, :], tl[:, 1, :], ALU.subtract))
            ev[("less_rows", k_)] = k1

        def w_exp_rows(k_):
            s = k_ % 2
            tl = tlog[s]
            AC.wait(ev[("less_rows", k_)])
            ev[("exp_rows", k_)] = AC.do(lambda e: e.activation(tl[:, 2, :], tl[:, 0, :], ACT.Exp))

        def w_exp_cols(k_):
            s, R = k_ % 2, TPB * H
            tl = tlog[s]
            PE.wait(ev[("exp_rows", k_)])
            PE.quiet(lambda e: e.transpose(bank[6][:, 2 * P:2 * P + R], tl[:, 2, :], ident[0:R, 0:R]))
            kk = ev[("max_cols", k_)] = PE.do(lambda e: e.transpose(bank[6][:, P:P + R], tl[:, 1, :], ident[0:R, 0:R]))
            AC.wait(kk, got("pe_y", (0, k_ - 2)), got("ydma", (0, k_ - 2)))
            ev[("exp", (0, k_))] = AC.do(lambda e: e.activation(msg[s][:, :, D:D + H], v3(bank[6][:, 2 * P:2 * P + R]), ACT.Copy))
            ev["bank6_free"] = AC.do(lambda e: e.activation(ybuf[s][:, :, D + H:D + 2 * H], v3(bank[6][:, P:P + R]), ACT.Copy))

        def w_logits(k_):
            s = k_ % 2
            eu, d2, lg, t1 = small[s][:, 0, :], small[s][:, 1, 0:TPB], small[s][:, 3, :], small[s][:, 4, :]
            AC.wait(ev[("squares", k_)])
            ev[("dist", k_)] = AC.do(lambda e: e.activation(d2, d2, ACT.Sqrt))
            VE.wait(ev[("kq", (k_, 1))])
            ks = VE.do(lambda e: e.tensor_reduce(v3(eu), GS[k_ % RING][:, :, 0:D].rearrange("p t (h w) -> p t h w", h=H), AX, ALU.add))
            VE.wait(ev[("dist", k_)], ks, got("rows", (0, k_ - 2)))
            VE.do(lambda e: e.tensor_tensor(v3(t1), bc(d2, 2, H), bc(hrow[:, 2, :], 1, TPB), ALU.mult))
            VE.chain(lambda e: e.tensor_tensor(v3(eu), v3(eu), bc(hrow[:, 1, :], 1, TPB), ALU.mult))
            ev[("logits", (0, k_))] = VE.do(lambda e: e.tensor_tensor(lg, eu, t1, ALU.subtract))

        def w_products(k_, hf):
            s, r = k_ % 2, k_ % RING_W
            PE.wait(ev[("eat", k_)], ev.get("bank0_free"))
            ev[("time", (k_, hf))] = ev[("time_part", k_)] = PE.do(
                lambda e: e.matmul(bank[0][:, :], eat[s][:, hf, :], Wt4[:, :], start=True, stop=True))
            PE.wait(ev[("window", (0, k_))], ev[("pick", (0, k_, hf))])
            for name, bk, lo in (("q", 1, 0), ("m", 4, D)):
                PE.wait(ev.get(f"bank{bk}_free"))
                for t in range(4):
                    fn = lambda e, t=t, bk=bk, lo=lo: e.matmul(bank[bk][:, t * P:(t + 1) * P], pick[s][:, 4 * hf + t, :], win[r][:, lo:lo + D], start=True, stop=True)
                    if t == 3:
                        kk = PE.do(fn)
                    else:
                        PE.quiet(fn)
                ev[(name, (k_, hf))] = kk
            ev[("window_used", (0, k_))] = kk

        def w_scores(k_, hf):
            r, s = k_ % RING, k_ % 2
            K_, M_ = GS[r][:, 4 * hf:4 * hf + 4, 0:D], GS[r][:, 4 * hf:4 * hf + 4, 2 * D:3 * D]
            b4 = lambda i: bank[i][:, :].rearrange("p (t f) -> p t f", t=4)
            VE.wait(ev[("gs", (0, k_))], ev[("time", (k_, hf))])
            kt = ev["bank0_free"] = VE.do(lambda e: e.tensor_tensor(K_, K_, b4(0), ALU.add))
            VE.wait(ev[("m", (k_, hf))])
            km = ev["bank4_free"] = VE.do(lambda e: e.tensor_tensor(M_, M_, b4(4), ALU.subtract))
            VE.wait(kt, ev[("q", (k_, hf))])
            kq = ev["bank1_free"] = ev[("kq", (k_, hf))] = VE.do(lambda e: e.tensor_tensor(K_, K_, b4(1), ALU.mult))
            d2 = small[s][:, 1, 0:TPB]
            AC.wait(km, got("logits", (0, k_ - 2)))
            for t in range(4 * hf, 4 * hf + 4):
                ksq = AC.do(lambda e, t=t: e.activation(GS[r][:, t, 2 * D:3 * D], GS[r][:, t, 2 * D:3 * D], ACT.Square, accum_out=d2[:, t:t + 1]))
            ev[("squares", k_)] = ksq

        def w_messages(k_):
            s, r = k_ % 2, k_ % RING
            VE.wait(ev[("exp", (0, k_))], got("pe_y", (0, k_ - 2)))
            ev[("gs_used", (0, k_))] = VE.do(lambda e: e.tensor_tensor(
                msg[s][:, :, 0:D].rearrange("p t (h w) -> p t h w", h=H), GS[r][:, :, D:2 * D].rearrange("p t (h w) -> p t h w", h=H),
                bc(msg[s][:, :, D:D + H], 3, DH), ALU.mult))

        def l0_edges_windows():
            VE.wait(*tables0, windows_ready)
            VE.do(lambda e: e.memset(wd2_wide, 0.0))
            SP.wait(VE.do(lambda e: e.memset(wd1_2, 0.0)), decay_weights)
            o_ = (TPB - 1) * H
            SP.dma(l_dec, wd2_wide[0:HID, o_:o_ + H], a["L0_gnn_Wd2"])
            SP.dma(l_dec, wd2_wide[HID:2 * HID, o_ + 4 * H:o_ + 5 * H], a["L0_gnn_Wd2"])
            SP.dma(l_dec, wd1_2[0:NDEC, 0:HID], Wd1a[:, :])
            SP.dma(l_dec, wd1_2[NDEC:2 * NDEC, HID:2 * HID], Wd1a[:, :])
            for t in range(TPB):
                k = SP.dma(l_dec, bias_col[t * H:(t + 1) * H, :], col(a["L0_gnn_bd2"]))
            PE.wait(k)
            AC.wait(k)
            PL.wait(windows_ready)
            SP.wait(*tables0)
            o_ = 4096
            positions = node_positions(arena_b[:, o_:o_ + TT], last_row,
                                       [arena_b[:, o_ + TT + i * P:o_ + TT + (i + 1) * P] for i in range(2)])
            for n in range(NBLK + 3):
                next(positions, None)
                i0, i1, i2, i3 = n, n - 1, n - 2, n - 3
                b0, b1, b2, b3 = n < NBLK, 0 <= n - 1 < NBLK, 0 <= n - 2 < NBLK, 0 <= n - 3
                if b0:
                    load_window(0, i0, dst_win, 2 * D)
                    gather_block("gs", 0, i0, l_gs, GS, 3 * D, src0, src_tix, got("gs_used", (0, i0 - RING)), got("dist", i0 - RING))
                for j in (0, 1) if n == 0 else (n + 1,):
                    if j < NBLK:
                        load_window_keys(0, j)
                        l0_loads(j, True)
                if b1:
                    load_runs(0, i1, H)
                    load_keys(0, i1, dst_hl)
                if b3:
                    w_messages(i3)
                if b1:
                    w_products(i1, 0)
                if b0:
                    w_time_cols(i0)
                if b1:
                    w_scores(i1, 0)
                if b2:
                    w_run_maxima(i2)
                if b3:
                    PE.wait(ev[("gs_used", (0, i3))])
                    sum_pair(0, i3, D + H, 0)
                if b0:
                    w_hidden(i0)
                if b2:
                    w_exp_rows(i2)
                    same_half(0, i2, dst_col, 0)
                if b1:
                    w_products(i1, 1)
                if b3:
                    sum_pair(0, i3, D + H, 1)
                if b1:
                    w_scores(i1, 1)
                if b2:
                    w_exp_cols(i2)
                    same_half(0, i2, dst_col, 1)
                if b3:
                    sum_pair(0, i3, D + H, 2)
                if b0:
                    pick_matrix(0, i0, 0)
                if b3:
                    sum_pair(0, i3, D + H, 3)
                    store_sums(0, i3)
                if b0:
                    pick_matrix(0, i0, 1)
                if b1:
                    w_logits(i1)
                if b0:
                    w_decay(i0)

        def l0_edges_any():
            q_m = arena_a[:, 0:2 * D]
            stage = arena_a[:, 2 * D:6 * D].rearrange("p (y w) -> p y w", y=NET)
            stored = None
            SP.wait(*tables0)
            VE.wait(*tables0)
            for b in range(NB):
                np_ = P if b < NB - 1 else NLAST
                SP.wait(stored, (VE.sem, VE.n))
                k = SP.dma(l_dst, q_m[0:np_, :], dst_win[b * P:b * P + np_, :])
                VE.wait(k)
                VE.do(lambda e: e.tensor_tensor(stage[:, :, 0:D], bc(q_m[:, 0:D], 1, NET), relb[:, :, 0:D], ALU.add))
                k = VE.do(lambda e: e.tensor_copy(stage[:, :, D:2 * D], bc(q_m[:, D:2 * D], 1, NET)))
                SP.wait(k)
                stored = SP.dma(l_dst, dst0.rearrange("(y n) w -> n y w", y=NET)[b * P:b * P + np_], stage[0:np_])
            PL.wait(stored)
            for n in range(NBLK + 3):
                i0, i1, i2, i3 = n, n - 1, n - 2, n - 3
                b0, b1, b2, b3 = n < NBLK, 0 <= n - 1 < NBLK, 0 <= n - 2 < NBLK, 0 <= n - 3
                if b0:
                    gather_block("gd", 0, i0, l_gd, GD, 2 * D, dst0, dst_tix, got("gd_used", (0, i0 - RING_D)))
                    gather_block("gs", 0, i0, l_gs, GS, 3 * D, src0, src_tix, got("gs_used", (0, i0 - RING)), got("dist", i0 - RING))
                for j in (0, 1) if n == 0 else (n + 1,):
                    if j < NBLK:
                        l0_loads(j)
                if b1:
                    load_runs(0, i1, H)
                if b2:
                    load_keys(0, i2, dst_hl)
                    logits_to_rows(0, i2, H, lg0(i2))
                if b0:
                    l0_time_cols(i0)
                if b1:
                    l0_distance(i1)
                if b2:
                    run_scans(0, i2, H)
                if b0:
                    l0_hidden(i0)
                if b1:
                    l0_scores(i1)
                if b2:
                    less_max(0, i2, H, lg0(i2))
                    exponentials(0, i2, H)
                if b3:
                    same_matrix(0, i3, dst_col)
                if b0:
                    l0_time_part(i0)
                if b3:
                    l0_messages(i3)
                if b1:
                    l0_logits(i1)
                if b0:
                    l0_decay(i0)

            SP.wait((PL.sem, PL.n), ev[("gs", (0, NBLK - 1))], ev[("gd", (0, NBLK - 1))], (VE.sem, VE.n))
            for _ in node_positions(first_row[:, :], last_row[:, :], [YE_flat[:, i * P:(i + 1) * P] for i in range(2)]):
                pass

        engines = (SP, PL, AC, VE, PE)
        l_far = l_gd + l_win + l_hlt + [l_dst, l_dec]
        lanes_ = [l_pos, *l_pos_keys, l_w, l_w2, l_frow, l_x, l_prep, l_tab, l_node, l_nodeg, l_zero, l_out] + l_stage + l_rows + l_hl + l_runs + l_gs + l_y + l_far
        either(engines, lanes_, l_far, ev, all_near[0:1, 0:1], l0_edges_windows, l0_edges_any)

        def join_runs(L, nh):
            wy = W_Y[L]
            YE = YE_flat[:, 0:NB * wy].rearrange("p (b w) -> p b w", b=NB)
            CE = CE_flat[:, 0:NB * wy].rearrange("p (b w) -> p b w", b=NB)
            LR = arena_b[:, 0:TC * wy].rearrange("p (c w) -> p c w", c=TC)
            work = arena_b[:, TC * WMAX:TC * WMAX + 5 * TT].rearrange("p (k t) -> p k t", k=5)
            y_out = ((l_y[0].sem, l_y[0].n), (l_y[1].sem, l_y[1].n))
            PL.wait(*y_out, (VE.sem, VE.n))
            for b in range(NB):
                ye_ready = PL.gather(l_nodeg, YE[:, b, :], y_rows[L], end_ix[:, b:b + 1])
            lasts = y_rows[L].rearrange("(t e) w -> t e w", e=P)[:, P - 1, :]
            SP.wait(*y_out, (VE.sem, VE.n))
            SP.dma(l_tab, LR[:, 0:TC - 1, :], lasts[0:(TC - 1) * P, :].rearrange("(c p) w -> p c w", p=P))
            rest = TT - (TC - 1) * P
            k_ = SP.dma(l_tab, LR[0:rest, TC - 1, :], lasts[(TC - 1) * P:TT, :])
            PE.wait(k_, (VE.sem, VE.n), (AC.sem, AC.n))
            parts = [(0, D, P)] + ([(D, D + nh, nh), (D + nh, D + 2 * nh, nh)] if nh else [])
            rows = [work[:, i, :] for i in range(5)]
            for i, (lo, hi, m_) in enumerate(parts):
                for g in range(2):
                    bk = 2 * (i % 2) + g
                    cs = range(4 * g, min(4 * g + 4, TC))
                    PE.wait((VE.sem, VE.n), (AC.sem, AC.n))
                    for q in cs:
                        np_ = P if q < TC - 1 else rest
                        k_ = PE.do(lambda e, bk=bk, q=q, np_=np_, lo=lo, hi=hi, m_=m_: e.transpose(
                            bank[bk][0:m_, (q % 4) * P:(q % 4) * P + np_], LR[0:np_, q, lo:hi], ident[0:np_, 0:np_]))
                    w_ = min(TT - 4 * g * P, 4 * P)
                    VE.wait(k_)
                    VE.do(lambda e, bk=bk, g=g, w_=w_, i=i, m_=m_: e.tensor_copy(rows[i][0:m_, 4 * g * P:4 * g * P + w_], bank[bk][0:m_, 0:w_]))
            VE.wait((VE.sem, VE.n))
            num, den, mx, gg, ff = rows
            S_num, S_den, S_mx = first_row, last_row, gg
            VE.chain(lambda e: e.memset(S_num[:, 0:1], 0.0))
            if nh:
                cr = chain_row[0:nh, 1:TT]
                sm_, ex_g, ex_f, sd_ = rows4[0][:, 0:TT], rows4[1][:, 0:TT], hid[0][:, 0:TT], hid[1][:, 0:TT]
                VE.chain(lambda e: e.memset(sm_[0:nh, 0:1], -BIG))
                VE.chain(lambda e: e.memset(sd_[0:nh, 0:1], 0.0))
                VE.chain(lambda e: e.tensor_scalar(ex_g[0:nh, 1:TT], cr, BIG, -BIG, ALU.mult, ALU.add))
                VE.chain(lambda e: e.tensor_tensor_scan(sm_[0:nh, 1:TT], ex_g[0:nh, 1:TT], mx[0:nh, 0:TT - 1], -BIG, ALU.add, ALU.max))
                VE.chain(lambda e: e.tensor_tensor(ex_g[0:nh, 1:TT], sm_[0:nh, 0:TT - 1], sm_[0:nh, 1:TT], ALU.subtract))
                k_ = VE.chain(lambda e: e.tensor_tensor(ex_f[0:nh, 1:TT], mx[0:nh, 0:TT - 1], sm_[0:nh, 1:TT], ALU.subtract))
                AC.wait(k_)
                AC.do(lambda e: e.activation(ex_g[0:nh, 1:TT], ex_g[0:nh, 1:TT], ACT.Exp))
                k_ = AC.do(lambda e: e.activation(ex_f[0:nh, 1:TT], ex_f[0:nh, 1:TT], ACT.Exp))
                VE.wait(k_)
                VE.chain(lambda e: e.tensor_tensor(ex_g[0:nh, 1:TT], ex_g[0:nh, 1:TT], cr, ALU.mult))
                VE.chain(lambda e: e.tensor_tensor(den[0:nh, 0:TT - 1], den[0:nh, 0:TT - 1], ex_f[0:nh, 1:TT], ALU.mult))
                k_ = VE.chain(lambda e: e.tensor_tensor_scan(sd_[0:nh, 1:TT], ex_g[0:nh, 1:TT], den[0:nh, 0:TT - 1], 0.0, ALU.mult, ALU.add))
                PE.wait(k_)
                rp = rep8[:, :] if nh == H else ones[0:1, :]
                HALF = TT // 2
                for i, src_ in enumerate((ex_g, ex_f)):
                    for g in range(2):
                        lo_ = max(1, g * HALF)
                        k_ = PE.do(lambda e, i=i, g=g, src_=src_, lo_=lo_: e.matmul(
                            bank[2 * i + g][:, lo_ - g * HALF:HALF], rp, src_[0:nh, lo_:(g + 1) * HALF], start=True, stop=True))
                VE.wait(k_)
                for g in range(2):
                    lo_ = max(1, g * HALF)
                    VE.do(lambda e, g=g, lo_=lo_: e.tensor_copy(gg[:, lo_:(g + 1) * HALF], bank[g][:, lo_ - g * HALF:HALF]))
                    VE.do(lambda e, g=g, lo_=lo_: e.tensor_tensor(ff[:, lo_:(g + 1) * HALF], num[:, lo_ - 1:(g + 1) * HALF - 1], bank[2 + g][:, lo_ - g * HALF:HALF], ALU.mult))
                VE.wait((VE.sem, VE.n))
                k_ = VE.chain(lambda e: e.tensor_tensor_scan(S_num[:, 1:TT], gg[:, 1:TT], ff[:, 1:TT], 0.0, ALU.mult, ALU.add))
                outs_ = [(S_num, 0, D, P), (sd_, D, D + nh, nh), (sm_, D + nh, D + 2 * nh, nh)]
            else:
                k_ = VE.chain(lambda e: e.tensor_tensor_scan(S_num[:, 1:TT], chain_row[:, 1:TT], num[:, 0:TT - 1], 0.0, ALU.mult, ALU.add))
                outs_ = [(S_num, 0, D, P)]
            PE.wait(k_)
            for src_, lo, hi, m_ in outs_:
                for g in range(2):
                    PE.wait((VE.sem, VE.n))
                    cs = range(4 * g, min(4 * g + 4, TC))
                    for q in cs:
                        np_ = P if q < TC - 1 else rest
                        k_ = PE.do(lambda e, g=g, q=q, np_=np_, m_=m_, src_=src_: e.transpose(
                            bank[g][0:np_, (q % 4) * m_:(q % 4 + 1) * m_], src_[0:m_, q * P:q * P + np_], ident[0:m_, 0:m_]))
                    VE.wait(k_)
                    nf = len([q for q in cs if q < TC - 1])
                    VE.do(lambda e, g=g, nf=nf, m_=m_, lo=lo, hi=hi: e.tensor_copy(
                        LR[:, 4 * g:4 * g + nf, lo:hi], bank[g][:, 0:nf * m_].rearrange("p (c w) -> p c w", c=nf)))
                    if g:
                        VE.do(lambda e, g=g, nf=nf, m_=m_, lo=lo, hi=hi: e.tensor_copy(
                            LR[0:rest, TC - 1, lo:hi], bank[g][0:rest, nf * m_:(nf + 1) * m_]))
            SP.wait((VE.sem, VE.n))
            SP.dma(l_tab, c_rows[L][0:(TC - 1) * P, :].rearrange("(c p) w -> p c w", p=P), LR[:, 0:TC - 1, :])
            k_ = SP.dma(l_tab, c_rows[L][(TC - 1) * P:TT, :], LR[0:rest, TC - 1, :])
            PL.wait(k_)
            for b in range(NB):
                ce_ready = PL.gather(l_nodeg, CE[:, b, :], c_rows[L], tile_ix[:, b:b + 1])
            VE.wait(ce_ready, ye_ready)
            return YE, CE

        def softmax_rows(L, nh):
            YE, CE = join_runs(L, nh)
            w_h = D // nh
            fE, fC, M, dn = (nodeh[:, i, :].rearrange("p (b h) -> p b h", b=NB)[:, :, 0:nh] for i in range(4))
            mE, mC = YE[:, :, D + nh:D + 2 * nh], CE[:, :, D + nh:D + 2 * nh]
            hc = bc(has_carry, 2, nh)
            VE.chain(lambda e: e.tensor_tensor(mC, mC, hc, ALU.mult))
            VE.chain(lambda e: e.tensor_scalar(stat[:, 0, :], has_carry, BIG, -BIG, ALU.mult, ALU.add))
            VE.chain(lambda e: e.tensor_tensor(mC, mC, bc(stat[:, 0, :], 2, nh), ALU.add))
            VE.chain(lambda e: e.tensor_tensor(M, mE, mC, ALU.max))
            VE.chain(lambda e: e.tensor_tensor(fE, mE, M, ALU.subtract))
            k_ = VE.chain(lambda e: e.tensor_tensor(fC, mC, M, ALU.subtract))
            AC.wait(k_)
            AC.do(lambda e: e.activation(fE, fE, ACT.Exp))
            k_ = AC.do(lambda e: e.activation(fC, fC, ACT.Exp))
            VE.wait(k_)
            VE.chain(lambda e: e.tensor_tensor(dn, fE, YE[:, :, D:D + nh], ALU.mult))
            VE.chain(lambda e: e.tensor_tensor(M, fC, CE[:, :, D:D + nh], ALU.mult))
            VE.chain(lambda e: e.tensor_tensor(dn, dn, M, ALU.add))
            VE.chain(lambda e: e.tensor_scalar(dn, dn, 1e-30, None, ALU.max))
            VE.chain(lambda e: e.reciprocal(dn, dn))
            VE.chain(lambda e: e.tensor_tensor(dn, dn, bc(valid, 2, nh), ALU.mult))
            VE.chain(lambda e: e.tensor_tensor(fE, fE, dn, ALU.mult))
            VE.chain(lambda e: e.tensor_tensor(fC, fC, dn, ALU.mult))
            heads = lambda v: v.rearrange("p b (h w) -> p b h w", h=nh)
            c_ = CE[:, :, 0:D]
            VE.do(lambda e: e.tensor_tensor(heads(S1), heads(YE[:, :, 0:D]), bc(fE, 3, w_h), ALU.mult))
            VE.do(lambda e: e.tensor_tensor(heads(c_), heads(c_), bc(fC, 3, w_h), ALU.mult))
            VE.wait((VE.sem, VE.n))
            return VE.chain(lambda e: e.tensor_tensor(S1, S1, CE[:, :, 0:D], ALU.add))

        nodeh = same[0][:, :, :].rearrange("p t f -> p (t f)")[:, 0:4 * NB * H].rearrange("p (k n) -> p k n", k=4)

        def project(dstT, weight, ready, consume):
            PE.wait(*ready)
            for g in range(-(-NB // 4)):
                bs = list(range(4 * g, min(4 * g + 4, NB)))
                bk = g % 2
                PE.wait(ev.get(("proj", bk)))
                for b in bs:
                    k_ = PE.do(lambda e, b=b, bk=bk: e.matmul(bank[bk][:, (b % 4) * P:(b % 4 + 1) * P], dstT[:, b * P:(b + 1) * P], weight, start=True, stop=True))
                VE.wait(k_)
                AC.wait(k_)
                ev[("proj", bk)] = consume(bs, bank[bk][:, 0:len(bs) * P].rearrange("p (b f) -> p b f", b=len(bs)))

        def affine(v, g_row, b_row):
            VE.chain(lambda e: e.tensor_tensor(v, v, bc(g_row, 1, NB), ALU.mult))
            return VE.chain(lambda e: e.tensor_tensor(v, v, bc(b_row, 1, NB), ALU.add))

        agg = softmax_rows(0, H)
        aggT = transpose_nodes(S1, HT, (agg,))
        VE.wait(frow_ready, weights_rest)
        PE.wait(weights_rest)
        AC.wait(weights_rest)

        def add_out(bs, ps):
            o_ = Hn[:, bs[0]:bs[-1] + 1, :]
            return VE.do(lambda e: e.tensor_tensor(o_, o_, ps, ALU.add))

        project(HT, wsq[:, 0, :], aggT, add_out)
        k = (VE.sem, VE.n)
        norm_rows(Hn[:, :, :], Hn[:, :, :], (k,), S2)
        y1 = affine(Hn[:, :, :], frow[:, 1, :], frow[:, 2, :])
        y1T = transpose_nodes(Hn, HT, (y1,))
        VE.wait(*y1T)
        VE.chain(lambda e: e.tensor_tensor(Hn[:, :, :], Hn[:, :, :], bc(frow[:, 3, :], 1, NB), ALU.add))
        PE.wait(*y1T, frow_ready)
        AC.wait(frow_ready, y1)
        hidT = [arena_a[:, s * 2048:(s + 1) * 2048].rearrange("p (c n) -> p c n", c=4) for s in range(2)]
        for g in range(-(-NB // 4)):
            bs = list(range(4 * g, min(4 * g + 4, NB)))
            w_ = len(bs) * P
            s = g % 2
            for c_ in range(4):
                bk = 4 + c_ % 2
                PE.wait(ev.get(("ff", bk)))
                k_ = PE.do(lambda e, c_=c_, bk=bk, g=g, w_=w_: e.matmul(bank[bk][:, 0:w_], Wf1[:, c_ * P:(c_ + 1) * P], HT[:, 4 * g * P:4 * g * P + w_], start=True, stop=True))
                AC.wait(k_, ev.get(("ff2", g - 2)))
                ev[("ff", bk)] = AC.do(lambda e, c_=c_, bk=bk, w_=w_, s=s: e.activation(hidT[s][:, c_, 0:w_], bank[bk][:, 0:w_], ACT.Gelu, bias=bf1[:, c_:c_ + 1]))
            PE.wait(ev[("ff", bk)], ev.get(("proj", s)))
            for j, b in enumerate(bs):
                for c_ in range(4):
                    k_ = PE.do(lambda e, c_=c_, j=j, s=s: e.matmul(bank[s][:, j * P:(j + 1) * P], hidT[s][:, c_, j * P:(j + 1) * P], Wf2[:, c_, :], start=(c_ == 0), stop=(c_ == 3)))
            ev[("ff2", g)] = k_
            VE.wait(k_)
            ev[("proj", s)] = VE.do(lambda e, bs=bs, s=s, w_=w_: e.tensor_tensor(
                Hn[:, bs[0]:bs[-1] + 1, :], Hn[:, bs[0]:bs[-1] + 1, :], bank[s][:, 0:w_].rearrange("p (b f) -> p b f", b=len(bs)), ALU.add))
        k = ev[("proj", s)]
        norm_rows(Hn[:, :, :], Hn[:, :, :], (k,), S2)
        affine(Hn[:, :, :], frow[:, 4, :], frow[:, 5, :])
        x1 = VE.chain(lambda e: e.tensor_tensor(X[:, :, :], X[:, :, :], Hn[:, :, :], ALU.add))

        frow_ready = load_frow(1, (x1,))
        h_ready = relu_norm((x1,))
        hT = transpose_nodes(Hn, HT, (h_ready,))
        w1T = transpose_weight(wsq[:, 1, :], wsq[:, 1, :], (frow_ready,))

        def tanh_out(bs, ps):
            return AC.do(lambda e: e.activation(S1[:, bs[0]:bs[-1] + 1, :], ps, ACT.Tanh))

        AC.wait(x1)
        project(HT, wsq[:, 1, :], hT, tanh_out)
        VE.wait((AC.sem, AC.n), frow_ready)
        TB = arena_a[:, 0:NB * (D + 1)].rearrange("p (b w) -> p b w", b=NB)
        VE.chain(lambda e: e.tensor_tensor(S1, S1, bc(frow[:, 0, :], 1, NB), ALU.mult))
        VE.chain(lambda e: e.tensor_reduce(stat[:, 0, :], S1, AX, ALU.add))
        VE.do(lambda e: e.tensor_copy(TB[:, :, D], stat[:, 0, :]))
        k = VE.do(lambda e: e.tensor_copy(TB[:, :, 0:D], Hn[:, :, :]))
        SP.wait(k)
        tables1 = store_nodes(tab1, TB, l_node)

        def lg1(k_):
            return small[k_ % 2][:, 3, 0:TPB]

        def l1_logits(k_):
            VE.wait(ev[("gs", (1, k_))], got("less", (1, k_ - 2)), got("rows", (1, k_ - 2)))
            ev[("logits", (1, k_))] = VE.do(lambda e: e.tensor_copy(lg1(k_), GS[k_ % RING][:, :, D]))

        def l1_messages(k_):
            s, r = k_ % 2, k_ % RING
            VE.wait(ev[("exp", (1, k_))])
            km = ev[("gs_used", (1, k_))] = VE.do(lambda e: e.tensor_tensor(
                msg[s][:, :, 0:D], GS[r][:, :, 0:D], msg[s][:, :, D:D + 1].broadcast_to([P, TPB, D]), ALU.mult))
            sum_runs(1, k_, D + 1, (km,))

        PL.wait(tables1)
        SP.wait((PE.sem, PE.n), (VE.sem, VE.n))
        e2 = arena_b[:, 0:TC * 2 * P].rearrange("p (c f) -> p c f", c=TC)
        e2s = arena_b[:, TC * 2 * P:2 * TC * 2 * P].rearrange("p (k c f) -> p k c f", k=2, c=TC)
        k = VE.do(lambda e: e.memset(e2[:, TC - 1, :], 0.0))
        ZB = -(-NB // 2)
        zeros = arena_b[:, 2 * TC * 2 * P:2 * TC * 2 * P + ZB * (D + 1)].rearrange("p (b w) -> p b w", b=ZB)
        zeros_set = VE.do(lambda e: e.memset(zeros, 0.0))
        SP.wait(k, zeros_set, tables1)
        e2_in = load_tiled(l_prep, e2, a["edge_attr_2"].rearrange("e k -> (e k)"), 2)

        def layer2_prep():
            VE.wait(e2_in)
            VE.do(lambda e: e.tensor_copy(e2s[:, 0], e2.rearrange("p c (f k) -> p c f k", k=2)[:, :, :, 0]))
            k = VE.do(lambda e: e.tensor_copy(e2s[:, 1], e2.rearrange("p c (f k) -> p c f k", k=2)[:, :, :, 1]))
            yield
            SP.wait(k)
            for i in range(2):
                SP.dma(l_zero, ea2_rows[i, :].rearrange("(c p f) -> p c f", p=P, f=P), e2s[:, i])
            for i in range(NACC):
                for lo, hi in ((0, ZB), (ZB, NB)):
                    yield
                    SP.dma(l_zero, acc_rows[i][lo * P:hi * P, :].rearrange("(b p) w -> p b w", p=P), zeros[:, 0:hi - lo])
                SP.dma(l_zero, acc_rows[i][NB * P:N + P, :], zeros[0:N + P - NB * P, 0, :])

        prep = layer2_prep()
        for n in range(NBLK + 2):
            i0, i1, i2 = n, n - 1, n - 2
            b0, b1, b2 = n < NBLK, 0 <= n - 1 < NBLK, 0 <= n - 2
            if n >= 4:
                next(prep, None)
            if b0:
                gather_block("gs", 1, i0, l_gs, GS, D + 1, tab1, src_ix, got("gs_used", (1, i0 - RING)), got("logits", (1, i0 - RING)))
                load_runs(1, i0, 1)
            if b1:
                load_keys(1, i1, dst_hl)
                logits_to_rows(1, i1, 1, lg1(i1))
                run_scans(1, i1, 1)
            if b2:
                same_matrix(1, i2, dst_col)
            if b1:
                less_max(1, i1, 1, lg1(i1))
                exponentials(1, i1, 1)
            if b2:
                l1_messages(i2)
            if b0:
                l1_logits(i0)
        layer2_inputs = l_zero.at()
        VE.wait(layer2_inputs)
        agg = softmax_rows(1, 1)
        x2 = VE.chain(lambda e: e.tensor_tensor(X[:, :, :], X[:, :, :], S1, ALU.add))

        frow_ready = load_frow(2, (x2,))
        h_ready = relu_norm((x2,))
        hT = transpose_nodes(Hn, HT, (h_ready,))
        VE.wait(*hT)
        VE.chain(lambda e: e.tensor_reduce(cmag[:, 0:1], HT[:, 0:N], AX, ALU.add))
        VE.chain(lambda e: e.tensor_scalar(cmag[:, 0:1], cmag[:, 0:1], 1.0 / N, None, ALU.mult))
        k = VE.chain(lambda e: e.tensor_scalar(HT[:, :], HT[:, :], cmag[:, 0:1], None, ALU.subtract))
        VE.wait(frow_ready)

        def a_out(bs, ps):
            return VE.do(lambda e: e.tensor_tensor(S1[:, bs[0]:bs[-1] + 1, :], ps, bc(frow[:, 0, :], 1, len(bs)), ALU.add))

        def b_out(bs, ps):
            return AC.do(lambda e: e.activation(S2[:, bs[0]:bs[-1] + 1, :], ps, ACT.Copy))

        project(HT, wsq[:, 3, :], (k,), a_out)
        project(HT, wsq[:, 4, :], (k,), b_out)
        SP.wait((VE.sem, VE.n), (AC.sem, AC.n))
        store_nodes(tab2a, S1, l_node)
        tables2 = store_nodes(tab2b, S2, l_node)
        PL.wait(tables2, layer2_inputs)
        SP.wait(layer2_inputs)
        def e2_load(k_, s):
            return SP.dma(l_rows[s], rows4[s][0:2, :], ea2_rows[:, k_ * TPB * P:(k_ + 1) * TPB * P])

        hb_ = [ybuf[s][:, :, 0:D] for s in range(2)]
        sums, squares = bank[6][0:1, :], bank[7][0:1, :]

        def l2_attr_part(i):
            s = i % 2
            PE.wait(ev[("in2", i)])
            for hf in range(2):
                PE.wait(ev.get(f"bank{hf}_free"))
                for t in range(4):
                    tt = 4 * hf + t
                    fn = lambda e, hf=hf, t=t, tt=tt: e.matmul(bank[hf][:, t * P:(t + 1) * P], rows4[s][0:2, tt * P:(tt + 1) * P], W1c[:, :], start=True, stop=True)
                    if t == 3:
                        kk = PE.do(fn)
                    else:
                        PE.quiet(fn)
                ev[("attr", (i, hf))] = kk
            ev[("t2", i)] = kk

        def l2_sum(i, far=True):
            s, r, rd = i % 2, i % RING, i % RING_D
            VE.wait(ev[("gs", (2, i))], got("gd", (2, i)), got("hdma", i - 2), got("st2", i - 2))
            if far:
                kg = ev[("gd_used", (2, i))] = VE.do(lambda e: e.tensor_tensor(GS[r][:, :, 0:D], GS[r][:, :, 0:D], GD[rd][:, :, 0:D], ALU.add))
                VE.wait(kg)
            for hf in range(2):
                VE.wait(ev[("attr", (i, hf))])
                kh = VE.do(lambda e, hf=hf: e.tensor_tensor(
                    hb_[s][:, 4 * hf:4 * hf + 4, :], GS[r][:, 4 * hf:4 * hf + 4, 0:D], bank[hf][:, :].rearrange("p (t f) -> p t f", t=4), ALU.add))
                ev[f"bank{hf}_free"] = kh
            ev[("h_used", i)] = kh
            AC.wait(kh, got("st2", i - 2))
            ev[("square", i)] = AC.do(lambda e: e.activation(msg[s][:, :, 0:D], hb_[s], ACT.Square))
            SP.wait(kh)
            ev[("hdma", i)] = SP.dma(l_y[s], h_rows[i * TPB * P:(i + 1) * TPB * P, :].rearrange("(t p) w -> p t w", p=P), hb_[s])

        def l2_stats(i):
            s = i % 2
            PE.wait(ev[("square", i)])
            if i < NBLK - 1:
                for hf in range(2):
                    for dst_, v_ in ((sums, hb_[s]), (squares, msg[s][:, :, 0:D])):
                        kk = PE.do(lambda e, dst_=dst_, v_=v_, hf=hf: e.matmul(dst_, ones[:, 0:1], v_[:, 4 * hf:4 * hf + 4, :], start=(i == 0 and hf == 0), stop=False, skip_group_check=True))
            else:
                for t in range(TPB):
                    for dst_, v_ in ((sums, hb_[s]), (squares, msg[s][:, :, 0:D])):
                        kk = PE.do(lambda e, dst_=dst_, v_=v_, t=t: e.matmul(dst_[:, (t % 4) * P:(t % 4 + 1) * P], edge_ok[:, t:t + 1], v_[:, t, :], start=False, stop=(t >= TPB - 4), skip_group_check=True))
            ev[("st2", i)] = kk

        def w2_rows(i):
            s, r = i % 2, i % RING_W
            PE.wait(ev[("in2", i)], ev[("window", (2, i))])
            for hf in range(2):
                PE.wait(ev.get(f"bank{hf}_free"), ev[("pick", (2, i, hf))])
                for t in range(4):
                    tt = 4 * hf + t
                    PE.quiet(lambda e, hf=hf, t=t, tt=tt: e.matmul(bank[hf][:, t * P:(t + 1) * P], rows4[s][0:2, tt * P:(tt + 1) * P], W1c[:, :], start=True, stop=False))
                    kk = PE.do(lambda e, hf=hf, t=t, tt=tt: e.matmul(bank[hf][:, t * P:(t + 1) * P], pick[s][:, tt, :], win[r][:, 0:D], start=False, stop=True))
                ev[("attr", (i, hf))] = kk
            ev[("t2", i)] = ev[("window_used", (2, i))] = kk

        def l2_edges_windows():
            VE.wait(tables2, windows_ready)
            SP.wait(tables2)
            for n in range(NBLK + 3):
                if n < NBLK:
                    load_window(2, n, tab2b, D)
                    gather_block("gs", 2, n, l_gs, GS, D, tab2a, src_ix, got("h_used", n - RING))
                for j in (0, 1) if n == 0 else (n + 1,):
                    if j < NBLK:
                        load_window_keys(2, j)
                if n < NBLK:
                    pick_matrix(2, n, 0)
                    pick_matrix(2, n, 1)
                if 0 <= n - 1 < NBLK:
                    w2_rows(n - 1)
                    l2_sum(n - 1, False)
                for j in (0, 1) if n == 0 else (n + 1,):
                    if j < NBLK:
                        SP.wait(got("t2", j - 2))
                        ev[("in2", j)] = e2_load(j, j % 2)
                if 0 <= n - 2 < NBLK:
                    l2_stats(n - 2)

        def l2_edges_any():
            for n in range(NBLK + 2):
                if n < NBLK:
                    gather_block("gs", 2, n, l_gs, GS, D, tab2a, src_ix, got("h_used", n - RING))
                    gather_block("gd", 2, n, l_gd, GD, D, tab2b, dst_ix, got("gd_used", (2, n - RING_D)))
                for j in (0, 1) if n == 0 else (n + 1,):
                    if j < NBLK:
                        SP.wait(got("t2", j - 2))
                        ev[("in2", j)] = e2_load(j, j % 2)
                if 0 <= n - 1 < NBLK:
                    l2_sum(n - 1)
                if n < NBLK:
                    l2_attr_part(n)
                if n >= 2:
                    l2_stats(n - 2)

        either(engines, lanes_, l_far, ev, all_near[0:1, 0:1], l2_edges_windows, l2_edges_any)
        bn = relb[0:1, :, :].rearrange("p y (k f) -> p (y k) f", f=D)
        gb = Wqkv[0:1, 0:2 * D].rearrange("p (k f) -> p k f", k=2)
        gb_in = [SP.dma(l_w2, gb[:, 0, :], a["L2_gnn_gamma"].unsqueeze(0)), SP.dma(l_w2, gb[:, 1, :], a["L2_gnn_beta"].unsqueeze(0))][-1]
        VE.wait(gb_in)
        mu_, ms_, va_ = bn[:, 0, :], bn[:, 1, :], bn[:, 2, :]
        VE.chain(lambda e: e.tensor_reduce(mu_, sums.rearrange("p (t f) -> p f t", t=4), AX, ALU.add))
        VE.chain(lambda e: e.tensor_reduce(ms_, squares.rearrange("p (t f) -> p f t", t=4), AX, ALU.add))
        VE.chain(lambda e: e.tensor_scalar(bn[:, 0:2, :], bn[:, 0:2, :], 1.0 / E, None, ALU.mult))
        VE.chain(lambda e: e.tensor_tensor(va_, mu_, mu_, ALU.mult))
        VE.chain(lambda e: e.tensor_tensor(va_, ms_, va_, ALU.subtract))
        VE.chain(lambda e: e.tensor_scalar(va_, va_, 0.0, EPS, ALU.max, ALU.add))
        k = VE.chain(lambda e: e.reciprocal(va_, va_))
        AC.wait(k)
        k = AC.do(lambda e: e.activation(va_, va_, ACT.Sqrt))
        VE.wait(k)
        VE.chain(lambda e: e.tensor_tensor(bn[:, 3, :], va_, gb[:, 0, :], ALU.mult))
        VE.chain(lambda e: e.tensor_tensor(bn[:, 5, :], mu_, bn[:, 3, :], ALU.mult))
        k = VE.chain(lambda e: e.tensor_tensor(bn[:, 4, :], gb[:, 1, :], bn[:, 5, :], ALU.subtract))
        PE.wait(k)
        k = PE.do(lambda e: e.matmul(bank[4][:, 0:2 * D], ones[0:1, :], bn[:, 3:5, :].rearrange("p k f -> p (k f)"), start=True, stop=True))
        bnr = Wf1[:, 0:2 * D].rearrange("p (k f) -> p k f", k=2)
        VE.wait(k)
        bn_ready = VE.chain(lambda e: e.tensor_copy(bnr[:, :, :], bank[4][:, 0:2 * D].rearrange("p (k f) -> p k f", k=2)))
        VE.do(lambda e: e.tensor_tensor(X[:, :, :], X[:, :, :], Hn[:, :, :], ALU.add))
        for s in range(2):
            VE.do(lambda e, s=s: e.memset(msg[s][:, :, D:D + 1], 1.0))
        VE.wait((VE.sem, VE.n))
        SP.wait((l_y[0].sem, l_y[0].n), (l_y[1].sem, l_y[1].n))

        def l2_h_in(i):
            r = i % RING
            SP.wait(got("m2", i - RING))
            ev[("hin", i)] = SP.dma(l_hin[r], GS[r][:, :, 0:D], h_rows[i * TPB * P:(i + 1) * TPB * P, :].rearrange("(t p) w -> p t w", p=P))

        def l2_targets(i):
            s = i % 2
            tri = GD[s][:, :, 0:P]
            cnt_, tgt = small[s][:, 0, 0:TPB], small[s][:, 1, 0:TPB]
            sc_ = src_col[:, i * TPB:(i + 1) * TPB]
            VE.wait(ev[("same", (2, i))])
            VE.chain(lambda e: e.tensor_tensor(tri, same[s][:, :, :], bc(lower[:, :], 1, TPB), ALU.mult))
            VE.chain(lambda e: e.tensor_reduce(cnt_, tri, AX, ALU.add))
            VE.chain(lambda e: e.tensor_scalar(cnt_, cnt_, 0.0, None, ALU.is_equal))
            VE.do(lambda e: e.tensor_scalar(tgt, sc_, junk[:, 0:1], None, ALU.subtract))
            VE.chain(lambda e: e.scalar_tensor_tensor(out=cnt_, in0=sc_, scalar=float(N), in1=cnt_, op0=ALU.is_lt, op1=ALU.mult))
            VE.chain(lambda e: e.tensor_tensor(tgt, tgt, cnt_, ALU.mult))
            VE.wait(*got_all("ydma", (2, i - RING_IX)))
            ev[("targets", i)] = VE.do(lambda e: e.tensor_scalar(add_ix[i % RING_IX][:, :], tgt, junk[:, 0:1], None, ALU.add))

        def l2_relu(i):
            s, r = i % 2, i % RING
            g_ = GS[r][:, :, 0:D]
            VE.wait(ev[("hin", i)])
            VE.chain(lambda e: e.tensor_tensor(g_, g_, bc(bnr[:, 0, :], 1, TPB), ALU.mult))
            kb = VE.do(lambda e: e.tensor_tensor(g_, g_, bc(bnr[:, 1, :], 1, TPB), ALU.add))
            AC.wait(kb, got("pe_y", (2, i - 2)))
            ev[("m2", i)] = AC.do(lambda e: e.activation(msg[s][:, :, 0:D], g_, ACT.Relu))

        def l2_add(i, ready):
            s = i % 2
            PL.wait(ev[("targets", i)], ready)
            for t in range(TPB):
                j = t % NACC
                PL.wait(l_acc[j].at() if l_acc[j].n else None)
                PL.scatter_add(l_acc[j], acc_rows[j], add_ix[i % RING_IX][:, t:t + 1], ybuf[s][:, t, 0:D + 1])
            return [l_acc[j].at() for j in range(NACC)]

        for n in range(NBLK + 1):
            if n < NBLK:
                for j in (0, 1) if n == 0 else (n + 1,):
                    if j < NBLK:
                        load_keys(2, j, src_hl)
                for j in (0, 1, 2) if n == 0 else (n + 2,):
                    if j < NBLK:
                        l2_h_in(j)
                same_matrix(2, n, src_col)
                l2_relu(n)
            if n >= 1:
                sum_runs(2, n - 1, D + 1, (ev[("m2", n - 1)],), lambda ready, i=n - 1: l2_add(i, ready))
            if n < NBLK:
                l2_targets(n)
        ev[("acc", NBLK - 1)] = ev[("ydma", (2, NBLK - 1))]
        SP.wait((VE.sem, VE.n), (PE.sem, PE.n), (AC.sem, AC.n), *ev[("acc", NBLK - 1)])
        places = [arena_a[:, j * NB * (D + 1):(j + 1) * NB * (D + 1)] for j in range(NACC - 1)] + [arena_b[:, 0:NB * (D + 1)]]
        AB = [v.rearrange("p (b w) -> p b w", b=NB) for v in places]
        summed_in = [SP.dma(l_hin[j], AB[j], acc_rows[j][0:NB * P, :].rearrange("(b p) w -> p b w", p=P)) for j in range(NACC)]
        VE.wait(summed_in[0])
        for j in range(1, NACC):
            VE.wait(summed_in[j])
            k = VE.chain(lambda e, j=j: e.tensor_tensor(AB[0], AB[0], AB[j], ALU.add))
        sT = transpose_nodes(AB[0][:, :, 0:D], HT, (k,))
        cnts, rc, share = stat[:, 2, :], stat[:, 3, :], stat[:, 4, :]
        VE.chain(lambda e: e.tensor_copy(cnts, AB[0][:, :, D]))
        VE.chain(lambda e: e.tensor_scalar(rc, cnts, 1.0, None, ALU.add))
        VE.chain(lambda e: e.reciprocal(rc, rc))
        VE.chain(lambda e: e.tensor_tensor(share, cnts, rc, ALU.mult))
        VE.chain(lambda e: e.tensor_tensor(S2, bc(share, 2, D), bc(frow[:, 1, :], 1, NB), ALU.mult))
        VE.chain(lambda e: e.tensor_tensor(X[:, :, :], X[:, :, :], S2, ALU.add))

        def w2_out(bs, ps):
            sl = slice(bs[0], bs[-1] + 1)
            read = VE.chain(lambda e: e.tensor_tensor(S1[:, sl, :], ps, bc(rc[:, sl], 2, D), ALU.mult))
            VE.do(lambda e: e.tensor_tensor(X[:, sl, :], X[:, sl, :], S1[:, sl, :], ALU.add))
            return read

        project(HT, wsq[:, 2, :], sT, w2_out)
        x3 = (VE.sem, VE.n)

        frow_ready = load_frow(3, (x3,))
        h_ready = relu_norm((x3,))
        hT = transpose_nodes(Hn, HT, (h_ready,))
        transpose_weight(wtmp[:, D:D + T_DIM], We3[:, :], (frow_ready,), width=T_DIM)
        transpose_weight(emb[:, :], embT[:, :], (), parts=NT16, width=T_DIM)
        transpose_weight(wtmp[:, 0:D], wsq[:, 3, :], ())
        transpose_weight(wsq[:, 5, :], wsq[:, 4, :], ())
        k = PE.do(lambda e: e.matmul(bank[6][0:NT16, 0:D], embT[:, :], We3[:, :], start=True, stop=True))
        VE.wait(k, frow_ready)
        em_ready = VE.do(lambda e: e.tensor_tensor(Em[:, :], bank[6][0:NT16, 0:D], frow[0:NT16, 0, :], ALU.add))

        def xm_out(bs, ps):
            return VE.do(lambda e: e.tensor_copy(S1[:, bs[0]:bs[-1] + 1, :], ps))

        project(HT, wsq[:, 3, :], hT, xm_out)
        SP.wait((VE.sem, VE.n))
        tables3 = store_nodes(tab3, S1, l_node)
        L = 3
        PL.wait(tables3)
        PE.wait(em_ready)


        def l3_type_part(i):
            s = i % 2
            VE.wait(ev[("types", i)])
            k1 = VE.do(lambda e: e.tensor_scalar(rows4[s][:, :], rows4[s][:, :], iota16[:, 0:1], None, ALU.is_equal))
            PE.wait(k1)
            for hf in range(2):
                PE.wait(ev.get(f"bank{hf}_free"))
                for t in range(4):
                    tt = 4 * hf + t
                    fn = lambda e, hf=hf, t=t, tt=tt: e.matmul(bank[hf][:, t * P:(t + 1) * P], rows4[s][:, tt * P:(tt + 1) * P], Em[:, :], start=True, stop=True)
                    if t == 3:
                        kk = PE.do(fn)
                    else:
                        PE.quiet(fn)
                ev[("type", (i, hf))] = kk
            ev[("types_used", i)] = kk

        def l3_relu(i):
            s, r = i % 2, i % RING
            VE.wait(ev[("gs", (3, i))])
            for hf in range(2):
                VE.wait(ev[("type", (i, hf))])
                g_ = GS[r][:, 4 * hf:4 * hf + 4, 0:D]
                kg = VE.do(lambda e, g_=g_, hf=hf: e.tensor_tensor(g_, g_, bank[hf][:, :].rearrange("p (t f) -> p t f", t=4), ALU.add))
                ev[f"bank{hf}_free"] = kg
            AC.wait(kg, got("pe_y", (3, i - 2)))
            ev[("gs_used", (3, i))] = AC.do(lambda e: e.activation(msg[s][:, :, 0:D], GS[r][:, :, 0:D], ACT.Relu))

        for n in range(NBLK + 2):
            if n < NBLK:
                gather_block("gs", 3, n, l_gs, GS, D, tab3, src_ix, got("gs_used", (3, n - RING)))
            for j in (0, 1) if n == 0 else (n + 1,):
                if j < NBLK:
                    SP.wait(got("types_used", j - 2))
                    ev[("types", j)] = SP.dma(l_rows[j % 2], rows4[j % 2][:, :], t16_row[:, j * TPB * P:(j + 1) * TPB * P].broadcast_to([NT16, TPB * P]))
            if 0 <= n - 1 < NBLK:
                load_keys(3, n - 1, dst_hl)
                l3_relu(n - 1)
            if n < NBLK:
                l3_type_part(n)
            if n >= 2:
                same_matrix(3, n - 2, dst_col)
                sum_runs(3, n - 2, D, (ev[("gs_used", (3, n - 2))],))
        YE, CE = join_runs(3, 0)
        VE.chain(lambda e: e.tensor_tensor(CE, CE, bc(has_carry, 2, D), ALU.mult))
        VE.chain(lambda e: e.tensor_tensor(YE, YE, CE, ALU.add))
        VE.chain(lambda e: e.tensor_scalar(stat[:, 0, :], degree, 1.0, None, ALU.max))
        VE.chain(lambda e: e.reciprocal(stat[:, 0, :], stat[:, 0, :]))
        VE.chain(lambda e: e.tensor_tensor(stat[:, 0, :], stat[:, 0, :], valid, ALU.mult))
        k = VE.chain(lambda e: e.tensor_tensor(S1, YE, bc(stat[:, 0, :], 2, D), ALU.mult))
        aT = transpose_nodes(S1, HT, (k,))

        def upd_out(bs, ps):
            return VE.do(lambda e: e.tensor_tensor(S1[:, bs[0]:bs[-1] + 1, :], ps, bc(frow[:, 1, :], 1, len(bs)), ALU.add))

        project(HT, wsq[:, 4, :], aT, upd_out)
        VE.wait((VE.sem, VE.n))
        k = VE.chain(lambda e: e.tensor_tensor(Hn[:, :, :], Hn[:, :, :], S1, ALU.add))
        norm_rows(Hn[:, :, :], Hn[:, :, :], (k,), S2)
        affine(Hn[:, :, :], frow[:, 2, :], frow[:, 3, :])
        k = VE.chain(lambda e: e.tensor_tensor(X[:, :, :], X[:, :, :], Hn[:, :, :], ALU.add))
        SP.wait(k)
        done = store_nodes(out, X, l_out)
        SP.wait(done)

        block = ctx.enter_context(nc.Block())
        block.sync(SP.play)
        block.gpsimd(PL.play)
        block.scalar(AC.play)
        block.vector(VE.play)
        block.tensor(PE.play)


def kernel(**inputs):
    import concourse.bacc as bacc
    from concourse.bass_utils import run_bass_kernel_spmd

    nc = bacc.Bacc("TRN2", target_bir_lowering=False, num_devices=1)
    arrays, aps = {}, {}
    for name, value in inputs.items():
        v = np.ascontiguousarray(value).reshape(np.shape(value) or (1,))
        arrays[name] = v
        aps[name] = nc.dram_tensor(name, v.shape, mybir.dt.from_np(v.dtype), kind="ExternalInput").ap()
    out = nc.dram_tensor("out", (N, D), F32, kind="ExternalOutput").ap()
    program(nc, aps, out)
    r = run_bass_kernel_spmd(nc, [arrays], core_ids=[0])
    return r.results[0]["out"]
```
